# Optimizing a Trainium2 kernel written in Bass

```python
import numpy as np
import jax
import jax.numpy as jnp

def _softmax(x, axis=-1):
    return jax.nn.softmax(x, axis=axis)

def _gelu(x):
    return jax.nn.gelu(x, approximate=True)

def _silu(x):
    return jax.nn.silu(x)

def _sigmoid(x):
    return jax.nn.sigmoid(x)

def _layernorm(x, axis=-1, eps=1e-05):
    m = jnp.mean(x, axis=axis, keepdims=True)
    v = jnp.var(x, axis=axis, keepdims=True)
    return (x - m) / jnp.sqrt(v + eps)

def _scatter_add(tgt, idx, src, axis=0):
    return tgt.at[idx].add(src)

def _segment_sum(src, seg, n):
    return jax.ops.segment_sum(src, seg, n)
kernel_name = 'mk_seq_postln_d1_jaxref_r8_0adee2'

def setup_inputs(seed: int=0):
    np.random.seed(seed)
    _w = jnp.asarray

    def _L0_attn_setup():
        import jax, jax.numpy as jnp
        import numpy as np
        B, N, EMBED, HEADS = (1, 256, 128, 16)
        HD = EMBED // HEADS
        BASE = 10000.0
        EPS = 1e-05

        def _rope(t):
            d = t.shape[-1]
            n = t.shape[-2]
            inv_freq = 1.0 / BASE ** (jnp.arange(0, d, 2, dtype=jnp.float32) / d)
            pos = jnp.arange(n, dtype=jnp.float32)
            ang = pos[:, None] * inv_freq[None, :]
            cos = jnp.concatenate([jnp.cos(ang), jnp.cos(ang)], axis=-1)
            sin = jnp.concatenate([jnp.sin(ang), jnp.sin(ang)], axis=-1)
            t1, t2 = (t[..., :d // 2], t[..., d // 2:])
            rot = jnp.concatenate([-t2, t1], axis=-1)
            return t * cos + rot * sin
        key = jax.random.key(seed)
        ks = jax.random.split(key, 7)
        s = EMBED ** (-0.5)
        return {'x': jax.random.normal(ks[0], (B, N, EMBED), dtype=jnp.float32), 'Wq': jax.random.normal(ks[1], (EMBED, EMBED), dtype=jnp.float32) * s, 'Wk': jax.random.normal(ks[2], (EMBED, EMBED), dtype=jnp.float32) * s, 'Wv': jax.random.normal(ks[3], (EMBED, EMBED), dtype=jnp.float32) * s, 'Wo': jax.random.normal(ks[4], (EMBED, EMBED), dtype=jnp.float32) * s, 'Wg1': jax.random.normal(ks[5], (EMBED, HD), dtype=jnp.float32) * s, 'Wg2': jax.random.normal(ks[6], (HD, EMBED), dtype=jnp.float32) * HD ** (-0.5), 'ln_w': jnp.ones((EMBED,), dtype=jnp.float32), 'ln_b': jnp.zeros((EMBED,), dtype=jnp.float32)}
    _L0_attn_in = _L0_attn_setup()

    def _L0_ffn_setup():
        import jax, jax.numpy as jnp
        import numpy as np
        B, S = (4, 64)
        H = 128
        I = 352
        E = 8
        K = 2
        IS = 176
        key = jax.random.key(seed)
        ks = jax.random.split(key, 8)

        def init(k, shape, fan_in):
            return (jax.random.normal(k, shape, jnp.float32) / np.sqrt(fan_in)).astype(jnp.float32)
        return {'hidden_states': jax.random.normal(ks[0], (B, S, H), jnp.float32), 'gate_w': init(ks[1], (H, E), H), 'Wg': init(ks[2], (E, H, I), H), 'Wu': init(ks[3], (E, H, I), H), 'Wd': init(ks[4], (E, I, H), I), 'Sg': init(ks[5], (H, IS), H), 'Su': init(ks[6], (H, IS), H), 'Sd': init(ks[7], (IS, H), IS)}
    _L0_ffn_in = _L0_ffn_setup()
    _d = {'L0_attn_x': _L0_attn_in['x'], 'L0_attn_Wq': _L0_attn_in['Wq'], 'L0_attn_Wk': _L0_attn_in['Wk'], 'L0_attn_Wv': _L0_attn_in['Wv'], 'L0_attn_Wo': _L0_attn_in['Wo'], 'L0_attn_Wg1': _L0_attn_in['Wg1'], 'L0_attn_Wg2': _L0_attn_in['Wg2'], 'L0_attn_ln_w': _L0_attn_in['ln_w'], 'L0_attn_ln_b': _L0_attn_in['ln_b'], 'L0_ffn_gate_w': _L0_ffn_in['gate_w'], 'L0_ffn_Wg': _L0_ffn_in['Wg'], 'L0_ffn_Wu': _L0_ffn_in['Wu'], 'L0_ffn_Wd': _L0_ffn_in['Wd'], 'L0_ffn_Sg': _L0_ffn_in['Sg'], 'L0_ffn_Su': _L0_ffn_in['Su'], 'L0_ffn_Sd': _L0_ffn_in['Sd']}
    _x0 = _d['L0_attn_x']
    _d['L0_attn_x'] = jax.random.normal(jax.random.fold_in(jax.random.key(seed), 1), (4, 1024, 128), dtype=_x0.dtype)
    del _x0
    return _d

def reference(L0_attn_x, L0_attn_Wq, L0_attn_Wk, L0_attn_Wv, L0_attn_Wo, L0_attn_Wg1, L0_attn_Wg2, L0_attn_ln_w, L0_attn_ln_b, L0_ffn_gate_w, L0_ffn_Wg, L0_ffn_Wu, L0_ffn_Wd, L0_ffn_Sg, L0_ffn_Su, L0_ffn_Sd):

    def _L0_attn_ref(x, Wq, Wk, Wv, Wo, Wg1, Wg2, ln_w, ln_b):
        import jax, jax.numpy as jnp
        import numpy as np
        B, N, EMBED, HEADS = (1, 256, 128, 16)
        HD = EMBED // HEADS
        BASE = 10000.0
        EPS = 1e-05

        def _rope(t):
            d = t.shape[-1]
            n = t.shape[-2]
            inv_freq = 1.0 / BASE ** (jnp.arange(0, d, 2, dtype=jnp.float32) / d)
            pos = jnp.arange(n, dtype=jnp.float32)
            ang = pos[:, None] * inv_freq[None, :]
            cos = jnp.concatenate([jnp.cos(ang), jnp.cos(ang)], axis=-1)
            sin = jnp.concatenate([jnp.sin(ang), jnp.sin(ang)], axis=-1)
            t1, t2 = (t[..., :d // 2], t[..., d // 2:])
            rot = jnp.concatenate([-t2, t1], axis=-1)
            return t * cos + rot * sin
        b, n, _ = x.shape
        q = jax.nn.silu(x @ Wq)
        k = jax.nn.silu(x @ Wk)
        v = x @ Wv
        split = lambda t: t.reshape(b, n, HEADS, HD).transpose(0, 2, 1, 3)
        q, k, v = (split(q), split(k), split(v))
        q = _rope(q)
        k = _rope(k)
        energy = jnp.einsum('bhnd,bhmd->bhnm', q, k)
        mask = jnp.tril(jnp.ones((n, n), dtype=energy.dtype))
        energy = energy * mask
        out = jnp.einsum('bhnm,bhmd->bhnd', energy, v)
        out = out.transpose(0, 2, 1, 3).reshape(b, n, EMBED)
        gate = jax.nn.sigmoid(x @ Wg1 @ Wg2)
        out = out * gate
        mu = out.mean(axis=-1, keepdims=True)
        var = ((out - mu) ** 2).mean(axis=-1, keepdims=True)
        out = (out - mu) / jnp.sqrt(var + EPS) * ln_w + ln_b
        return out @ Wo

    def _L0_ffn_ref(hidden_states, gate_w, Wg, Wu, Wd, Sg, Su, Sd):
        import jax, jax.numpy as jnp
        import numpy as np
        B, S = (4, 64)
        H = 128
        I = 352
        E = 8
        K = 2
        IS = 176
        b, s, h = hidden_states.shape
        x = hidden_states.reshape(-1, h)
        T = x.shape[0]
        logits = x @ gate_w
        top_v, top_i = jax.lax.top_k(logits, K)
        top_p = jax.nn.softmax(top_v, axis=-1)
        combine = jnp.zeros((T, E), x.dtype).at[jnp.arange(T)[:, None], top_i].add(top_p)
        g = jnp.einsum('th,ehi->tei', x, Wg)
        u = jnp.einsum('th,ehi->tei', x, Wu)
        d = jnp.einsum('tei,eih->teh', jax.nn.silu(g) * u, Wd)
        expert_out = jnp.einsum('te,teh->th', combine, d)
        shared = jax.nn.silu(x @ Sg) * (x @ Su) @ Sd
        return (expert_out + shared).reshape(b, s, h)
    x = L0_attn_x
    x = _layernorm(x + _L0_attn_ref(x, L0_attn_Wq, L0_attn_Wk, L0_attn_Wv, L0_attn_Wo, L0_attn_Wg1, L0_attn_Wg2, L0_attn_ln_w, L0_attn_ln_b), axis=-1)
    x = _layernorm(x + _L0_ffn_ref(x, L0_ffn_gate_w, L0_ffn_Wg, L0_ffn_Wu, L0_ffn_Wd, L0_ffn_Sg, L0_ffn_Su, L0_ffn_Sd), axis=-1)
    return x

_drawn_inputs = setup_inputs


def setup_inputs(seed=0):
    import zlib

    import numpy as np

    out = dict(_drawn_inputs(seed))
    spreads = {'L0_attn_ln_w': (1.0, 0.2), 'L0_attn_ln_b': (0.0, 0.1)}
    factors = {}
    for name, (base, spread) in spreads.items():
        noise = np.random.default_rng([zlib.crc32(name.encode()), seed]).standard_normal(out[name].shape)
        drawn = base * np.exp(spread * noise) if base else spread * noise
        out[name] = jnp.asarray(drawn.astype(out[name].dtype))
    for name, factor in factors.items():
        out[name] = (out[name] * factor).astype(out[name].dtype)
    return out
```

```python
import math
from contextlib import ExitStack

import numpy as np
import concourse.bass as bass
from concourse import mybir

TOKENS, CH, HEADS, HD = 4096, 128, 16, 8
P = 128
TILES = TOKENS // P
SEQ = 1024
BATCH_TILES = SEQ // P
EPS = 1e-5
ROWS_PER_HEAD = 32
BLOCKS = 4
U = 4
EXPERTS, TOP, INNER, SHARED = 8, 2, 352, 176
IC = 3
SC = 2
SLOTS = 2 * P
REGION = TOKENS + SLOTS
SLOT_TILES = 40
DUMMY = SLOT_TILES - TOP * TOKENS // SLOTS
ROW = 132
DEST, WEIGHT = 128, 129
FINALS, FT = 8, TILES // 8
YROWS = TOP * TOKENS + (EXPERTS + DUMMY) * SLOTS


def constants():
    f = np.float32
    d = HD
    inv = (f(1.0) / np.power(f(10000.0), np.arange(0, d, 2, dtype=f) / f(d))).astype(f)
    ang = (np.arange(SEQ, dtype=f)[:, None] * inv[None, :]).astype(f).astype(np.float64)
    cos = np.concatenate([np.cos(ang), np.cos(ang)], -1)
    sin = np.concatenate([-np.sin(ang), np.sin(ang)], -1)
    tab = lambda a: np.tile(a.reshape(BATCH_TILES, P, d).transpose(1, 0, 2), (1, TOKENS // SEQ, 1)).reshape(P, TILES * d)
    tri = (np.arange(P)[:, None] <= np.arange(P)[None, :])
    row = np.arange(P)
    col = np.arange(P)
    own = (row[:, None] // 32) == ((col[None, :] % 32) // 8)
    keep = np.tile(((np.arange(TILES) + 1) % BATCH_TILES != 0).astype(f)[None, :], (P, 1))
    center = 0.5 * (np.eye(P) - 1.0 / P)
    parts = {"cos": tab(cos), "sin": tab(sin), "tri": tri, "own": own, "keep": keep, "center": center,
             "iota": np.tile(np.arange(EXPERTS)[None, :], (P, 1)),
             "first": np.tile(np.arange(EXPERTS)[None, :] * REGION, (P, 1)),
             "row": np.arange(P)[:, None],
             "small": np.tile(np.array([[CH * EPS, EPS, -0.5]]), (P, 1))}
    at, n = {}, 0
    for k, a in parts.items():
        at[k] = (n, a.shape[1]); n += a.shape[1]
    return np.concatenate([np.asarray(a, f) for a in parts.values()], 1), at


def index_constants():
    p = np.arange(P)[:, None, None]
    pairs = (np.arange(TOP)[None, None, :] * TOKENS + np.arange(TILES)[None, :, None] * P + p).reshape(P, -1)
    return pairs.astype(np.int32)


def pad_rows():
    rows = np.zeros(((EXPERTS + DUMMY) * SLOTS, ROW), np.int32)
    rows[:, DEST] = TOP * TOKENS + np.arange(len(rows))
    return rows.view(np.float32)


def half_constants():
    r = np.arange(P)
    return np.concatenate([np.eye(P), r[:, None] < r[None, :], np.ones((P, P))], 1).astype(np.float16)


_, CONST_AT = constants()
CONST_W = sum(w for _, w in CONST_AT.values())


def build(nc, x, xT, Wqkv, Wg1T, Wg2, Wo, ln, gate_w, Wg, Wu, Wd, Sgu, Sd, consts, halves, indices, pads, out):
    f32, f16, i32, u32 = mybir.dt.float32, mybir.dt.float16, mybir.dt.int32, mybir.dt.uint32
    ALU, ACT, AX = mybir.AluOpType, mybir.ActivationFunctionType, mybir.AxisListType
    ctx = ExitStack()
    with ctx:
        sb = lambda n, s, d=f32: ctx.enter_context(nc.sbuf_tensor(n, s, d))
        ps = lambda n, s, d=f32: ctx.enter_context(nc.psum_tensor(n, s, d))
        sem = lambda n: ctx.enter_context(nc.semaphore(n))
        cst = sb("cst", [P, CONST_W])
        C = lambda k: cst[:, CONST_AT[k][0]:CONST_AT[k][0] + CONST_AT[k][1]]
        half = sb("half", [P, 3 * P], f16)
        idh, before, onesh = half[:, 0:P], half[:, P:2 * P], half[:, 2 * P:]
        ind = sb("ind", [P, TOP * TILES], i32)
        lnc = sb("lnc", [P, 2])
        w_in = sb("w_in", [P, 4 * P])
        g1T = sb("g1T", [HD, P]); g2 = sb("g2", [HD, P])
        wo = sb("wo", [P, P]); wos = sb("wos", [P, P]); lnbb = sb("lnbb", [P, P]); ones = sb("ones", [P, P])
        rhs2 = sb("rhs2", [P, 2 * P])
        brow = sb("brow", [P, P])
        gw = sb("gw", [P, 8]); gwh = sb("gwh", [P, 8], f16); gwl = sb("gwl", [P, 8], f16)
        x_sb = sb("x_sb", [P, TILES, P])
        x1 = sb("x1", [P, TILES, P])
        lg = sb("lg", [P, U, 8]); mx = sb("mx", [P, 2, 8]); ix = sb("ix", [P, 2, 8], u32); ef = sb("ef", [P, 2, TOP])
        oh = sb("oh", [P, 2, TOP, EXPERTS]); chosen = sb("chosen", [P, 2, EXPERTS], f16)
        gap = sb("gap", [P, U]); tw = sb("tw", [P, U])
        base = sb("base", [P, EXPERTS]); pe_ = sb("pe_", [P, 2, EXPERTS]); pr = sb("pr", [P, 2, TOP, EXPERTS]); pf = sb("pf", [P, 2, TOP])
        place = sb("place", [P, U, TOP], u32)
        pay = sb("pay", [P, U, TOP, ROW])
        ends = sb("ends", [P, EXPERTS], i32)
        cnt = sb("cnt", [P, EXPERTS]); nti = sb("nti", [P, EXPERTS], i32); ntj = sb("ntj", [P, EXPERTS], i32)
        nt = [sb(f"nt{n}", [P, EXPERTS]) for n in range(4)]
        ge = sb("ge", [P, EXPERTS]); gn = sb("gn", [P, EXPERTS]); te = sb("te", [P, 8]); tab = sb("tab", [P, 2], i32)
        tabr = sb("tabr", [1, 2 * P], i32)
        wst = sb("wst", [P, EXPERTS, 2, INNER])
        wh = sb("wh", [P, EXPERTS, 2, IC * P], f16); wl = sb("wl", [P, EXPERTS, 2, IC * P], f16)
        wd = sb("wd", [P, EXPERTS, IC * P])
        sst_ = sb("sst_", [P, 2, SHARED]); sh = sb("sh", [P, 2, SC * P], f16); sl = sb("sl", [P, 2, SC * P], f16)
        sd = sb("sd", [P, SC, P])
        meta = sb("meta", [P, U, 2, 2])
        xs16 = sb("xs16", [P, 2, 2, SLOTS], f16)
        rows = nc.dram_tensor("rows", [(EXPERTS + 1) * REGION, ROW], f32).ap()
        ydram = nc.dram_tensor("ydram", [YROWS, P], f32).ap()
        xTr = sb("xTr", [P, U, P])
        qk = sb("qk", [P, U, 2 * P])
        rc = sb("rc", [P, U, 2 * P]); rs = sb("rs", [P, U, 2 * P])
        qk16 = sb("qk16", [P, U, 2 * 4 * P], f16)
        qkT = sb("qkT", [P, 2, 8, P], f16)
        th = sb("th", [P, U, P])
        vexp = sb("vexp", [P, U, 4, P])
        vh = sb("vh", [P, U, P], f16); vl = sb("vl", [P, U, P], f16)
        em = sb("em", [P, 2, 4, 4 * P])
        dm = sb("dm", [P, 2, P]); zero = sb("zero", [P, P]); dmk = sb("dmk", [P, P]); sacc = sb("sacc", [P, 2, P]); shi = sb("shi", [P, 2, P], f16)
        slo = sb("slo", [P, 2, P], f16)
        og = sb("og", [P, 2, P])
        sqj = sb("sqj", [P, P]); ve = sb("ve", [P, 2]); vsum = sb("vsum", [P, U]); rstd = sb("rstd", [P, U])
        xp = sb("xp", [P, 2, P]); st6 = sb("st6", [P, 2, 6]); mv = sb("mv", [P, 2, 2]); rstd2 = sb("rstd2", [P, 2])
        x1hl = sb("x1hl", [P, 2, 2, P], f16)
        ybuf = sb("ybuf", [P, U, 2, P])
        x1Tr = sb("x1Tr", [P, 2, TOKENS], f16)
        xbr = sb("xbr", [P, 2, P])

        y0 = x_sb[:, :, :]
        flat = lambda a: a[:, :, :, :].rearrange("p a b c -> p (a b c)")
        xin = flat(vexp)[:, 0:U * 2 * ROW].rearrange("p (a b n) -> p a b n", a=U, b=2)
        yb = flat(ybuf).rearrange("p (a b n) -> p a b n", a=U, b=2)
        sg = flat(em)[:, 0:2 * IC * SLOTS].rearrange("p (a c n) -> p a c n", a=2, c=IC)
        hT = flat(em)[:, 2 * IC * SLOTS:4 * IC * SLOTS].rearrange("p (a c n) -> p a c n", a=2, c=IC)
        hS = em[:, :, :, :].rearrange("p a h n -> p (a h n)")[:, 0:4 * 512].rearrange("p (a c n) -> p a c n", a=2, c=2)
        sS = em[:, :, :, :].rearrange("p a h n -> p (a h n)")[:, 2048:4096].rearrange("p (a c n) -> p a c n", a=2, c=2)
        whf, wlf = wh[:, :, :, :].rearrange("p e g n -> p (e g n)"), wl[:, :, :, :].rearrange("p e g n -> p (e g n)")
        wdf = wd[:, :, :].rearrange("p e n -> p (e n)")
        wh3, wl3 = wh[:, :, :, :].rearrange("p e g n -> p (e g) n"), wl[:, :, :, :].rearrange("p e g n -> p (e g) n")
        wst3 = wst[:, :, :, :].rearrange("p e g n -> p (e g) n")
        FFN_LOADS = 16 * 9
        y1 = bass.AP(wst, offset=0, ap=[[EXPERTS * 2 * INNER, P], [P, TILES], [1, P]])
        pay16 = lambda k: pay[:, k, :, 0:P].bitcast(f16)

        def vdiag(k):
            return bass.AP(vexp, offset=k * 4 * P, ap=[[U * 4 * P, P], [P + HD, 4], [32, 4], [1, HD]])

        b_in = ps("b_in", [P, 4 * P]); b_t = ps("b_t", [P, 8, P], f16)
        b_e = [ps(f"b_e{i}", [P, 4 * P]) for i in range(4)]
        b_o = ps("b_o", [P, 4 * P]); b_p = ps("b_p", [P, 4 * P])
        slotsT = b_in[:, 0:SLOTS].bitcast(f16).rearrange("p (a n) -> p a n", a=2)
        y_ps = b_t[:, :, :].rearrange("p a c -> p (a c)").bitcast(f32)
        up_banks = [(b_e[0], b_e[1], b_e[2]), (b_e[3], b_o, b_p)]
        delta, outT = b_o[:, 0:P], b_o[:, P:2 * P]
        p2 = b_p[:, 0:2 * P]
        x1T_ps = b_p[:, 2 * P:3 * P].bitcast(f16)
        lg_ps = b_p[:, 3 * P:3 * P + 8]
        rank_ps, total_ps = b_p[:, 3 * P + 8:3 * P + 16], b_p[:, 3 * P + 16:3 * P + 24]

        weights_loaded = sem("weights_loaded"); x_loaded = sem("x_loaded"); xT_loaded = [sem(f"xT_loaded{k}") for k in range(U)]
        setup_act = sem("setup_act"); setup_products = sem("setup_products"); setup_dve = sem("setup_dve"); setup_pool = sem("setup_pool")
        attended = sem("attended"); base_moved = sem("base_moved"); base_set = sem("base_set")
        choice_marked = sem("choice_marked"); cos_done = sem("cos_done"); delta_done = sem("delta_done")
        delta_kept = sem("delta_kept"); delta_masked = sem("delta_masked"); dummy_rows_stored = sem("dummy_rows_stored")
        expert_found = sem("expert_found"); expert_numbered = sem("expert_numbered")
        expert_y_done = sem("expert_y_done")
        ffn_loaded = sem("ffn_loaded"); fill_rows_stored = sem("fill_rows_stored")
        final_moments = sem("final_moments"); final_rstd = sem("final_rstd"); final_stats = sem("final_stats")
        final_var_eps = sem("final_var_eps"); first_added = sem("first_added"); gap_done = sem("gap_done")
        gap_tanh_done = sem("gap_tanh_done"); gate_tanh_done = sem("gate_tanh_done"); gated = sem("gated")
        hidden_done = sem("hidden_done"); inner_rstd_done = sem("inner_rstd_done"); inner_var_eps = sem("inner_var_eps")
        logits_copied = sem("logits_copied"); logits_done = sem("logits_done"); max_found = sem("max_found")
        meta_copied = sem("meta_copied"); normalised = sem("normalised"); one_hot_done = sem("one_hot_done")
        out_stored = sem("out_stored"); place_picked = sem("place_picked"); place_summed = sem("place_summed")
        projected = sem("projected"); projected_out = sem("projected_out"); qkT_copied = sem("qkT_copied")
        qk_hi_done = sem("qk_hi_done"); qk_lo_done = sem("qk_lo_done"); qk_silu_done = sem("qk_silu_done")
        qk_turned = sem("qk_turned"); rank_based = sem("rank_based"); ranked = sem("ranked")
        roped = sem("roped"); second_added = sem("second_added"); shared_added = sem("shared_added")
        shared_gate_done = sem("shared_gate_done"); shared_hidden_done = sem("shared_hidden_done"); shared_silu_done = sem("shared_silu_done")
        shared_up_done = sem("shared_up_done"); shared_y_done = sem("shared_y_done"); sin_done = sem("sin_done")
        slots_copied = sem("slots_copied"); slots_turned = sem("slots_turned"); squares_summed = sem("squares_summed")
        state_added = sem("state_added"); state_hi_done = sem("state_hi_done"); state_lo_done = sem("state_lo_done")
        table_loaded = sem("table_loaded"); table_made = sem("table_made"); table_step = sem("table_step")
        v_hi_done = sem("v_hi_done"); v_lo_done = sem("v_lo_done"); v_spread = sem("v_spread")
        weights_hi_done = sem("weights_hi_done"); weights_lo_done = sem("weights_lo_done"); weights_padded = sem("weights_padded")
        x1T_copied = sem("x1T_copied"); x1_done = sem("x1_done"); x1_hi_done = sem("x1_hi_done")
        x1_lo_done = sem("x1_lo_done"); x1_moments = sem("x1_moments"); x1_rstd_done = sem("x1_rstd_done")
        x1_stats = sem("x1_stats"); x1_turned = sem("x1_turned"); x1_var_eps = sem("x1_var_eps")
        x_biased = sem("x_biased"); x_summed = sem("x_summed")
        final_recip = sem("final_recip")
        expert_up_done = [sem(f"expert_up_done{c}") for c in range(IC)]; expert_silu_done = [sem(f"expert_silu_done{c}") for c in range(IC)]
        energies_done = [sem(f"energies_done{h}") for h in range(4)]; masked = [sem(f"masked{h}") for h in range(4)]
        rows_scattered = [sem(f"rows_scattered{k}") for k in range(U)]
        slots_loaded = [sem(f"slots_loaded{k}") for k in range(U)]
        placed = [sem(f"placed{k}") for k in range(U)]; weighed = [sem(f"weighed{k}") for k in range(U)]
        yscaled = [sem(f"yscaled{k}") for k in range(U)]
        y_scattered = [sem(f"y_scattered{k}") for k in range(U)]
        fst = sb("fst", [P, TILES, 6]); fmv = sb("fmv", [P, TILES, 2]); frs = sb("frs", [P, TILES]); fve = sb("fve", [P, TILES]); fnb = sb("fnb", [P, TILES])
        results_loaded = [sem(f"results_loaded{k}") for k in range(FINALS)]
        block = ctx.enter_context(nc.Block())

        def steps(eng, body, n=TILES, u=U):
            for i in range(2):
                for j in range(u):
                    body(i, j, i == 0, False)
            with eng.Fori(2, n // u - 1) as i:
                for j in range(u):
                    body(i, j, False, False)
            for j in range(u):
                body(n // u - 1, j, False, True)

        def exists(t):
            return not isinstance(t, int) or t >= 0

        def stage(i, j, lag, first, last, u=U):
            k = j + lag
            ok = not ((first and k < 0) or (last and k >= u))
            return ok, u * i + k, k % u, i + k // u

        @block.sync
        def _(sp):
            sp.dma_start(cst[:, :], consts).then_inc(weights_loaded, 16)
            sp.dma_start(w_in[:, 0:3 * P], Wqkv).then_inc(weights_loaded, 16)
            sp.dma_start(g1T[:, :], Wg1T).then_inc(weights_loaded, 16)
            sp.dma_start(g2[:, :], Wg2).then_inc(weights_loaded, 16)
            sp.dma_start(wo[:, :], Wo).then_inc(weights_loaded, 16)
            sp.dma_start(lnc[:, :], ln).then_inc(weights_loaded, 16)
            sp.dma_start(gw[:, :], gate_w).then_inc(weights_loaded, 16)
            sp.dma_start(half[:, :], halves).then_inc(weights_loaded, 16)
            for k in range(U):
                sp.dma_start(xTr[:, k, :], xT[:, k * P:(k + 1) * P]).then_inc(xT_loaded[k], 16)
            for b in range(4):
                sp.dma_start(x_sb[:, 8 * b:8 * b + 8, :], x[SEQ * b:SEQ * (b + 1), :].rearrange("(t p) c -> p t c", p=P)).then_inc(x_loaded, 16)
            sp.dma_start(ind[:, :], indices).then_inc(ffn_loaded, 16)
            sp.dma_start(sst_[:, :, :], Sgu).then_inc(ffn_loaded, 16)
            sp.dma_start(wst[:, :, 0, :], Wg.rearrange("e h i -> h e i")).then_inc(ffn_loaded, 16)
            sp.dma_start(wst[:, :, 1, :], Wu.rearrange("e h i -> h e i")).then_inc(ffn_loaded, 16)
            wdv = wd[:, :, :].rearrange("p e (c h) -> p e c h", c=IC)
            for c in range(IC):
                n = min(P, INNER - c * P)
                sp.dma_start(wdv[0:n, :, c, :], Wd[:, c * P:c * P + n, :].rearrange("e i h -> i e h")).then_inc(ffn_loaded, 16)
            sp.dma_start(sd[:, 0, :], Sd[0:P, :]).then_inc(ffn_loaded, 16)
            sp.dma_start(sd[0:SHARED - P, 1, :], Sd[P:SHARED, :]).then_inc(ffn_loaded, 16)
            sp.dma_start(rows[EXPERTS * REGION:EXPERTS * REGION + DUMMY * SLOTS, :], pads[EXPERTS * SLOTS:, :]).then_inc(dummy_rows_stored, 16)
            with sp.Fori(0, TILES // U - 1) as i:
                for j in range(U):
                    sp.wait_ge(projected, U * i + j + 1)
                    sp.dma_start(xTr[:, j, :], xT[:, bass.ds((U * i + j + U) * P, P)]).then_inc(xT_loaded[j], 16)
            sp.wait_ge(table_made, 2)
            sp.dma_start(tabr[0:1, :], tab[:, :]).then_inc(table_loaded, 16)
            for e in range(EXPERTS):
                end = sp.value_load(ends[0:1, e:e + 1], min_val=0, max_val=EXPERTS * REGION)
                sp.dma_start(rows[bass.ds(end, SLOTS), :], pads[e * SLOTS:(e + 1) * SLOTS, :]).then_inc(fill_rows_stored, 16)
            sp.wait_ge(table_loaded, 16)
            for k in range(U):
                sp.wait_ge(rows_scattered[k], 2 * 16 * (TILES // U))
            sp.wait_ge(fill_rows_stored, 16 * EXPERTS)
            sp.wait_ge(dummy_rows_stored, 16)

            def load(i, j, first, last):
                t = U * i + j
                at = sp.value_load(tabr[0:1, bass.ds(2 * t, 1)], min_val=0, max_val=EXPERTS * REGION + (DUMMY - 1) * SLOTS)
                at = sp.snap(at)
                if exists(t - U):
                    sp.wait_ge(slots_turned, t - U + 1)
                    sp.wait_ge(meta_copied, t - U + 1)
                    sp.wait_ge(table_loaded, 16)
                sp.dma_start(xin[:, j, :, :], rows[bass.ds(at, SLOTS), :].rearrange("(b p) w -> p b w", p=P)).then_inc(slots_loaded[j], 16)
            steps(sp, load, SLOT_TILES)

            for k in range(U):
                sp.wait_ge(y_scattered[k], 32 * (SLOT_TILES // U))
            for q in range(FINALS):
                for c, dst in enumerate((y0, y1)):
                    sp.dma_start(dst[:, FT * q:FT * q + FT, :], ydram[c * TOKENS + q * FT * P:c * TOKENS + (q + 1) * FT * P, :]
                                 .rearrange("(t p) c -> p t c", p=P)).then_inc(results_loaded[q], 16)
            for q in range(FINALS):
                sp.wait_ge(normalised, FT * (q + 1))
                sp.dma_start(out[q * FT * P:(q + 1) * FT * P, :].rearrange("(t p) c -> p t c", p=P), x1[:, FT * q:FT * q + FT, :]).then_inc(out_stored, 16)
            sp.wait_ge(out_stored, 16 * FINALS)

        @block.tensor
        def _(pe):
            pe.wait_ge(weights_loaded, 128)
            pe.wait_ge(setup_dve, 3)
            nc.tensor.matmul(b_p[:, 0:P], C("center"), wos[:, :], start=True, stop=True)
            nc.tensor.matmul(b_p[:, P:2 * P], g1T[:, :], g2[:, :], start=True, stop=True)
            nc.tensor.matmul(b_p[:, 2 * P:3 * P], lnbb[:, :], wo[:, :], start=True, stop=True).then_inc(setup_products, 1)

            def proj(i, j, first, last, lag):
                ok, t, k, r = stage(i, j, lag, first, last)
                if not ok:
                    return
                pe.wait_ge(xT_loaded[k], 16 * (r + 1))
                if exists(t - 1):
                    pe.wait_ge(v_hi_done, t)
                nc.tensor.matmul(b_in[:, 0:3 * P], xTr[:, k, :], w_in[:, 0:3 * P], start=True, stop=True)
                nc.tensor.matmul(b_in[:, 3 * P:], w_in[:, 3 * P:], xTr[:, k, :], start=True, stop=True).then_inc(projected, 1)

            def qk_turn(i, j, first, last, lag):
                ok, t, k, r = stage(i, j, lag, first, last)
                if not ok:
                    return
                pe.wait_ge(qk_lo_done, t + 1); pe.wait_ge(qk_hi_done, t + 1)
                if exists(t - 1):
                    pe.wait_ge(qkT_copied, t)
                for b in range(2 * BLOCKS):
                    mm = nc.tensor.transpose(b_t[:, b, :], qk16[:, k, b * P:(b + 1) * P], idh)
                mm.then_inc(qk_turned, 1)

            def energies(i, j, first, last):
                t = U * i + j
                pe.wait_ge(qkT_copied, t + 1)
                for pair in ((0, 1), (2, 3)):
                    if exists(t - 1):
                        for h4 in pair:
                            pe.wait_ge(masked[h4], t)
                    for b in range(BLOCKS):
                        for h4 in pair:
                            rows = slice(32 * h4, 32 * h4 + 32)
                            mm = nc.tensor.matmul(b_e[h4][:, b * P:(b + 1) * P], qkT[rows, j % 2, 4 + b, :],
                                                  qkT[rows, j % 2, b, :], start=True, stop=True)
                            if b == BLOCKS - 1:
                                mm.then_inc(energies_done[h4], 1)

            def state(i, j, first, last):
                t = U * i + j
                pe.wait_ge(v_lo_done, t + 1); pe.wait_ge(v_hi_done, t + 1)
                if exists(t - 1):
                    pe.wait_ge(gated, t)
                for b in range(BLOCKS):
                    kk = qk16[:, j, (4 + b) * P:(5 + b) * P]
                    o = delta[:, 32 * b:32 * b + 32]
                    vcol = slice(32 * b, 32 * b + 32)
                    nc.tensor.matmul(o, kk, vh[:, j, vcol], start=True, stop=False)
                    mm = nc.tensor.matmul(o, kk, vl[:, j, vcol], start=False, stop=True)
                mm.then_inc(delta_done, 1)

            def attend(i, j, first, last):
                t = U * i + j
                pe.wait_ge(delta_masked, t + 1)
                for h4 in range(4):
                    pe.wait_ge(masked[h4], t + 1)
                    for b in range(BLOCKS):
                        cols = slice(32 * b, 32 * b + 32)
                        nc.tensor.matmul(outT[cols, :], vexp[:, j, h4, cols], em[:, j % 2, h4, b * P:(b + 1) * P],
                                         start=(h4 == 0), stop=False, tile_position=(0, 32 * b))
                pe.wait_ge(state_lo_done, t + 1)
                for b in range(BLOCKS):
                    cols = slice(32 * b, 32 * b + 32)
                    nc.tensor.matmul(outT[cols, :], shi[:, j % 2, cols], qkT[:, j % 2, b, :], start=False, stop=False, tile_position=(0, 32 * b))
                    mm = nc.tensor.matmul(outT[cols, :], slo[:, j % 2, cols], qkT[:, j % 2, b, :], start=False, stop=True, tile_position=(0, 32 * b))
                mm.then_inc(attended, 1)

            def router(i, j, first, last, lag):
                ok, t, k, r = stage(i, j, lag, first, last)
                if not ok:
                    return
                pe.wait_ge(x1T_copied, t + 1)
                xh, xl = x1Tr[:, 0, bass.ds(t * P, P)], x1Tr[:, 1, bass.ds(t * P, P)]
                nc.tensor.matmul(lg_ps, xh, gwh[:, :], start=True, stop=False)
                nc.tensor.matmul(lg_ps, xl, gwh[:, :], start=False, stop=False)
                nc.tensor.matmul(lg_ps, xh, gwl[:, :], start=False, stop=True).then_inc(logits_done, 1)

            def rank(i, j, first, last, lag):
                ok, t, k, r = stage(i, j, lag, first, last)
                if not ok:
                    return
                pe.wait_ge(choice_marked, t + 1)
                nc.tensor.matmul(rank_ps, before, chosen[:, k % 2, :], start=True, stop=True)
                nc.tensor.matmul(total_ps, onesh, chosen[:, k % 2, :], start=True, stop=True).then_inc(ranked, 1)

            def proj2(i, j, first, last, lag):
                ok, t, k, r = stage(i, j, lag, first, last)
                if not ok:
                    return
                pe.wait_ge(gated, t + 1)
                if exists(t - 2):
                    pe.wait_ge(x1T_copied, t - 1)
                if exists(t - 4):
                    pe.wait_ge(base_moved, t - 3)
                nc.tensor.matmul(p2, og[:, k % 2, :], rhs2[:, :], start=True, stop=True).then_inc(projected_out, 1)

            def x1_turn(i, j, first, last, lag):
                ok, t, k, r = stage(i, j, lag, first, last)
                if not ok:
                    return
                pe.wait_ge(x1_lo_done, t + 1); pe.wait_ge(x1_hi_done, t + 1)
                pe.wait_ge(x_summed, t + 2 if lag else TILES)
                if exists(t - 1):
                    pe.wait_ge(logits_copied, t)
                if lag and exists(t - 2):
                    pe.wait_ge(base_moved, t - 1)
                nc.tensor.transpose(x1T_ps[:, 0:P], x1hl[:, k % 2, 0, :], idh)
                nc.tensor.transpose(x1T_ps[:, P:2 * P], x1hl[:, k % 2, 1, :], idh).then_inc(x1_turned, 1)

            pe.wait_ge(setup_act, 4)
            proj(0, 0, True, False, 0)
            proj(0, 0, True, False, 1)
            qk_turn(0, 0, True, False, 0)

            def body(i, j, first, last):
                energies(i, j, first, last)
                state(i, j, first, last)
                router(i, j, first, last, -3)
                rank(i, j, first, last, -4)
                proj2(i, j, first, last, -1)
                proj(i, j, first, last, 2)
                qk_turn(i, j, first, last, 1)
                attend(i, j, first, last)
                x1_turn(i, j, first, last, -2)
            steps(pe, body)
            L = TILES // U - 1
            pe.wait_ge(x1T_copied, TILES - 2); pe.wait_ge(squares_summed, TILES - 1)
            rank(L, 0, False, False, 0)
            router(L, U - 3, False, False, 0)
            pe.wait_ge(base_moved, TILES - U + 1); pe.wait_ge(logits_copied, TILES - 2)
            proj2(L, U - 1, False, False, 0)
            for k in (U - 2, U - 1):
                pe.wait_ge(base_moved, TILES - U + k - 1); pe.wait_ge(logits_copied, TILES - U + k)
                x1_turn(L, k, False, False, 0)
                pe.wait_ge(x1T_copied, TILES - U + k + 1)
                rank(L, k - 1, False, False, 0)
                router(L, k, False, False, 0)
            pe.wait_ge(logits_copied, TILES); pe.wait_ge(base_moved, TILES - 1)
            rank(L, U - 1, False, False, 0)

            pe.wait_ge(weights_hi_done, TILES // U + 1); pe.wait_ge(weights_lo_done, TILES // U + 1)
            pe.wait_ge(x1T_copied, TILES)
            pe.wait_ge(weights_padded, 4)
            pe.wait_ge(ffn_loaded, FFN_LOADS)
            pe.wait_ge(base_moved, TILES)

            def shared_up(q):
                for c in range(SC):
                    if q:
                        pe.wait_ge(shared_hidden_done, 2 * q - 1 + c)
                    for gu in range(2):
                        bank = b_e[2 * gu + c][:, :]
                        w, wlo = sh[:, gu, c * P:(c + 1) * P], sl[:, gu, c * P:(c + 1) * P]
                        xh, xl = x1Tr[:, 0, q * 512:(q + 1) * 512], x1Tr[:, 1, q * 512:(q + 1) * 512]
                        nc.tensor.matmul(bank, w, xh, start=True, stop=False)
                        nc.tensor.matmul(bank, w, xl, start=False, stop=False)
                        nc.tensor.matmul(bank, wlo, xh, start=False, stop=True).then_inc(shared_up_done if gu else shared_gate_done, 1)

            def shared_down(q):
                k = q % 2
                pe.wait_ge(shared_hidden_done, 2 * q + 2)
                if q >= 2:
                    pe.wait_ge(shared_added, q - 1)
                for n in range(4):
                    o = (b_o, b_p)[k % 2][:, n * P:(n + 1) * P]
                    nc.tensor.matmul(o, hS[:, k, 0, n * P:(n + 1) * P], sd[:, 0, :], start=True, stop=False)
                    mm = nc.tensor.matmul(o, hS[0:SHARED - P, k, 1, n * P:(n + 1) * P], sd[0:SHARED - P, 1, :], start=False, stop=True)
                mm.then_inc(shared_y_done, 1)

            for q in range(8):
                shared_up(q)
                if q:
                    shared_down(q - 1)
            shared_down(7)

            pe.wait_ge(table_loaded, 16)
            pe.wait_ge(shared_hidden_done, 16); pe.wait_ge(shared_added, 8)

            def turn(i, j, first, last, lag):
                ok, t, k, r = stage(i, j, lag, first, last)
                if not ok:
                    return
                pe.wait_ge(slots_loaded[k], 16 * (r + 1))
                for b in range(2):
                    for a in range(2):
                        mm = nc.tensor.transpose(slotsT[:, a, b * P:(b + 1) * P], xin[:, k, b, 64 * a:64 * a + 64].bitcast(f16), idh)
                mm.then_inc(slots_turned, 1)

            def expert_of(t):
                return pe.value_load(tabr[0:1, bass.ds(2 * t + 1, 1)], min_val=0, max_val=EXPERTS - 1)

            def up(i, j, first, last, e):
                t = U * i + j
                pe.wait_ge(slots_copied, t + 1)
                for c in range(IC):
                    for gu in range(2):
                        o = up_banks[j % 2][c][:, gu * SLOTS:(gu + 1) * SLOTS]
                        at = e * (2 * IC * P) + (gu * IC + c) * P
                        w, wlo = whf[:, bass.ds(at, P)], wlf[:, bass.ds(at, P)]
                        nc.tensor.matmul(o, w, xs16[:, j % 2, 0, :], start=True, stop=False)
                        nc.tensor.matmul(o, w, xs16[:, j % 2, 1, :], start=False, stop=False)
                        mm = nc.tensor.matmul(o, wlo, xs16[:, j % 2, 0, :], start=False, stop=True)
                    mm.then_inc(expert_up_done[c], 1)

            def down(i, j, first, last, lag, e):
                ok, t, k, r = stage(i, j, lag, first, last)
                if not ok:
                    return
                pe.wait_ge(hidden_done, t + 1)
                if exists(t - 1):
                    pe.wait_ge(yscaled[(j + lag - 1) % U], i + (j + lag - 1) // U + 1)
                for b in range(2):
                    for c in range(IC):
                        n = min(P, INNER - c * P)
                        mm = nc.tensor.matmul(y_ps[:, b * P:(b + 1) * P], hT[0:n, k % 2, c, b * P:(b + 1) * P],
                                              wdf[0:n, bass.ds(e * (IC * P) + c * P, P)], start=(c == 0), stop=(c == IC - 1))
                mm.then_inc(expert_y_done, 1)

            turn(0, 0, True, False, 0)
            owner = [None] * U

            def experts(i, j, first, last):
                t = U * i + j
                before = owner[j - 1] if j else (expert_of(t - 1) if exists(t - 1) else None)
                owner[j] = expert_of(t)
                up(i, j, first, last, owner[j])
                turn(i, j, first, last, 1)
                down(i, j, first, last, -1, before)
            steps(pe, experts, SLOT_TILES)
            down(SLOT_TILES // U - 1, U - 1, False, False, 0, owner[U - 1])

        @block.scalar
        def _(act):
            act.wait_ge(weights_loaded, 128)
            act.wait_ge(setup_products, 1)
            nc.scalar.activation(rhs2[:, P:], b_p[:, 0:P], ACT.Copy, scale=math.sqrt(CH)).then_inc(setup_act, 1)
            nc.scalar.activation(w_in[:, 3 * P:], b_p[:, P:2 * P], ACT.Copy).then_inc(setup_act, 1)
            nc.scalar.activation(brow[:, :], b_p[:, 2 * P:3 * P], ACT.Copy).then_inc(setup_act, 1)
            nc.scalar.activation(rhs2[:, 0:P], C("center"), ACT.Copy).then_inc(setup_act, 1)
            act.wait_ge(setup_pool, 6)

            def evac(i, j, first, last, lag):
                ok, t, k, r = stage(i, j, lag, first, last)
                if not ok:
                    return
                act.wait_ge(projected, t + 1)
                if exists(t - U):
                    act.wait_ge(cos_done, t - U + 1); act.wait_ge(sin_done, t - U + 1)
                nc.scalar.activation(qk[:, k, :], b_in[:, 0:2 * P], ACT.Silu).then_inc(qk_silu_done, 1)
                if exists(t - U):
                    act.wait_ge(gated, t - U + 1)
                nc.scalar.activation(th[:, k, :], b_in[:, 3 * P:], ACT.Tanh, scale=0.5).then_inc(gate_tanh_done, 1)
                if exists(t - U):
                    act.wait_ge(attended, t - U + 1)
                nc.scalar.activation(vdiag(k), b_in[:, 2 * P:3 * P].rearrange("p (b h d) -> p h b d", b=4, h=4),
                                     ACT.Copy).then_inc(v_spread, 1)
                if exists(t - U):
                    act.wait_ge(delta_done, t - U + 1)
                nc.scalar.activation(vh[:, k, :], b_in[:, 2 * P:3 * P], ACT.Copy).then_inc(v_hi_done, 1)

            def hi16(i, j, first, last, lag):
                ok, t, k, r = stage(i, j, lag, first, last)
                if not ok:
                    return
                act.wait_ge(roped, t + 1)
                if exists(t - U):
                    act.wait_ge(qk_turned, t - U + 1); act.wait_ge(delta_done, t - U + 1)
                out = bass.AP(qk16, offset=k * 8 * P, ap=[[U * 8 * P, P], [4 * P + HD, 2], [32, HEADS], [HD, 2], [1, HD]])
                src = bass.AP(rc, offset=k * 2 * P, ap=[[U * 2 * P, P], [P, 2], [HD, HEADS], [0, 2], [1, HD]])
                nc.scalar.activation(out, src, ACT.Copy).then_inc(qk_hi_done, 1)

            def squares(i, j, first, last, lag):
                ok, t, k, r = stage(i, j, lag, first, last)
                if not ok:
                    return
                act.wait_ge(projected_out, t + 1)
                act.wait_ge(squares_summed, t) if exists(t - 1) else None
                nc.scalar.activation(sqj[:, :], p2[:, 0:P], ACT.Square, accum_out=vsum[:, k:k + 1]).then_inc(squares_summed, 1)

            def logit_out(i, j, first, last, lag):
                ok, t, k, r = stage(i, j, lag, first, last)
                if not ok:
                    return
                act.wait_ge(logits_done, t + 1)
                if exists(t - 2):
                    act.wait_ge(expert_found, t - 1)
                nc.scalar.activation(lg[:, k, :], lg_ps, ACT.Copy).then_inc(logits_copied, 1)

            def payload(i, j, first, last, lag):
                ok, t, k, r = stage(i, j, lag, first, last)
                if not ok:
                    return
                act.wait_ge(x1_lo_done, t + 1); act.wait_ge(x1_hi_done, t + 1)
                if exists(t - U):
                    act.wait_ge(rows_scattered[k], 32 * r)
                both = x1hl[:, k % 2, :, :].rearrange("p a c -> p (a c)").unsqueeze(1).broadcast_to([P, TOP, 2 * P])
                nc.scalar.activation(pay16(k), both, ACT.Copy)

            def weights(i, j, first, last, lag):
                ok, t, k, r = stage(i, j, lag, first, last)
                if not ok:
                    return
                act.wait_ge(gap_done, t + 1)
                nc.scalar.activation(tw[:, k:k + 1], gap[:, k:k + 1], ACT.Tanh, scale=0.5).then_inc(gap_tanh_done, 1)
                act.wait_ge(gap_tanh_done, t + 1)
                if exists(t - U):
                    act.wait_ge(rows_scattered[k], 32 * r)
                nc.scalar.activation(pay[:, k, 0, WEIGHT:WEIGHT + 1], tw[:, k:k + 1], ACT.Copy, scale=0.5, bias=0.5)
                nc.scalar.activation(pay[:, k, 1, WEIGHT:WEIGHT + 1], tw[:, k:k + 1], ACT.Copy, scale=-0.5, bias=0.5).then_inc(weighed[k], 1)

            def split(i, first):
                if first:
                    act.wait_ge(ffn_loaded, FFN_LOADS)
                    nc.scalar.activation(sh[:, :, 0:SHARED], sst_[:, :, :], ACT.Copy).then_inc(weights_hi_done, 1)
                n = 2 * INNER
                nc.scalar.activation(wh3[:, bass.ds(2 * i, 2), 0:INNER], wst3[:, bass.ds(2 * i, 2), :], ACT.Copy).then_inc(weights_hi_done, 1)

            def x1hi(i, j, first, last, lag):
                ok, t, k, r = stage(i, j, lag, first, last)
                if not ok:
                    return
                act.wait_ge(x1_done, t + 1)
                if exists(t - 2):
                    act.wait_ge(x1_turned, t - 1); 
                nc.scalar.activation(x1hl[:, k % 2, 0, :], x1[:, t, :], ACT.Copy).then_inc(x1_hi_done, 1)

            evac(0, 0, True, False, 0); evac(0, 0, True, False, 1)
            hi16(0, 0, True, False, 0); hi16(0, 0, True, False, 1)

            def body(i, j, first, last):
                if stage(i, j, -1, first, last)[0]:
                    act.wait_ge(projected_out, U * i + j)
                logit_out(i, j, first, last, -3)
                squares(i, j, first, last, -1)
                payload(i, j, first, last, -3)
                evac(i, j, first, last, 2)
                hi16(i, j, first, last, 2)
                if j == 1:
                    split(i, first)
                weights(i, j, first, last, -3)
                x1hi(i, j, first, last, -1)
            steps(act, body)
            L = TILES // U - 1
            logit_out(L, U - 3, False, False, 0)
            squares(L, U - 1, False, False, 0)
            payload(L, U - 3, False, False, 0)
            weights(L, U - 3, False, False, 0)
            x1hi(L, U - 1, False, False, 0)
            for k in (U - 2, U - 1):
                logit_out(L, k, False, False, 0)
                payload(L, k, False, False, 0)
                weights(L, k, False, False, 0)

            for q in range(8):
                for c in range(SC):
                    act.wait_ge(shared_gate_done, 2 * q + c + 1)
                    if q >= 2:
                        act.wait_ge(shared_hidden_done, 2 * (q - 2) + c + 1)
                    elif q == 0 and c == 0:
                        act.wait_ge(attended, TILES)
                    nc.scalar.activation(sS[:, q % 2, c, :], b_e[c][:, :], ACT.Silu).then_inc(shared_silu_done, 1)

            def silu(i, j, first, last):
                t = U * i + j
                if exists(t - 2):
                    act.wait_ge(hidden_done, t - 1)
                for c in range(IC):
                    act.wait_ge(expert_up_done[c], t + 1)
                    nc.scalar.activation(sg[:, j % 2, c, :], up_banks[j % 2][c][:, 0:SLOTS], ACT.Silu).then_inc(expert_silu_done[c], 1)

            def scale(i, j, first, last, lag):
                ok, t, k, r = stage(i, j, lag, first, last)
                if not ok:
                    return
                act.wait_ge(expert_y_done, t + 1); act.wait_ge(meta_copied, t + 1)
                if exists(t - U):
                    act.wait_ge(y_scattered[k], 32 * r)
                for b in range(2):
                    ins = nc.scalar.activation(yb[:, k, b, :], y_ps[:, b * P:(b + 1) * P], ACT.Copy, scale=meta[:, k, b, 1:2])
                ins.then_inc(yscaled[k], 1)

            def experts(i, j, first, last):
                silu(i, j, first, last)
                scale(i, j, first, last, -1)
            steps(act, experts, SLOT_TILES)
            scale(SLOT_TILES // U - 1, U - 1, False, False, 0)

            for q in range(FINALS):
                cols = slice(FT * q, FT * q + FT)
                act.wait_ge(final_rstd, q + 1)
                for t in range(FT * q, FT * q + FT):
                    nc.scalar.activation(x1[:, t, :], x1[:, t, :], ACT.Identity, scale=frs[:, t:t + 1], bias=fnb[:, t:t + 1]).then_inc(normalised, 1)

        @block.vector
        def _(dve):
            dve.wait_ge(weights_loaded, 128)
            nc.vector.memset(ones[:, :], 1.0).then_inc(setup_dve, 1)
            nc.vector.tensor_copy(base[:, :], C("first")).then_inc(base_set, 1)
            nc.vector.memset(wh3[:, :, INNER:], 0.0).then_inc(weights_padded, 1)
            nc.vector.memset(wl3[:, :, INNER:], 0.0).then_inc(weights_padded, 1)
            nc.vector.memset(sh[:, :, SHARED:], 0.0).then_inc(weights_padded, 1)
            nc.vector.memset(sl[:, :, SHARED:], 0.0).then_inc(weights_padded, 1)
            nc.vector.tensor_scalar(wos[:, :], wo[:, :], lnc[:, 0:1], None, ALU.mult).then_inc(setup_dve, 1)
            dve.wait_ge(setup_dve, 1)
            nc.vector.tensor_scalar(lnbb[:, :], ones[:, :], lnc[:, 1:2], None, ALU.mult).then_inc(setup_dve, 1)
            nc.vector.tensor_copy(gwh[:, :], gw[:, :]).then_inc(setup_dve, 1)
            dve.wait_ge(setup_dve, 4)
            nc.vector.tensor_tensor(gwl[:, :], gw[:, :], gwh[:, :], ALU.subtract).then_inc(setup_dve, 1)

            def rope_cos(i, j, first, last, lag):
                ok, t, k, r = stage(i, j, lag, first, last)
                if not ok:
                    return
                dve.wait_ge(qk_silu_done, t + 1)
                if exists(t - U):
                    dve.wait_ge(qk_lo_done, t - U + 1); dve.wait_ge(qk_hi_done, t - U + 1)
                cos = cst[:, bass.ds(CONST_AT["cos"][0] + t * HD, HD)].unsqueeze(1).broadcast_to([P, 2 * HEADS, HD])
                nc.vector.tensor_tensor(rc[:, k, :].rearrange("p (h d) -> p h d", d=HD),
                                        qk[:, k, :].rearrange("p (h d) -> p h d", d=HD), cos, ALU.mult).then_inc(cos_done, 1)

            def rope_add(i, j, first, last, lag):
                ok, t, k, r = stage(i, j, lag, first, last)
                if not ok:
                    return
                dve.wait_ge(cos_done, t + 1); dve.wait_ge(sin_done, t + 1)
                nc.vector.tensor_tensor(rc[:, k, :], rc[:, k, :], rs[:, k, :], ALU.add).then_inc(roped, 1)

            def rope_lo(i, j, first, last, lag):
                ok, t, k, r = stage(i, j, lag, first, last)
                if not ok:
                    return
                dve.wait_ge(qk_hi_done, t + 1)
                v = lambda o, w: bass.AP(qk16, offset=k * 8 * P + o, ap=[[U * 8 * P, P], [w, 2], [32, HEADS], [1, HD]])
                nc.vector.tensor_tensor(v(2 * HD, 4 * P - 2 * HD), rc[:, k, :].rearrange("p (a h d) -> p a h d", a=2, d=HD),
                                        v(0, 4 * P + HD), ALU.subtract).then_inc(qk_lo_done, 1)

            def turn_evac(i, j, first, last, lag):
                ok, t, k, r = stage(i, j, lag, first, last)
                if not ok:
                    return
                dve.wait_ge(qk_turned, t + 1)
                if exists(t - 2):
                    dve.wait_ge(attended, t - 1)
                nc.vector.tensor_copy(qkT[:, k % 2, :, :], b_t[:, :, :]).then_inc(qkT_copied, 1)

            def mask(i, j, first, last, h4):
                t = U * i + j
                dve.wait_ge(energies_done[h4], t + 1)
                if exists(t - 2):
                    dve.wait_ge(attended, t - 1)
                tri = C("tri").unsqueeze(1).broadcast_to([P, BLOCKS, P])
                nc.vector.tensor_tensor(em[:, j % 2, h4, :].rearrange("p (b n) -> p b n", b=BLOCKS),
                                        b_e[h4][:, :].rearrange("p (b n) -> p b n", b=BLOCKS), tri, ALU.mult).then_inc(masked[h4], 1)

            def dmask(i, j, first, last):
                t = U * i + j
                dve.wait_ge(delta_done, t + 1)
                if exists(t - 2):
                    dve.wait_ge(state_hi_done, t - 1)
                if j < U - 1:
                    nc.vector.tensor_tensor(dm[:, j % 2, :], delta, C("own"), ALU.mult).then_inc(delta_masked, 1)
                    return
                keep = cst[:, bass.ds(CONST_AT["keep"][0] + t, 1)]
                nc.vector.scalar_tensor_tensor(out=dmk[:, :], in0=delta, scalar=keep, in1=C("own"),
                                               op0=ALU.mult, op1=ALU.mult).then_inc(delta_kept, 1)
                dve.wait_ge(delta_kept, i + 1); dve.wait_ge(state_added, t)
                nc.vector.scalar_tensor_tensor(out=dm[:, j % 2, :], in0=sacc[:, j % 2, :], scalar=keep, in1=dmk[:, :],
                                               op0=ALU.mult, op1=ALU.add).then_inc(delta_masked, 1)

            def gate(i, j, first, last):
                t = U * i + j
                dve.wait_ge(attended, t + 1); dve.wait_ge(gate_tanh_done, t + 1)
                if exists(t - 2):
                    dve.wait_ge(projected_out, t - 1)
                nc.vector.scalar_tensor_tensor(out=og[:, j % 2, :], in0=th[:, j, :], scalar=1.0, in1=outT,
                                               op0=ALU.add, op1=ALU.mult).then_inc(gated, 1)

            def tail(i, j, first, last, lag, part):
                ok, t, k, r = stage(i, j, lag, first, last)
                if not ok:
                    return
                k2 = k % 2
                if part == 1:
                    dve.wait_ge(inner_rstd_done, t + 1); dve.wait_ge(x_biased, t + 1)
                    nc.vector.scalar_tensor_tensor(out=xp[:, k2, :], in0=p2[:, P:2 * P], scalar=rstd[:, k:k + 1], in1=xbr[:, k2, :],
                                                   op0=ALU.mult, op1=ALU.add).then_inc(x_summed, 1)
                if part == 2:
                    dve.wait_ge(x_summed, t + 1)
                    nc.vector.bn_stats(st6[:, k2, :], xp[:, k2, :]).then_inc(x1_stats, 1)
                if part == 3:
                    nc.vector.bn_aggr(mv[:, k2, :], st6[:, k2, :]).then_inc(x1_moments, 1)
                if part == 5:
                    dve.wait_ge(x1_rstd_done, t + 1)
                    nc.vector.tensor_scalar(x1[:, t, :], xp[:, k2, :], mv[:, k2, 0:1], rstd2[:, k2:k2 + 1],
                                            ALU.subtract, ALU.mult).then_inc(x1_done, 1)
                if part == 6:
                    dve.wait_ge(x1_hi_done, t + 1)
                    nc.vector.tensor_tensor(x1hl[:, k2, 1, :], x1[:, t, :], x1hl[:, k2, 0, :], ALU.subtract).then_inc(x1_lo_done, 1)

            def x1T_evac(i, j, first, last, lag):
                ok, t, k, r = stage(i, j, lag, first, last)
                if not ok:
                    return
                dve.wait_ge(x1_turned, t + 1)
                if exists(t - 2):
                    dve.wait_ge(logits_done, t - 1)
                nc.vector.tensor_copy(x1Tr[:, :, bass.ds(t * P, P)], x1T_ps.rearrange("p (a c) -> p a c", a=2)).then_inc(x1T_copied, 1)

            def route(i, j, first, last, lag, part):
                ok, t, k, r = stage(i, j, lag, first, last)
                if not ok:
                    return
                k2 = k % 2
                if part == 0:
                    dve.wait_ge(weights_loaded, 128)
                    dve.wait_ge(logits_copied, t + 1)
                    if exists(t - 2):
                        dve.wait_ge(expert_found, t - 1)
                    nc.vector.max(mx[:, k2, :], lg[:, k, :]).then_inc(max_found, 1)
                if part == 1:
                    dve.wait_ge(weights_loaded, 128)
                    dve.wait_ge(max_found, t + 1)
                    nc.vector.max_index(ix[:, k2, :], mx[:, k2, :], lg[:, k, :]).then_inc(expert_found, 1)
                    if exists(t - U):
                        dve.wait_ge(weighed[k], r)
                    nc.vector.tensor_tensor(gap[:, k:k + 1], mx[:, k2, 0:1], mx[:, k2, 1:2], ALU.subtract).then_inc(gap_done, 1)
                if part == 2:
                    dve.wait_ge(expert_found, t + 1)
                    nc.vector.tensor_copy(ef[:, k2, :], ix[:, k2, 0:TOP]).then_inc(expert_numbered, 1)
                if part == 3:
                    dve.wait_ge(expert_numbered, t + 1)
                    nc.vector.tensor_tensor(oh[:, k2, :, :], C("iota").unsqueeze(1).broadcast_to([P, TOP, EXPERTS]),
                                            ef[:, k2, :].unsqueeze(2).broadcast_to([P, TOP, EXPERTS]), ALU.is_equal).then_inc(one_hot_done, 1)
                if part == 4:
                    dve.wait_ge(one_hot_done, t + 1)
                    if exists(t - 2):
                        dve.wait_ge(ranked, t - 1)
                    nc.vector.tensor_tensor(chosen[:, k2, :], oh[:, k2, 0, :], oh[:, k2, 1, :], ALU.add).then_inc(choice_marked, 1)
                if part == 5:
                    dve.wait_ge(ranked, t + 1)
                    if exists(t - 1):
                        dve.wait_ge(base_moved, t)
                    nc.vector.tensor_tensor(pe_[:, k2, :], rank_ps, base[:, :], ALU.add).then_inc(rank_based, 1)
                    dve.wait_ge(rank_based, t + 1)
                    nc.vector.tensor_tensor(base[:, :], total_ps, base[:, :], ALU.add).then_inc(base_moved, 1)
                if part == 6:
                    dve.wait_ge(rank_based, t + 1)
                    nc.vector.tensor_tensor(pr[:, k2, :, :], oh[:, k2, :, :], pe_[:, k2, :].unsqueeze(1).broadcast_to([P, TOP, EXPERTS]),
                                            ALU.mult).then_inc(place_picked, 1)
                if part == 7:
                    dve.wait_ge(place_picked, t + 1)
                    nc.vector.tensor_reduce(pf[:, k2, :], pr[:, k2, :, :], AX.X, ALU.add).then_inc(place_summed, 1)
                if part == 8:
                    dve.wait_ge(place_summed, t + 1)
                    if exists(t - U):
                        dve.wait_ge(rows_scattered[k], 32 * r)
                    nc.vector.tensor_copy(place[:, k, :], pf[:, k2, :])
                    nc.vector.tensor_copy(pay[:, k, :, DEST:DEST + 1].bitcast(i32), ind[:, bass.ds(TOP * t, TOP)].unsqueeze(2)).then_inc(placed[k], 1)

            for lag in (0, 1):
                rope_cos(0, 0, True, False, lag); rope_add(0, 0, True, False, lag); rope_lo(0, 0, True, False, lag)
            turn_evac(0, 0, True, False, 0)

            def body(i, j, first, last):
                x1T_evac(i, j, first, last, -3)
                dmask(i, j, first, last)
                for h4 in range(4):
                    mask(i, j, first, last, h4)
                tail(i, j, first, last, -2, 6)
                tail(i, j, first, last, -1, 1)
                route(i, j, first, last, -4, 5)
                rope_cos(i, j, first, last, 2)
                route(i, j, first, last, -4, 6)
                tail(i, j, first, last, -1, 2)
                route(i, j, first, last, -4, 7)
                rope_add(i, j, first, last, 2)
                route(i, j, first, last, -4, 8)
                route(i, j, first, last, -3, 0)
                if stage(i, j, -1, first, last)[0]:
                    dve.wait_ge(x1_stats, U * i + j)
                turn_evac(i, j, first, last, 1)
                tail(i, j, first, last, -1, 3)
                route(i, j, first, last, -3, 1)
                rope_lo(i, j, first, last, 2)
                route(i, j, first, last, -3, 2)
                gate(i, j, first, last)
                route(i, j, first, last, -3, 3)
                tail(i, j, first, last, -1, 5)
                route(i, j, first, last, -3, 4)
            dve.wait_ge(ffn_loaded, FFN_LOADS)
            steps(dve, body)
            L = TILES // U - 1
            def place_tile(k):
                for part in (5, 6, 7, 8):
                    route(L, k, False, False, 0, part)

            def choose(k):
                for part in range(5):
                    route(L, k, False, False, 0, part)
            x1T_evac(L, U - 3, False, False, 0)
            tail(L, U - 2, False, False, 0, 6)
            dve.wait_ge(logits_copied, TILES - 2)
            place_tile(0)
            choose(U - 3)
            for part in (1, 2, 3, 5):
                if part == 3:
                    dve.wait_ge(x1_stats, TILES)
                tail(L, U - 1, False, False, 0, part)
            for k in (U - 2, U - 1):
                x1T_evac(L, k, False, False, 0)
                if k == U - 2:
                    tail(L, U - 1, False, False, 0, 6)
                dve.wait_ge(logits_copied, TILES - U + k + 1)
                place_tile(k - 1)
                choose(k)
            place_tile(U - 1)

            link = [0]

            def chain(ins):
                link[0] += 1
                ins.then_inc(table_step, 1)
                dve.wait_ge(table_step, link[0])
            dve.wait_ge(base_moved, TILES)
            nc.vector.tensor_copy(ends[:, :], base[:, :]).then_inc(table_made, 1)
            chain(nc.vector.tensor_tensor(cnt[:, :], base[:, :], C("first"), ALU.subtract))
            chain(nc.vector.tensor_scalar(nti[:, :], cnt[:, :], float(SLOTS - 1), None, ALU.add))
            chain(nc.vector.tensor_scalar(ntj[:, :], nti[:, :], SLOTS.bit_length() - 1, None, ALU.logical_shift_right))
            chain(nc.vector.tensor_copy(nt[0][:, :], ntj[:, :]))
            for n in range(3):
                d = 1 << n
                nc.vector.tensor_copy(nt[n + 1][:, 0:d], nt[n][:, 0:d]).then_inc(table_step, 1)
                link[0] += 1
                chain(nc.vector.tensor_tensor(nt[n + 1][:, d:], nt[n][:, d:], nt[n][:, 0:EXPERTS - d], ALU.add))
            chain(nc.vector.tensor_scalar(ge[:, :], nt[3][:, :], C("row"), None, ALU.is_le))
            chain(nc.vector.tensor_tensor(gn[:, :], ge[:, :], nt[0][:, :], ALU.mult))
            chain(nc.vector.tensor_reduce(te[:, 0:1], ge[:, :], AX.X, ALU.add))
            chain(nc.vector.tensor_reduce(te[:, 1:2], gn[:, :], AX.X, ALU.add))
            chain(nc.vector.tensor_tensor(te[:, 2:3], C("row"), te[:, 1:2], ALU.subtract))
            chain(nc.vector.tensor_scalar(te[:, 3:4], te[:, 2:3], float(SLOTS), None, ALU.mult))
            chain(nc.vector.tensor_scalar(te[:, 4:5], te[:, 0:1], float(REGION), None, ALU.mult))
            chain(nc.vector.tensor_tensor(te[:, 5:6], te[:, 3:4], te[:, 4:5], ALU.add))
            chain(nc.vector.tensor_scalar(te[:, 6:7], te[:, 0:1], float(EXPERTS - 1), None, ALU.min))
            nc.vector.tensor_copy(tab[:, :], te[:, 5:7]).then_inc(table_made, 1)

            def shared_add(q):
                dve.wait_ge(shared_y_done, q + 1)
                xq = x1[:, 4 * q:4 * q + 4, :].rearrange("p t c -> p (t c)")
                nc.vector.tensor_tensor(xq, (b_o, b_p)[q % 2][:, :], xq, ALU.add).then_inc(shared_added, 1)

            dve.wait_ge(x1_hi_done, TILES)
            for q in range(8):
                for c in range(SC):
                    dve.wait_ge(shared_up_done, 2 * q + c + 1); dve.wait_ge(shared_silu_done, 2 * q + c + 1)
                    if q >= 2 and c == 0:
                        dve.wait_ge(shared_y_done, q - 1)
                    nc.vector.tensor_tensor(hS[:, q % 2, c, :], sS[:, q % 2, c, :], b_e[2 + c][:, :], ALU.mult).then_inc(shared_hidden_done, 1)
                if q:
                    shared_add(q - 1)
            shared_add(7)

            def evac(i, j, first, last, lag):
                ok, t, k, r = stage(i, j, lag, first, last)
                if not ok:
                    return
                dve.wait_ge(slots_turned, t + 1)
                nc.vector.tensor_copy(xs16[:, k % 2, :, :], slotsT).then_inc(slots_copied, 1)
                if exists(t - U):
                    dve.wait_ge(y_scattered[k], 32 * r)
                    dve.wait_ge(yscaled[k], r)
                nc.vector.tensor_copy(meta[:, k, :, :].bitcast(i32), xin[:, k, :, DEST:DEST + 2].bitcast(i32)).then_inc(meta_copied, 1)

            def hidden(i, j, first, last, c):
                t = U * i + j
                dve.wait_ge(expert_silu_done[c], t + 1)
                if c == 0 and exists(t - 2):
                    dve.wait_ge(expert_y_done, t - 1)
                ins = nc.vector.tensor_tensor(hT[:, j % 2, c, :], sg[:, j % 2, c, :], up_banks[j % 2][c][:, SLOTS:], ALU.mult)
                if c == IC - 1:
                    ins.then_inc(hidden_done, 1)

            evac(0, 0, True, False, 0)

            def experts(i, j, first, last):
                hidden(i, j, first, last, 0)
                hidden(i, j, first, last, 1)
                evac(i, j, first, last, 1)
                hidden(i, j, first, last, 2)
            steps(dve, experts, SLOT_TILES)

            def final_scale(q):
                cols = slice(FT * q, FT * q + FT)
                dve.wait_ge(final_recip, q + 1)
                nc.vector.scalar_tensor_tensor(out=fnb[:, cols], in0=fmv[:, cols, 0], scalar=-1.0, in1=frs[:, cols],
                                               op0=ALU.mult, op1=ALU.mult).then_inc(final_rstd, 1)

            for q in range(FINALS):
                a, b = FT * q, FT * (q + 1)
                dve.wait_ge(first_added, q + 1)
                nc.vector.tensor_tensor(x1[:, a:b, :], x1[:, a:b, :], y1[:, a:b, :], ALU.add).then_inc(second_added, 1)
                dve.wait_ge(second_added, q + 1)
                for t in range(a, b):
                    nc.vector.bn_stats(fst[:, t, :], x1[:, t, :]).then_inc(final_stats, 1)
                for t in range(a, b):
                    dve.wait_ge(final_stats, t + 1)
                    nc.vector.bn_aggr(fmv[:, t, :], fst[:, t, :]).then_inc(final_moments, 1)
                if q:
                    final_scale(q - 1)
            final_scale(FINALS - 1)

        @block.gpsimd
        def _(pool):
            nc.gpsimd.memset(vexp[:, :, :, :], 0.0).then_inc(setup_pool, 1)
            nc.gpsimd.memset(sacc[:, 0, :], 0.0).then_inc(setup_pool, 1)
            nc.gpsimd.memset(zero[:, :], 0.0).then_inc(setup_pool, 1)
            nc.gpsimd.memset(qk16[:, :, :], 0.0).then_inc(setup_pool, 1)
            nc.gpsimd.memset(shi[:, 0, :], 0.0).then_inc(setup_pool, 1)
            nc.gpsimd.memset(slo[:, 0, :], 0.0).then_inc(state_lo_done, 1)
            nc.gpsimd.memset(pay[:, :, :, :], 0.0).then_inc(setup_pool, 1)
            pool.wait_ge(weights_loaded, 128)

            def rope_sin(i, j, first, last, lag):
                ok, t, k, r = stage(i, j, lag, first, last)
                if not ok:
                    return
                pool.wait_ge(qk_silu_done, t + 1)
                if exists(t - U):
                    pool.wait_ge(roped, t - U + 1)
                for half in range(2):
                    sin = cst[:, bass.ds(CONST_AT["sin"][0] + t * HD + 4 * half, 4)].unsqueeze(1).broadcast_to([P, 2 * HEADS, 4])
                    a = qk[:, k, :].rearrange("p (h d) -> p h d", d=HD)
                    o = rs[:, k, :].rearrange("p (h d) -> p h d", d=HD)
                    ins = nc.gpsimd.tensor_tensor(o[:, :, 4 * half:4 * half + 4], a[:, :, 4 - 4 * half:8 - 4 * half], sin, ALU.mult)
                ins.then_inc(sin_done, 1)

            def v16(i, j, first, last, lag):
                ok, t, k, r = stage(i, j, lag, first, last)
                if not ok:
                    return
                v4 = lambda a: a[:, k, :].rearrange("p (b h d) -> p h b d", b=4, h=4)
                pool.wait_ge(v_hi_done, t + 1)
                nc.gpsimd.tensor_tensor(v4(vl), vdiag(k), v4(vh), ALU.subtract).then_inc(v_lo_done, 1)

            def st(i, j, first, last, part):
                t = U * i + j
                n = (j + 1) % 2
                o = j % 2
                before = zero[:, :] if j == U - 1 else sacc[:, o, :]
                if part == 0:
                    pool.wait_ge(delta_masked, t + 1)
                    if exists(t - 1):
                        pool.wait_ge(state_added, t); pool.wait_ge(state_lo_done, t + 1)
                    nc.gpsimd.tensor_tensor(sacc[:, n, :], before, dm[:, o, :], ALU.add).then_inc(state_added, 1)
                if part == 1:
                    if exists(t - 1):
                        pool.wait_ge(attended, t)
                    nc.gpsimd.tensor_tensor(shi[:, n, :], before, dm[:, o, :], ALU.add).then_inc(state_hi_done, 1)
                if part == 2:
                    pool.wait_ge(state_hi_done, t + 1)
                    nc.gpsimd.tensor_tensor(slo[:, n, :], sacc[:, n, :], shi[:, n, :], ALU.subtract).then_inc(state_lo_done, 1)

            def power(i, j, first, last, lag, part):
                ok, t, k, r = stage(i, j, lag, first, last)
                if not ok:
                    return
                small = C("small")
                if part == 0:
                    nc.gpsimd.tensor_tensor(ve[:, 0:1], vsum[:, k:k + 1], small[:, 0:1], ALU.add).then_inc(inner_var_eps, 1)
                    pool.wait_ge(inner_var_eps, t + 1)
                    nc.gpsimd.tensor_tensor(rstd[:, k:k + 1], ve[:, 0:1], small[:, 2:3], ALU.pow).then_inc(inner_rstd_done, 1)
                else:
                    nc.gpsimd.tensor_tensor(ve[:, 1:2], mv[:, k % 2, 1:2], small[:, 1:2], ALU.add).then_inc(x1_var_eps, 1)
                    pool.wait_ge(x1_var_eps, t + 1)
                    nc.gpsimd.tensor_tensor(rstd2[:, k % 2:k % 2 + 1], ve[:, 1:2], small[:, 2:3], ALU.pow).then_inc(x1_rstd_done, 1)

            def xb(i, j, first, last):
                t = U * i + j
                if exists(t - 2):
                    pool.wait_ge(x_summed, t - 1)
                nc.gpsimd.tensor_tensor(xbr[:, j % 2, :], x_sb[:, t, :], brow[:, :], ALU.add).then_inc(x_biased, 1)

            for lag in (0, 1):
                rope_sin(0, 0, True, False, lag); v16(0, 0, True, False, lag)
            pool.wait_ge(x_loaded, 64)
            pool.wait_ge(setup_act, 4)
            pool.wait_ge(ffn_loaded, FFN_LOADS)

            def scatter(i, j, first, last, lag):
                ok, t, k, r = stage(i, j, lag, first, last)
                if not ok:
                    return
                pool.wait_ge(ffn_loaded, FFN_LOADS)
                done = i + k0 if (k0 := (j + lag) // U + 1) else i
                pool.wait_ge(placed[k], done); pool.wait_ge(weighed[k], done)
                for c in range(TOP):
                    nc.gpsimd.indirect_dma_start(out=rows, out_offset=bass.IndirectOffsetOnAxis(ap=place[:, k, c:c + 1], axis=0),
                                                 in_=pay[:, k, c, :], in_offset=None).then_inc(rows_scattered[k], 16)

            def split(i, first):
                if first:
                    pool.wait_ge(weights_hi_done, 1)
                    nc.gpsimd.tensor_tensor(sl[:, :, 0:SHARED], sst_[:, :, :], sh[:, :, 0:SHARED], ALU.subtract).then_inc(weights_lo_done, 1)
                pool.wait_ge(weights_hi_done, i + 2)
                nc.gpsimd.tensor_tensor(wl3[:, bass.ds(2 * i, 2), 0:INNER], wst3[:, bass.ds(2 * i, 2), :],
                                        wh3[:, bass.ds(2 * i, 2), 0:INNER], ALU.subtract).then_inc(weights_lo_done, 1)

            def body(i, j, first, last):
                if stage(i, j, -1, first, last)[0]:
                    pool.wait_ge(squares_summed, U * i + j)
                st(i, j, first, last, 0)
                power(i, j, first, last, -1, 0)
                st(i, j, first, last, 1)
                st(i, j, first, last, 2)
                rope_sin(i, j, first, last, 2)
                v16(i, j, first, last, 2)
                if stage(i, j, -1, first, last)[0]:
                    pool.wait_ge(x1_moments, U * i + j)
                xb(i, j, first, last)
                power(i, j, first, last, -1, 1)
                if j == 2:
                    split(i, first)
                scatter(i, j, first, last, -4)
            steps(pool, body)
            L = TILES // U - 1
            pool.wait_ge(squares_summed, TILES)
            power(L, U - 1, False, False, 0, 0)
            pool.wait_ge(x1_moments, TILES)
            power(L, U - 1, False, False, 0, 1)
            for k in range(U):
                scatter(L, k, False, False, 0)
            with pool.Fori(1, SLOT_TILES // U + 1) as n:
                for j in range(U):
                    pool.wait_ge(table_made, 1); pool.wait_ge(yscaled[j], n)
                    for b in range(2):
                        nc.gpsimd.indirect_dma_start(out=ydram, out_offset=bass.IndirectOffsetOnAxis(ap=meta[:, j, b, 0:1].bitcast(u32), axis=0),
                                                     in_=yb[:, j, b, :], in_offset=None).then_inc(y_scattered[j], 16)

            def inverse_deviation(q):
                cols, small = slice(FT * q, FT * q + FT), C("small")
                pool.wait_ge(final_moments, FT * (q + 1))
                nc.gpsimd.tensor_tensor(fve[:, cols], fmv[:, cols, 1], small[:, 1:2].broadcast_to([P, FT]), ALU.add).then_inc(final_var_eps, 1)
                pool.wait_ge(final_var_eps, q + 1)
                nc.gpsimd.tensor_tensor(frs[:, cols], fve[:, cols], small[:, 2:3].broadcast_to([P, FT]), ALU.pow).then_inc(final_recip, 1)

            for q in range(FINALS):
                a, b = FT * q, FT * (q + 1)
                pool.wait_ge(results_loaded[q], 32)
                nc.gpsimd.tensor_tensor(x1[:, a:b, :], x1[:, a:b, :], y0[:, a:b, :], ALU.add).then_inc(first_added, 1)
                if q:
                    inverse_deviation(q - 1)
            inverse_deviation(FINALS - 1)


def kernel(**inputs):
    import numpy as _np
    import concourse.bacc as _bacc
    from concourse import mybir as _mybir
    from concourse.bass_utils import run_bass_kernel_spmd as _run

    a = lambda n: _np.asarray(inputs["L0_attn_" + n])
    f = lambda n: _np.asarray(inputs["L0_ffn_" + n])
    x = a("x").reshape(TOKENS, CH)
    data = dict(
        x=x, xT=x.T, Wqkv=_np.concatenate([a("Wq"), a("Wk"), a("Wv")], 1), Wg1T=a("Wg1").T, Wg2=a("Wg2"), Wo=a("Wo"),
        ln=_np.stack([a("ln_w"), a("ln_b")], 1), gate_w=f("gate_w"), Wg=f("Wg"), Wu=f("Wu"), Wd=f("Wd"),
        Sgu=_np.stack([f("Sg"), f("Su")], 1), Sd=f("Sd"),
        consts=constants()[0], halves=half_constants(), indices=index_constants(), pads=pad_rows())
    nc = _bacc.Bacc("TRN2", target_bir_lowering=False, num_devices=1)
    arrays, args = {}, {}
    for name, array in data.items():
        array = _np.ascontiguousarray(array)
        arrays["in_" + name] = array
        args[name] = nc.dram_tensor("in_" + name, array.shape, _mybir.dt.from_np(array.dtype), kind="ExternalInput").ap()
    out = nc.dram_tensor("out_0", (TOKENS, CH), _mybir.dt.float32, kind="ExternalOutput").ap()
    build(nc, out=out, **args)
    r = _run(nc, [arrays], core_ids=[0])
    return _np.asarray(r.results[0]["out_0"]).reshape(4, SEQ, CH)
```

```python
import math
from contextlib import ExitStack

import numpy as np
import concourse.bass as bass
from concourse import mybir

TOKENS, CH, HEADS, HD = 4096, 128, 16, 8
P = 128
TILES = TOKENS // P
SEQ = 1024
BATCH_TILES = SEQ // P
EPS = 1e-5
ROWS_PER_HEAD = 32
BLOCKS = 4
U = 4
EXPERTS, TOP, INNER, SHARED = 8, 2, 352, 176
IC = 3
SC = 2
SLOTS = 2 * P
REGION = TOKENS + SLOTS
SLOT_TILES = 40
DUMMY = SLOT_TILES - TOP * TOKENS // SLOTS
ROW = 132
DEST, WEIGHT = 128, 129
PEEL, TAIL, AFTER = 3, 1, 8
GROUPS = TILES // 4
FINALS, FT = 8, TILES // 8
YROWS = TOP * TOKENS + (EXPERTS + DUMMY) * SLOTS


def constants():
    f = np.float32
    d = HD
    inv = (f(1.0) / np.power(f(10000.0), np.arange(0, d, 2, dtype=f) / f(d))).astype(f)
    ang = (np.arange(SEQ, dtype=f)[:, None] * inv[None, :]).astype(f).astype(np.float64)
    cos = np.concatenate([np.cos(ang), np.cos(ang)], -1)
    sin = np.concatenate([-np.sin(ang), np.sin(ang)], -1)
    tab = lambda a: np.tile(a.reshape(BATCH_TILES, P, d).transpose(1, 0, 2), (1, TOKENS // SEQ, 1)).reshape(P, TILES * d)
    tri = (np.arange(P)[:, None] <= np.arange(P)[None, :])
    row = np.arange(P)
    col = np.arange(P)
    own = (row[:, None] // 32) == ((col[None, :] % 32) // 8)
    keep = np.tile(((np.arange(TILES) + 1) % BATCH_TILES != 0).astype(f)[None, :], (P, 1))
    center = 0.5 * (np.eye(P) - 1.0 / P)
    parts = {"cos": tab(cos), "sin": tab(sin), "tri": tri, "own": own, "keep": keep, "center": center,
             "iota": np.tile(np.arange(EXPERTS)[None, :], (P, 1)),
             "first": np.tile(np.arange(EXPERTS)[None, :] * REGION, (P, 1)),
             "row": np.arange(P)[:, None],
             "small": np.tile(np.array([[CH * EPS, EPS, -0.5]]), (P, 1))}
    at, n = {}, 0
    for k, a in parts.items():
        at[k] = (n, a.shape[1]); n += a.shape[1]
    return np.concatenate([np.asarray(a, f) for a in parts.values()], 1), at


def index_constants():
    p = np.arange(P)[:, None, None]
    pairs = (np.arange(TOP)[None, None, :] * TOKENS + np.arange(TILES)[None, :, None] * P + p).reshape(P, -1)
    return pairs.astype(np.int32)


def pad_rows():
    rows = np.zeros(((EXPERTS + DUMMY) * SLOTS, ROW), np.int32)
    rows[:, DEST] = TOP * TOKENS + np.arange(len(rows))
    return rows.view(np.float32)


def half_constants():
    r = np.arange(P)
    return np.concatenate([np.eye(P), r[:, None] < r[None, :], np.ones((P, P))], 1).astype(np.float16)


_, CONST_AT = constants()
CONST_W = sum(w for _, w in CONST_AT.values())


def build(nc, x, xT, Wqkv, Wg1T, Wg2, Wo, ln, gate_w, Wg, Wu, Wd, Sgu, Sd, consts, halves, indices, pads, out):
    f32, f16, i32, u32 = mybir.dt.float32, mybir.dt.float16, mybir.dt.int32, mybir.dt.uint32
    ALU, ACT, AX = mybir.AluOpType, mybir.ActivationFunctionType, mybir.AxisListType
    ctx = ExitStack()
    with ctx:
        sb = lambda n, s, d=f32: ctx.enter_context(nc.sbuf_tensor(n, s, d))
        ps = lambda n, s, d=f32: ctx.enter_context(nc.psum_tensor(n, s, d))
        sem = lambda n: ctx.enter_context(nc.semaphore(n))
        cst = sb("cst", [P, CONST_W])
        C = lambda k: cst[:, CONST_AT[k][0]:CONST_AT[k][0] + CONST_AT[k][1]]
        half = sb("half", [P, 3 * P], f16)
        idh, before, onesh = half[:, 0:P], half[:, P:2 * P], half[:, 2 * P:]
        ind = sb("ind", [P, TOP * TILES], i32)
        lnc = sb("lnc", [P, 2])
        w_in = sb("w_in", [P, 4 * P])
        g1T = sb("g1T", [HD, P]); g2 = sb("g2", [HD, P])
        wo = sb("wo", [P, P]); wos = sb("wos", [P, P]); lnbb = sb("lnbb", [P, P]); ones = sb("ones", [P, P])
        rhs2 = sb("rhs2", [P, 2 * P])
        brow = sb("brow", [P, P])
        gw = sb("gw", [P, 8]); gwh = sb("gwh", [P, 8], f16); gwl = sb("gwl", [P, 8], f16)
        x_sb = sb("x_sb", [P, TILES, P])
        x1 = sb("x1", [P, TILES, P])
        lg = sb("lg", [P, U, 8]); mx = sb("mx", [P, 2, 8]); ix = sb("ix", [P, 2, 8], u32)
        oh = sb("oh", [P, 2, TOP, EXPERTS]); chosen = sb("chosen", [P, 2, EXPERTS], f16)
        gap = sb("gap", [P, U]); tw = sb("tw", [P, U])
        base = sb("base", [P, EXPERTS]); pe_ = sb("pe_", [P, 2, EXPERTS]); pr = sb("pr", [P, 2, TOP, EXPERTS])
        place = sb("place", [P, U, TOP], u32)
        pay = sb("pay", [P, U, TOP, ROW])
        ends = sb("ends", [P, EXPERTS], i32)
        cnt = sb("cnt", [P, EXPERTS]); nti = sb("nti", [P, EXPERTS], i32); ntj = sb("ntj", [P, EXPERTS], i32)
        nt = [sb(f"nt{n}", [P, EXPERTS]) for n in range(4)]
        ge = sb("ge", [P, EXPERTS]); gn = sb("gn", [P, EXPERTS]); te = sb("te", [P, 8]); tab = sb("tab", [P, 2], i32)
        tabr = sb("tabr", [1, 2 * P], i32)
        wst = sb("wst", [P, EXPERTS, 2, INNER])
        wh = sb("wh", [P, EXPERTS, 2, IC * P], f16); wl = sb("wl", [P, EXPERTS, 2, IC * P], f16)
        wd = sb("wd", [P, EXPERTS, IC * P])
        sst_ = sb("sst_", [P, 2, SHARED]); sh = sb("sh", [P, 2, SC * P], f16); sl = sb("sl", [P, 2, SC * P], f16)
        sd = sb("sd", [P, SC, P])
        meta = sb("meta", [P, U, 2, 2])
        xs16 = sb("xs16", [P, 2, 2, SLOTS], f16)
        rows = nc.dram_tensor("rows", [(EXPERTS + 1) * REGION, ROW], f32).ap()
        ydram = nc.dram_tensor("ydram", [YROWS, P], f32).ap()
        xTr = sb("xTr", [P, U, P])
        qk = sb("qk", [P, U, 2 * P])
        rc = sb("rc", [P, U, 2 * P]); rs = sb("rs", [P, U, 2 * P])
        qk16 = sb("qk16", [P, U, 2 * 4 * P], f16)
        qkT = sb("qkT", [P, U, 8, P], f16)
        th = sb("th", [P, U, P])
        vexp = sb("vexp", [P, U, 4, P])
        vh = sb("vh", [P, U, P], f16); vl = sb("vl", [P, U, P], f16)
        em = sb("em", [P, 2, 4, 4 * P])
        dm = sb("dm", [P, 2, P]); zero = sb("zero", [P, P]); dmk = sb("dmk", [P, P]); sacc = sb("sacc", [P, 2, P]); shi = sb("shi", [P, U, P], f16)
        slo = sb("slo", [P, U, P], f16)
        og = sb("og", [P, 2, P])
        sqj = sb("sqj", [P, P]); ve = sb("ve", [P, 2])
        xp = sb("xp", [P, 2, P]); st6 = sb("st6", [P, 2, 6]); stat = sb("stat", [P, 2, 3]); rstd = sb("rstd", [P, 2, 2])
        x1hl = sb("x1hl", [P, 2, 2, P], f16)
        ybuf = sb("ybuf", [P, U, 2, P])
        x1Tr = sb("x1Tr", [P, 2, TOKENS], f16)

        y0 = x_sb[:, :, :]
        flat = lambda a: a[:, :, :, :].rearrange("p a b c -> p (a b c)")
        xin = flat(vexp)[:, 0:U * 2 * ROW].rearrange("p (a b n) -> p a b n", a=U, b=2)
        yb = flat(ybuf).rearrange("p (a b n) -> p a b n", a=U, b=2)
        sg = flat(em)[:, 0:2 * IC * SLOTS].rearrange("p (a c n) -> p a c n", a=2, c=IC)
        hT = flat(em)[:, 2 * IC * SLOTS:4 * IC * SLOTS].rearrange("p (a c n) -> p a c n", a=2, c=IC)
        hS = em[:, :, :, :].rearrange("p a h n -> p (a h n)")[:, 0:4 * 512].rearrange("p (a c n) -> p a c n", a=2, c=2)
        sS = em[:, :, :, :].rearrange("p a h n -> p (a h n)")[:, 2048:4096].rearrange("p (a c n) -> p a c n", a=2, c=2)
        whf, wlf = wh[:, :, :, :].rearrange("p e g n -> p (e g n)"), wl[:, :, :, :].rearrange("p e g n -> p (e g n)")
        wdf = wd[:, :, :].rearrange("p e n -> p (e n)")
        wh3, wl3 = wh[:, :, :, :].rearrange("p e g n -> p (e g) n"), wl[:, :, :, :].rearrange("p e g n -> p (e g) n")
        wst3 = wst[:, :, :, :].rearrange("p e g n -> p (e g) n")
        FFN_LOADS = 16 * 8
        y1 = bass.AP(wst, offset=0, ap=[[EXPERTS * 2 * INNER, P], [P, TILES], [1, P]])
        pay16 = lambda k: pay[:, k, :, 0:P].bitcast(f16)

        def vdiag(k):
            return bass.AP(vexp, offset=k * 4 * P, ap=[[U * 4 * P, P], [P + HD, 4], [32, 4], [1, HD]])

        b_in = ps("b_in", [P, 4 * P]); b_t = ps("b_t", [P, 8, P], f16)
        b_es = ps("b_es", [P, 4, 4 * P])
        b_e = [b_es[:, i, :] for i in range(4)]
        b_o = ps("b_o", [P, 4 * P]); b_p = ps("b_p", [P, 4 * P])
        slotsT = b_in[:, 0:SLOTS].bitcast(f16).rearrange("p (a n) -> p a n", a=2)
        y_ps = b_t[:, :, :].rearrange("p a c -> p (a c)").bitcast(f32)
        shared_y = [b_in[:, :], y_ps]
        up_banks = [(b_e[0], b_e[1], b_e[2]), (b_e[3], b_o, b_p)]
        delta, outT = b_o[:, 0:P], b_o[:, P:2 * P]
        p2 = b_p[:, 0:2 * P]
        x1T_ps = b_p[:, 2 * P:3 * P].bitcast(f16)
        lg_ps = b_p[:, 3 * P:3 * P + 8]
        rank_ps, total_ps = b_p[:, 3 * P + 8:3 * P + 16], b_p[:, 3 * P + 16:3 * P + 24]

        weights_loaded = sem("weights_loaded"); x_loaded = sem("x_loaded"); xT_loaded = [sem(f"xT_loaded{k}") for k in range(U)]
        setup_act = sem("setup_act"); setup_products = sem("setup_products"); setup_dve = sem("setup_dve"); setup_pool = sem("setup_pool")
        attended = sem("attended"); base_moved = sem("base_moved"); base_set = sem("base_set")
        choice_marked = sem("choice_marked"); cos_done = sem("cos_done"); delta_done = sem("delta_done")
        delta_kept = sem("delta_kept"); delta_masked = sem("delta_masked"); dummy_rows_stored = sem("dummy_rows_stored")
        expert_found = sem("expert_found")
        expert_y_done = sem("expert_y_done")
        ffn_loaded = sem("ffn_loaded"); fill_rows_stored = sem("fill_rows_stored")
        final_moments = sem("final_moments"); final_rstd = sem("final_rstd"); final_stats = sem("final_stats")
        final_var_eps = sem("final_var_eps"); first_added = sem("first_added"); gap_done = sem("gap_done")
        gap_tanh_done = sem("gap_tanh_done"); gate_tanh_done = sem("gate_tanh_done"); gated = sem("gated")
        hidden_done = sem("hidden_done")
        logits_copied = sem("logits_copied"); logits_done = sem("logits_done"); max_found = sem("max_found")
        meta_copied = sem("meta_copied"); normalised = sem("normalised"); one_hot_done = sem("one_hot_done")
        out_stored = sem("out_stored"); place_picked = sem("place_picked")
        projected = sem("projected"); bank_p_written = sem("bank_p_written"); qkT_copied = sem("qkT_copied")
        qk_hi_done = sem("qk_hi_done"); qk_lo_done = sem("qk_lo_done"); qk_silu_done = sem("qk_silu_done")
        qk_turned = sem("qk_turned"); rank_based = sem("rank_based")
        roped = sem("roped"); second_added = sem("second_added"); shared_added = sem("shared_added")
        shared_gate_done = sem("shared_gate_done"); shared_hidden_done = sem("shared_hidden_done"); shared_silu_done = sem("shared_silu_done")
        shared_up_done = sem("shared_up_done"); shared_y_done = sem("shared_y_done"); sin_done = sem("sin_done")
        slots_copied = sem("slots_copied"); slots_turned = sem("slots_turned"); squares_summed = sem("squares_summed")
        state_added = sem("state_added"); state_hi_done = sem("state_hi_done"); state_lo_done = sem("state_lo_done")
        table_loaded = sem("table_loaded"); table_made = sem("table_made"); table_step = sem("table_step")
        v_hi_done = sem("v_hi_done"); v_lo_done = sem("v_lo_done"); v_spread = sem("v_spread")
        weights_hi_done = sem("weights_hi_done"); weights_lo_done = sem("weights_lo_done"); weights_padded = sem("weights_padded")
        x1T_copied = sem("x1T_copied"); x1_done = sem("x1_done"); x1_hi_done = sem("x1_hi_done")
        x1_lo_done = sem("x1_lo_done"); x1_moments = sem("x1_moments")
        x1_stats = sem("x1_stats")
        x_biased = sem("x_biased"); x_summed = sem("x_summed")
        indices_loaded = sem("indices_loaded"); var_eps_done = sem("var_eps_done"); powers_done = sem("powers_done")
        zeroed = sem("zeroed"); odd_added = sem("odd_added"); final_recip = sem("final_recip"); x1_packed = sem("x1_packed")
        expert_up_done = [sem(f"expert_up_done{c}") for c in range(IC)]; expert_silu_done = [sem(f"expert_silu_done{c}") for c in range(IC)]
        energies_done = [sem(f"energies_done{h}") for h in range(2)]; masked = [sem(f"masked{h}") for h in range(2)]
        rows_scattered = [sem(f"rows_scattered{k}") for k in range(U)]
        slots_loaded = [sem(f"slots_loaded{k}") for k in range(U)]
        placed = [sem(f"placed{k}") for k in range(U)]; weighed = [sem(f"weighed{k}") for k in range(U)]
        yscaled = [sem(f"yscaled{k}") for k in range(U)]
        y_scattered = [sem(f"y_scattered{k}") for k in range(U)]
        fst = sb("fst", [P, TILES, 6]); fmv = sb("fmv", [P, TILES, 2]); frs = sb("frs", [P, TILES]); fve = sb("fve", [P, TILES]); fnb = sb("fnb", [P, TILES])
        results_loaded = [sem(f"results_loaded{k}") for k in range(FINALS)]
        block = ctx.enter_context(nc.Block())

        def steps(eng, body, n, after, peel, tail):
            for i in range(peel):
                for j in range(U):
                    body(i, j)
            with eng.Fori(peel, n // U - tail) as i:
                for j in range(U):
                    body(i, j)
            for step in range(n - tail * U, n + after):
                body(step // U, step % U)

        def beside(i, j):
            return U * i + j - TILES - 1 if isinstance(i, int) and U * i + j > TILES else None

        def exists(t, n=TILES):
            return not isinstance(t, int) or 0 <= t < n

        def stage(i, j, lag, n=TILES):
            k = j + lag
            return exists(U * i + k, n), U * i + k, k % U, i + k // U

        @block.sync
        def _(sp):
            sp.dma_start(cst[:, :], consts).then_inc(weights_loaded, 16)
            sp.dma_start(w_in[:, 0:3 * P], Wqkv).then_inc(weights_loaded, 16)
            sp.dma_start(wo[:, :], Wo).then_inc(weights_loaded, 16)
            sp.dma_start(lnc[:, :], ln).then_inc(weights_loaded, 16)
            for k in range(U):
                sp.dma_start(xTr[:, k, :], xT[:, k * P:(k + 1) * P]).then_inc(xT_loaded[k], 16)
            sp.dma_start(ind[:, :], indices).then_inc(indices_loaded, 16)
            for b in range(4):
                sp.dma_start(x_sb[:, 8 * b:8 * b + 8, :], x[SEQ * b:SEQ * (b + 1), :].rearrange("(t p) c -> p t c", p=P)).then_inc(x_loaded, 16)
            sp.dma_start(rows[EXPERTS * REGION:EXPERTS * REGION + DUMMY * SLOTS, :], pads[EXPERTS * SLOTS:, :]).then_inc(dummy_rows_stored, 16)
            wdv = wd[:, :, :].rearrange("p e (c h) -> p e c h", c=IC)

            def load_xT(i):
                for j in range(U):
                    sp.wait_ge(projected, U * i + j + 1)
                    sp.dma_start(xTr[:, j, :], xT[:, bass.ds((U * i + j + U) * P, P)]).then_inc(xT_loaded[j], 16)

            load_xT(0)
            sp.dma_start(sst_[:, :, :], Sgu).then_inc(ffn_loaded, 16)
            sp.dma_start(wst[:, :, 0, :], Wg.rearrange("e h i -> h e i")).then_inc(ffn_loaded, 16)
            load_xT(1)
            sp.dma_start(wst[:, :, 1, :], Wu.rearrange("e h i -> h e i")).then_inc(ffn_loaded, 16)
            sp.dma_start(sd[:, 0, :], Sd[0:P, :]).then_inc(ffn_loaded, 16)
            sp.dma_start(sd[0:SHARED - P, 1, :], Sd[P:SHARED, :]).then_inc(ffn_loaded, 16)
            load_xT(2)
            for c in range(IC):
                n = min(P, INNER - c * P)
                sp.dma_start(wdv[0:n, :, c, :], Wd[:, c * P:c * P + n, :].rearrange("e i h -> i e h")).then_inc(ffn_loaded, 16)
            with sp.Fori(3, TILES // U - 1) as i:
                load_xT(i)
            sp.wait_ge(table_made, 1)
            for e in range(EXPERTS // 2):
                end = sp.value_load(ends[0:1, e:e + 1], min_val=0, max_val=EXPERTS * REGION)
                sp.dma_start(rows[bass.ds(end, SLOTS), :], pads[e * SLOTS:(e + 1) * SLOTS, :]).then_inc(fill_rows_stored, 16)
            sp.wait_ge(table_made, 2)
            sp.dma_start(tabr[0:1, :], tab[:, :]).then_inc(table_loaded, 16)
            sp.wait_ge(table_loaded, 16)
            for k in range(U):
                sp.wait_ge(rows_scattered[k], 2 * 16 * (TILES // U))
            sp.wait_ge(fill_rows_stored, 16 * EXPERTS)
            sp.wait_ge(dummy_rows_stored, 16)

            def load(i, j):
                t = U * i + j
                at = sp.value_load(tabr[0:1, bass.ds(2 * t, 1)], min_val=0, max_val=EXPERTS * REGION + (DUMMY - 1) * SLOTS)
                at = sp.snap(at)
                if exists(t - U, SLOT_TILES):
                    sp.wait_ge(slots_turned, t - U + 1)
                    sp.wait_ge(meta_copied, t - U + 1)
                    sp.wait_ge(table_loaded, 16)
                sp.dma_start(xin[:, j, :, :], rows[bass.ds(at, SLOTS), :].rearrange("(b p) w -> p b w", p=P)).then_inc(slots_loaded[j], 16)
            steps(sp, load, SLOT_TILES, 0, 2, 1)

            for k in range(U):
                sp.wait_ge(y_scattered[k], 32 * (SLOT_TILES // U))
            for q in range(FINALS):
                for c, dst in enumerate((y0, y1)):
                    sp.dma_start(dst[:, FT * q:FT * q + FT, :], ydram[c * TOKENS + q * FT * P:c * TOKENS + (q + 1) * FT * P, :]
                                 .rearrange("(t p) c -> p t c", p=P)).then_inc(results_loaded[q], 16)
            for q in range(FINALS):
                sp.wait_ge(normalised, FT * (q + 1))
                sp.dma_start(out[q * FT * P:(q + 1) * FT * P, :].rearrange("(t p) c -> p t c", p=P), x1[:, FT * q:FT * q + FT, :]).then_inc(out_stored, 16)
            sp.wait_ge(out_stored, 16 * FINALS)

        @block.tensor
        def _(pe):
            pe.wait_ge(weights_loaded, 128)
            pe.wait_ge(setup_dve, 3)
            nc.tensor.matmul(b_p[:, 0:P], C("center"), wos[:, :], start=True, stop=True)
            nc.tensor.matmul(b_p[:, P:2 * P], g1T[:, :], g2[:, :], start=True, stop=True)
            nc.tensor.matmul(b_p[:, 2 * P:3 * P], lnbb[:, :], wo[:, :], start=True, stop=True).then_inc(setup_products, 1)

            def proj(i, j, lag):
                ok, t, k, r = stage(i, j, lag)
                if not ok:
                    return
                pe.wait_ge(xT_loaded[k], 16 * (r + 1))
                if exists(t - 1):
                    pe.wait_ge(v_hi_done, t)
                nc.tensor.matmul(b_in[:, 0:3 * P], xTr[:, k, :], w_in[:, 0:3 * P], start=True, stop=True)
                nc.tensor.matmul(b_in[:, 3 * P:], w_in[:, 3 * P:], xTr[:, k, :], start=True, stop=True).then_inc(projected, 1)

            def qk_turn(i, j, lag):
                ok, t, k, r = stage(i, j, lag)
                if not ok:
                    return
                pe.wait_ge(qk_lo_done, t + 1); pe.wait_ge(qk_hi_done, t + 1)
                if exists(t - 1):
                    pe.wait_ge(qkT_copied, t)
                for b in range(2 * BLOCKS):
                    mm = nc.tensor.transpose(b_t[:, b, :], qk16[:, k, b * P:(b + 1) * P], idh)
                mm.then_inc(qk_turned, 1)

            def energies(i, j, lag):
                ok, t, k, r = stage(i, j, lag)
                if not ok:
                    return
                pe.wait_ge(qkT_copied, t + 1)
                for pair in ((0, 1), (2, 3)):
                    if exists(t - 1):
                        pe.wait_ge(masked[pair[0] // 2], t)
                    for b in range(BLOCKS):
                        for h4 in pair:
                            rows = slice(32 * h4, 32 * h4 + 32)
                            mm = nc.tensor.matmul(b_es[:, h4, b * P:(b + 1) * P], qkT[rows, k, 4 + b, :],
                                                  qkT[rows, k, b, :], start=True, stop=True)
                    mm.then_inc(energies_done[pair[0] // 2], 1)

            def state(i, j, lag):
                ok, t, k, r = stage(i, j, lag)
                if not ok:
                    return
                pe.wait_ge(v_lo_done, t + 1)
                if exists(t - 2):
                    pe.wait_ge(gated, t - 1)
                for b in range(BLOCKS):
                    kk = qk16[:, k, (4 + b) * P:(5 + b) * P]
                    o = delta[:, 32 * b:32 * b + 32]
                    vcol = slice(32 * b, 32 * b + 32)
                    nc.tensor.matmul(o, kk, vh[:, k, vcol], start=True, stop=False)
                    mm = nc.tensor.matmul(o, kk, vl[:, k, vcol], start=False, stop=True)
                mm.then_inc(delta_done, 1)

            def attend(i, j, lag):
                ok, t, k, r = stage(i, j, lag)
                if not ok:
                    return
                pe.wait_ge(delta_masked, t + 2 if exists(t + 1) else TILES)
                for h4 in range(4):
                    if h4 % 2 == 0:
                        pe.wait_ge(masked[h4 // 2], t + 1)
                    for b in range(BLOCKS):
                        cols = slice(32 * b, 32 * b + 32)
                        nc.tensor.matmul(outT[cols, :], vexp[:, k, h4, cols], em[:, k % 2, h4, b * P:(b + 1) * P],
                                         start=(h4 == 0), stop=False, tile_position=(0, 32 * b))
                pe.wait_ge(state_lo_done, t + 1)
                for b in range(BLOCKS):
                    cols = slice(32 * b, 32 * b + 32)
                    nc.tensor.matmul(outT[cols, :], shi[:, k, cols], qkT[:, k, b, :], start=False, stop=False, tile_position=(0, 32 * b))
                    mm = nc.tensor.matmul(outT[cols, :], slo[:, k, cols], qkT[:, k, b, :], start=False, stop=True, tile_position=(0, 32 * b))
                mm.then_inc(attended, 1)

            def router(i, j, lag):
                ok, t, k, r = stage(i, j, lag)
                if not ok:
                    return
                pe.wait_ge(x1T_copied, t + 1)
                xh, xl = x1Tr[:, 0, bass.ds(t * P, P)], x1Tr[:, 1, bass.ds(t * P, P)]
                nc.tensor.matmul(lg_ps, xh, gwh[:, :], start=True, stop=False)
                nc.tensor.matmul(lg_ps, xl, gwh[:, :], start=False, stop=False)
                nc.tensor.matmul(lg_ps, xh, gwl[:, :], start=False, stop=True).then_inc(logits_done, 1)

            def rank(i, j, lag):
                ok, t, k, r = stage(i, j, lag)
                if not ok:
                    return
                pe.wait_ge(choice_marked, t + 1)
                nc.tensor.matmul(rank_ps, before, chosen[:, k % 2, :], start=True, stop=True)
                return nc.tensor.matmul(total_ps, onesh, chosen[:, k % 2, :], start=True, stop=True)

            def proj2(i, j, lag):
                ok, t, k, r = stage(i, j, lag)
                if not ok:
                    return
                pe.wait_ge(gated, t + 1)
                return nc.tensor.matmul(p2, og[:, k % 2, :], rhs2[:, :], start=True, stop=True)

            def bank_p(i, j):
                step = U * i + j
                if not (exists(step - 2) or exists(step - 7)):
                    return
                if exists(step - 3):
                    pe.wait_ge(x_summed, step - 2)
                if exists(step - 6):
                    pe.wait_ge(x1T_copied, step - 5)
                if exists(step - 7):
                    pe.wait_ge(logits_copied, step - 6)
                if exists(step - 8):
                    pe.wait_ge(base_moved, step - 7)
                router(i, j, -6)
                last = rank(i, j, -7)
                last = x1_turn(i, j, -5) or last
                last = proj2(i, j, -2) or last
                last.then_inc(bank_p_written, 1)

            def x1_turn(i, j, lag):
                ok, t, k, r = stage(i, j, lag)
                if not ok:
                    return
                pe.wait_ge(x1_lo_done, t + 1)
                nc.tensor.transpose(x1T_ps[:, 0:P], x1hl[:, k % 2, 0, :], idh)
                return nc.tensor.transpose(x1T_ps[:, P:2 * P], x1hl[:, k % 2, 1, :], idh)

            pe.wait_ge(setup_act, 4)
            proj(0, 0, 0); proj(0, 0, 1)
            qk_turn(0, 0, 0)
            proj(0, 0, 2)

            def shared_up(q):
                for c in range(SC):
                    if q:
                        pe.wait_ge(shared_hidden_done, 2 * q - 1 + c)
                    for gu in range(2):
                        bank = b_e[2 * gu + c][:, :]
                        w, wlo = sh[:, gu, c * P:(c + 1) * P], sl[:, gu, c * P:(c + 1) * P]
                        xh, xl = x1Tr[:, 0, q * 512:(q + 1) * 512], x1Tr[:, 1, q * 512:(q + 1) * 512]
                        nc.tensor.matmul(bank, w, xh, start=True, stop=False)
                        nc.tensor.matmul(bank, w, xl, start=False, stop=False)
                        nc.tensor.matmul(bank, wlo, xh, start=False, stop=True).then_inc(shared_up_done if gu else shared_gate_done, 1)

            def shared_down(q):
                k = q % 2
                pe.wait_ge(shared_hidden_done, 2 * q + 2)
                if q >= 2:
                    pe.wait_ge(shared_added, q - 1)
                for n in range(4):
                    o = shared_y[k][:, n * P:(n + 1) * P]
                    nc.tensor.matmul(o, hS[:, k, 0, n * P:(n + 1) * P], sd[:, 0, :], start=True, stop=False)
                    mm = nc.tensor.matmul(o, hS[0:SHARED - P, k, 1, n * P:(n + 1) * P], sd[0:SHARED - P, 1, :], start=False, stop=True)
                mm.then_inc(shared_y_done, 1)

            def shared(q):
                if q == 0:
                    pe.wait_ge(weights_hi_done, 1); pe.wait_ge(weights_lo_done, 1)
                    pe.wait_ge(weights_padded, 4); pe.wait_ge(ffn_loaded, FFN_LOADS)
                    for pair in range(2):
                        pe.wait_ge(masked[pair], TILES)
                    pe.wait_ge(v_hi_done, TILES); pe.wait_ge(qkT_copied, TILES)
                if q < GROUPS:
                    pe.wait_ge(x1T_copied, 4 * q + 4)
                    shared_up(q)
                if q:
                    shared_down(q - 1)

            def body(i, j):
                energies(i, j, 0)
                state(i, j, 0)
                bank_p(i, j)
                proj(i, j, 3)
                qk_turn(i, j, 1)
                attend(i, j, -1)
                if beside(i, j) is not None:
                    shared(beside(i, j))
            steps(pe, body, TILES, AFTER, PEEL, TAIL)
            for q in range(AFTER - 1, GROUPS + 1):
                shared(q)

            pe.wait_ge(table_loaded, 16)
            pe.wait_ge(shared_hidden_done, 2 * GROUPS); pe.wait_ge(shared_added, GROUPS)
            pe.wait_ge(weights_hi_done, 1 + EXPERTS); pe.wait_ge(weights_lo_done, 1 + EXPERTS)
            pe.wait_ge(base_moved, TILES)

            def turn(i, j, lag):
                ok, t, k, r = stage(i, j, lag, SLOT_TILES)
                if not ok:
                    return
                pe.wait_ge(slots_loaded[k], 16 * (r + 1))
                for b in range(2):
                    for a in range(2):
                        mm = nc.tensor.transpose(slotsT[:, a, b * P:(b + 1) * P], xin[:, k, b, 64 * a:64 * a + 64].bitcast(f16), idh)
                mm.then_inc(slots_turned, 1)

            def expert_of(t):
                return pe.value_load(tabr[0:1, bass.ds(2 * t + 1, 1)], min_val=0, max_val=EXPERTS - 1)

            def up(i, j, e):
                t = U * i + j
                pe.wait_ge(slots_copied, t + 1)
                for c in range(IC):
                    for gu in range(2):
                        o = up_banks[j % 2][c][:, gu * SLOTS:(gu + 1) * SLOTS]
                        at = e * (2 * IC * P) + (gu * IC + c) * P
                        w, wlo = whf[:, bass.ds(at, P)], wlf[:, bass.ds(at, P)]
                        nc.tensor.matmul(o, w, xs16[:, j % 2, 0, :], start=True, stop=False)
                        nc.tensor.matmul(o, w, xs16[:, j % 2, 1, :], start=False, stop=False)
                        mm = nc.tensor.matmul(o, wlo, xs16[:, j % 2, 0, :], start=False, stop=True)
                    mm.then_inc(expert_up_done[c], 1)

            def down(i, j, lag, e):
                ok, t, k, r = stage(i, j, lag, SLOT_TILES)
                if not ok:
                    return
                pe.wait_ge(hidden_done, t + 1)
                if exists(t - 1, SLOT_TILES):
                    pe.wait_ge(yscaled[(j + lag - 1) % U], i + (j + lag - 1) // U + 1)
                for b in range(2):
                    for c in range(IC):
                        n = min(P, INNER - c * P)
                        mm = nc.tensor.matmul(y_ps[:, b * P:(b + 1) * P], hT[0:n, k % 2, c, b * P:(b + 1) * P],
                                              wdf[0:n, bass.ds(e * (IC * P) + c * P, P)], start=(c == 0), stop=(c == IC - 1))
                mm.then_inc(expert_y_done, 1)

            turn(0, 0, 0)
            owner = [None] * U

            def experts(i, j):
                t = U * i + j
                before = owner[j - 1] if j else (expert_of(t - 1) if exists(t - 1, SLOT_TILES) else None)
                if exists(t, SLOT_TILES):
                    owner[j] = expert_of(t)
                    up(i, j, owner[j])
                turn(i, j, 1)
                down(i, j, -1, before)
            steps(pe, experts, SLOT_TILES, 1, 2, 1)

        @block.scalar
        def _(act):
            act.dma_start(g1T[:, :], Wg1T).then_inc(weights_loaded, 16)
            act.dma_start(g2[:, :], Wg2).then_inc(weights_loaded, 16)
            act.dma_start(half[:, :], halves).then_inc(weights_loaded, 16)
            act.dma_start(gw[:, :], gate_w).then_inc(weights_loaded, 16)
            act.wait_ge(zeroed, 1)
            nc.scalar.activation(sqj[:, 0:1], zero[:, 0:1], ACT.Silu)
            act.wait_ge(weights_loaded, 128)
            act.wait_ge(setup_products, 1)
            nc.scalar.activation(rhs2[:, P:], b_p[:, 0:P], ACT.Copy, scale=math.sqrt(CH)).then_inc(setup_act, 1)
            nc.scalar.activation(w_in[:, 3 * P:], b_p[:, P:2 * P], ACT.Copy).then_inc(setup_act, 1)
            nc.scalar.activation(brow[:, :], b_p[:, 2 * P:3 * P], ACT.Copy).then_inc(setup_act, 1)
            nc.scalar.activation(rhs2[:, 0:P], C("center"), ACT.Copy).then_inc(setup_act, 1)
            act.wait_ge(setup_pool, 6)

            def silu_qk(i, j, lag):
                ok, t, k, r = stage(i, j, lag)
                if not ok:
                    return
                act.wait_ge(projected, t + 1)
                if exists(t - U):
                    act.wait_ge(cos_done, t - U + 1); act.wait_ge(sin_done, t - U + 1)
                nc.scalar.activation(qk[:, k, :], b_in[:, 0:2 * P], ACT.Silu).then_inc(qk_silu_done, 1)

            def gate_v(i, j, lag):
                ok, t, k, r = stage(i, j, lag)
                if not ok:
                    return
                if exists(t - U):
                    act.wait_ge(gated, t - U + 1)
                nc.scalar.activation(th[:, k, :], b_in[:, 3 * P:], ACT.Tanh, scale=0.5).then_inc(gate_tanh_done, 1)
                if exists(t - U):
                    act.wait_ge(attended, t - U + 1)
                nc.scalar.activation(vdiag(k), b_in[:, 2 * P:3 * P].rearrange("p (b h d) -> p h b d", b=4, h=4),
                                     ACT.Copy).then_inc(v_spread, 1)
                if exists(t - U):
                    act.wait_ge(delta_done, t - U + 1)
                nc.scalar.activation(vh[:, k, :], b_in[:, 2 * P:3 * P], ACT.Copy).then_inc(v_hi_done, 1)

            def hi16(i, j, lag):
                ok, t, k, r = stage(i, j, lag)
                if not ok:
                    return
                act.wait_ge(roped, t + 1)
                if exists(t - U):
                    act.wait_ge(qk_turned, t - U + 1); act.wait_ge(delta_done, t - U + 1)
                out = bass.AP(qk16, offset=k * 8 * P, ap=[[U * 8 * P, P], [4 * P + HD, 2], [32, HEADS], [HD, 2], [1, HD]])
                src = bass.AP(rc, offset=k * 2 * P, ap=[[U * 2 * P, P], [P, 2], [HD, HEADS], [0, 2], [1, HD]])
                nc.scalar.activation(out, src, ACT.Copy).then_inc(qk_hi_done, 1)

            def qkT_copy(i, j, lag):
                ok, t, k, r = stage(i, j, lag)
                if not ok:
                    return
                act.wait_ge(qk_turned, t + 1)
                if exists(t - U):
                    act.wait_ge(attended, t - U + 1)
                nc.scalar.activation(qkT[:, k, :, :], b_t[:, :, :], ACT.Copy).then_inc(qkT_copied, 1)

            def x1T_copy(i, j, lag):
                ok, t, k, r = stage(i, j, lag)
                if not ok:
                    return
                act.wait_ge(bank_p_written, t + 4)
                nc.scalar.activation(x1Tr[:, :, bass.ds(t * P, P)], x1T_ps.rearrange("p (a c) -> p a c", a=2), ACT.Copy).then_inc(x1T_copied, 1)

            def squares(i, j, lag):
                ok, t, k, r = stage(i, j, lag)
                if not ok:
                    return
                act.wait_ge(bank_p_written, t + 1)
                if exists(t - 1):
                    act.wait_ge(squares_summed, t)
                nc.scalar.activation(sqj[:, :], p2[:, 0:P], ACT.Square, accum_out=stat[:, k % 2, 0:1]).then_inc(squares_summed, 1)

            def logit_out(i, j, lag):
                ok, t, k, r = stage(i, j, lag)
                if not ok:
                    return
                act.wait_ge(logits_done, t + 1)
                if exists(t - 2):
                    act.wait_ge(expert_found, t - 1)
                nc.scalar.activation(lg[:, k, :], lg_ps, ACT.Copy).then_inc(logits_copied, 1)

            def payload(i, j, lag):
                ok, t, k, r = stage(i, j, lag)
                if not ok:
                    return
                act.wait_ge(x1_lo_done, t + 1); act.wait_ge(x1_hi_done, t + 1)
                if exists(t - U):
                    act.wait_ge(rows_scattered[k], 32 * r)
                both = x1hl[:, k % 2, :, :].rearrange("p a c -> p (a c)").unsqueeze(1).broadcast_to([P, TOP, 2 * P])
                nc.scalar.activation(pay16(k), both, ACT.Copy).then_inc(x1_packed, 1)

            def weights(i, j, lag):
                ok, t, k, r = stage(i, j, lag)
                if not ok:
                    return
                act.wait_ge(gap_done, t + 1)
                nc.scalar.activation(tw[:, k:k + 1], gap[:, k:k + 1], ACT.Tanh, scale=0.5).then_inc(gap_tanh_done, 1)
                act.wait_ge(gap_tanh_done, t + 1)
                if exists(t - U):
                    act.wait_ge(rows_scattered[k], 32 * r)
                nc.scalar.activation(pay[:, k, 0, WEIGHT:WEIGHT + 1], tw[:, k:k + 1], ACT.Copy, scale=0.5, bias=0.5)
                nc.scalar.activation(pay[:, k, 1, WEIGHT:WEIGHT + 1], tw[:, k:k + 1], ACT.Copy, scale=-0.5, bias=0.5).then_inc(weighed[k], 1)

            def split_shared():
                act.wait_ge(ffn_loaded, FFN_LOADS)
                nc.scalar.activation(sh[:, :, 0:SHARED], sst_[:, :, :], ACT.Copy).then_inc(weights_hi_done, 1)

            def split(e):
                nc.scalar.activation(wh[:, e, :, 0:INNER], wst[:, e, :, :], ACT.Copy).then_inc(weights_hi_done, 1)

            def x1hi(i, j, lag):
                ok, t, k, r = stage(i, j, lag)
                if not ok:
                    return
                act.wait_ge(x1_done, t + 1)
                if exists(t - 2):
                    act.wait_ge(bank_p_written, t + 2); act.wait_ge(x1_packed, t - 1)
                nc.scalar.activation(x1hl[:, k % 2, 0, :], x1[:, t, :], ACT.Copy).then_inc(x1_hi_done, 1)

            silu_qk(0, 0, 0); gate_v(0, 0, 0)
            hi16(0, 0, 0)
            silu_qk(0, 0, 1); gate_v(0, 0, 1)
            qkT_copy(0, 0, 0)
            hi16(0, 0, 1)
            silu_qk(0, 0, 2); gate_v(0, 0, 2)

            def shared(q):
                for c in range(SC):
                    act.wait_ge(shared_gate_done, 2 * q + c + 1)
                    if q >= 2:
                        act.wait_ge(shared_hidden_done, 2 * (q - 2) + c + 1)
                    elif q == 0 and c == 0:
                        act.wait_ge(attended, TILES)
                    nc.scalar.activation(sS[:, q % 2, c, :], b_e[c][:, :], ACT.Silu).then_inc(shared_silu_done, 1)

            def body(i, j):
                step = U * i + j
                hi16(i, j, 2)
                if exists(step - 2) or exists(step - 6):
                    act.wait_ge(bank_p_written, step - 1)
                logit_out(i, j, -6)
                x1T_copy(i, j, -5)
                squares(i, j, -2)
                silu_qk(i, j, 3)
                qkT_copy(i, j, 1)
                payload(i, j, -5)
                if isinstance(i, int) and step == TILES - 4:
                    split_shared()
                if isinstance(i, int) and step >= TILES:
                    split(step - TILES)
                x1hi(i, j, -3)
                weights(i, j, -6)
                gate_v(i, j, 3)
                if beside(i, j) is not None:
                    shared(beside(i, j))
            steps(act, body, TILES, AFTER, PEEL, TAIL)
            act.wait_ge(table_made, 1)
            for e in range(EXPERTS // 2, EXPERTS):
                end = act.value_load(ends[0:1, e:e + 1], min_val=0, max_val=EXPERTS * REGION)
                act.dma_start(rows[bass.ds(end, SLOTS), :], pads[e * SLOTS:(e + 1) * SLOTS, :]).then_inc(fill_rows_stored, 16)
            for q in range(AFTER - 1, GROUPS):
                shared(q)

            def silu(i, j):
                ok, t, k, r = stage(i, j, 0, SLOT_TILES)
                if not ok:
                    return
                if exists(t - 2, SLOT_TILES):
                    act.wait_ge(hidden_done, t - 1)
                for c in range(IC):
                    act.wait_ge(expert_up_done[c], t + 1)
                    nc.scalar.activation(sg[:, j % 2, c, :], up_banks[j % 2][c][:, 0:SLOTS], ACT.Silu).then_inc(expert_silu_done[c], 1)

            def scale(i, j, lag):
                ok, t, k, r = stage(i, j, lag, SLOT_TILES)
                if not ok:
                    return
                act.wait_ge(expert_y_done, t + 1); act.wait_ge(meta_copied, t + 1)
                if exists(t - U, SLOT_TILES):
                    act.wait_ge(y_scattered[k], 32 * r)
                for b in range(2):
                    ins = nc.scalar.activation(yb[:, k, b, :], y_ps[:, b * P:(b + 1) * P], ACT.Copy, scale=meta[:, k, b, 1:2])
                ins.then_inc(yscaled[k], 1)

            def experts(i, j):
                silu(i, j)
                scale(i, j, -1)
            steps(act, experts, SLOT_TILES, 1, 2, 1)

            for q in range(FINALS):
                cols = slice(FT * q, FT * q + FT)
                act.wait_ge(final_rstd, q + 1)
                for t in range(FT * q, FT * q + FT):
                    nc.scalar.activation(x1[:, t, :], x1[:, t, :], ACT.Identity, scale=frs[:, t:t + 1], bias=fnb[:, t:t + 1]).then_inc(normalised, 1)

        @block.vector
        def _(dve):
            dve.wait_ge(weights_loaded, 128)
            nc.vector.memset(ones[:, :], 1.0).then_inc(setup_dve, 1)
            nc.vector.tensor_copy(base[:, :], C("first")).then_inc(base_set, 1)
            nc.vector.memset(wh3[:, :, INNER:], 0.0).then_inc(weights_padded, 1)
            nc.vector.memset(wl3[:, :, INNER:], 0.0).then_inc(weights_padded, 1)
            nc.vector.memset(sh[:, :, SHARED:], 0.0).then_inc(weights_padded, 1)
            nc.vector.memset(sl[:, :, SHARED:], 0.0).then_inc(weights_padded, 1)
            nc.vector.tensor_scalar(wos[:, :], wo[:, :], lnc[:, 0:1], None, ALU.mult).then_inc(setup_dve, 1)
            dve.wait_ge(setup_dve, 1)
            nc.vector.tensor_scalar(lnbb[:, :], ones[:, :], lnc[:, 1:2], None, ALU.mult).then_inc(setup_dve, 1)
            nc.vector.tensor_copy(gwh[:, :], gw[:, :]).then_inc(setup_dve, 1)
            dve.wait_ge(setup_dve, 4)
            nc.vector.tensor_tensor(gwl[:, :], gw[:, :], gwh[:, :], ALU.subtract).then_inc(setup_dve, 1)

            def rope_cos(i, j, lag):
                ok, t, k, r = stage(i, j, lag)
                if not ok:
                    return
                dve.wait_ge(qk_silu_done, t + 1)
                if exists(t - U):
                    dve.wait_ge(qk_lo_done, t - U + 1); dve.wait_ge(qk_hi_done, t - U + 1)
                cos = cst[:, bass.ds(CONST_AT["cos"][0] + t * HD, HD)].unsqueeze(1).broadcast_to([P, 2 * HEADS, HD])
                nc.vector.tensor_tensor(rc[:, k, :].rearrange("p (h d) -> p h d", d=HD),
                                        qk[:, k, :].rearrange("p (h d) -> p h d", d=HD), cos, ALU.mult).then_inc(cos_done, 1)

            def rope_add(i, j, lag):
                ok, t, k, r = stage(i, j, lag)
                if not ok:
                    return
                dve.wait_ge(cos_done, t + 1); dve.wait_ge(sin_done, t + 1)
                nc.vector.tensor_tensor(rc[:, k, :], rc[:, k, :], rs[:, k, :], ALU.add).then_inc(roped, 1)

            def rope_lo(i, j, lag):
                ok, t, k, r = stage(i, j, lag)
                if not ok:
                    return
                dve.wait_ge(qk_hi_done, t + 1)
                v = lambda o, w: bass.AP(qk16, offset=k * 8 * P + o, ap=[[U * 8 * P, P], [w, 2], [32, HEADS], [1, HD]])
                nc.vector.tensor_tensor(v(2 * HD, 4 * P - 2 * HD), rc[:, k, :].rearrange("p (a h d) -> p a h d", a=2, d=HD),
                                        v(0, 4 * P + HD), ALU.subtract).then_inc(qk_lo_done, 1)

            def mask(i, j, lag, pair):
                ok, t, k, r = stage(i, j, lag)
                if not ok:
                    return
                dve.wait_ge(energies_done[pair], t + 1)
                if exists(t - 2):
                    dve.wait_ge(attended, t - 1)
                heads = slice(2 * pair, 2 * pair + 2)
                tri = C("tri").unsqueeze(1).broadcast_to([P, 2 * BLOCKS, P])
                nc.vector.tensor_tensor(em[:, k % 2, heads, :].rearrange("p h (b n) -> p (h b) n", b=BLOCKS),
                                        b_es[:, heads, :].rearrange("p h (b n) -> p (h b) n", b=BLOCKS), tri, ALU.mult).then_inc(masked[pair], 1)

            def dmask(i, j, lag):
                ok, t, k, r = stage(i, j, lag)
                if not ok:
                    return
                dve.wait_ge(delta_done, t + 1)
                if exists(t - 2):
                    dve.wait_ge(state_hi_done, t - 1)
                if j < U - 1:
                    nc.vector.tensor_tensor(dm[:, j % 2, :], delta, C("own"), ALU.mult).then_inc(delta_masked, 1)
                    return
                keep = cst[:, bass.ds(CONST_AT["keep"][0] + t, 1)]
                nc.vector.scalar_tensor_tensor(out=dmk[:, :], in0=delta, scalar=keep, in1=C("own"),
                                               op0=ALU.mult, op1=ALU.mult).then_inc(delta_kept, 1)
                dve.wait_ge(delta_kept, i + 1); dve.wait_ge(state_added, t)
                nc.vector.scalar_tensor_tensor(out=dm[:, j % 2, :], in0=sacc[:, j % 2, :], scalar=keep, in1=dmk[:, :],
                                               op0=ALU.mult, op1=ALU.add).then_inc(delta_masked, 1)

            def gate(i, j, lag):
                ok, t, k, r = stage(i, j, lag)
                if not ok:
                    return
                dve.wait_ge(attended, t + 1); dve.wait_ge(gate_tanh_done, t + 1)
                if exists(t - 2):
                    dve.wait_ge(bank_p_written, t - 1)
                nc.vector.scalar_tensor_tensor(out=og[:, k % 2, :], in0=th[:, k, :], scalar=1.0, in1=outT,
                                               op0=ALU.add, op1=ALU.mult).then_inc(gated, 1)

            def tail(i, j, lag, part):
                ok, t, k, r = stage(i, j, lag)
                if not ok:
                    return
                k2 = k % 2
                if part == 1:
                    dve.wait_ge(powers_done, t + 1)
                    nc.vector.scalar_tensor_tensor(out=xp[:, k2, :], in0=p2[:, P:2 * P], scalar=rstd[:, k2, 0:1], in1=x_sb[:, t, :],
                                                   op0=ALU.mult, op1=ALU.add).then_inc(x_summed, 1)
                if part == 2:
                    dve.wait_ge(x_summed, t + 1)
                    nc.vector.bn_stats(st6[:, k2, :], xp[:, k2, :]).then_inc(x1_stats, 1)
                if part == 3:
                    nc.vector.bn_aggr(stat[:, 1 - k2, 1:3], st6[:, k2, :]).then_inc(x1_moments, 1)
                if part == 5:
                    dve.wait_ge(powers_done, t + 2)
                    nc.vector.tensor_scalar(x1[:, t, :], xp[:, k2, :], stat[:, 1 - k2, 1:2], rstd[:, 1 - k2, 1:2],
                                            ALU.subtract, ALU.mult).then_inc(x1_done, 1)
                if part == 6:
                    dve.wait_ge(x1_hi_done, t + 1)
                    nc.vector.tensor_tensor(x1hl[:, k2, 1, :], x1[:, t, :], x1hl[:, k2, 0, :], ALU.subtract).then_inc(x1_lo_done, 1)

            def route(i, j, lag, part):
                ok, t, k, r = stage(i, j, lag)
                if not ok:
                    return
                k2 = k % 2
                if part == 0:
                    dve.wait_ge(weights_loaded, 128)
                    nc.vector.max(mx[:, k2, :], lg[:, k, :]).then_inc(max_found, 1)
                if part == 1:
                    dve.wait_ge(weights_loaded, 128)
                    dve.wait_ge(max_found, t + 1)
                    nc.vector.max_index(ix[:, k2, :], mx[:, k2, :], lg[:, k, :]).then_inc(expert_found, 1)
                    if exists(t - U):
                        dve.wait_ge(weighed[k], r)
                    nc.vector.tensor_tensor(gap[:, k:k + 1], mx[:, k2, 0:1], mx[:, k2, 1:2], ALU.subtract).then_inc(gap_done, 1)
                if part == 3:
                    dve.wait_ge(expert_found, t + 1)
                    nc.vector.tensor_tensor(oh[:, k2, :, :], C("iota").unsqueeze(1).broadcast_to([P, TOP, EXPERTS]),
                                            ix[:, k2, 0:TOP].unsqueeze(2).broadcast_to([P, TOP, EXPERTS]), ALU.is_equal).then_inc(one_hot_done, 1)
                if part == 4:
                    dve.wait_ge(one_hot_done, t + 1)
                    if exists(t - 2):
                        dve.wait_ge(bank_p_written, t + 4)
                    nc.vector.tensor_tensor(chosen[:, k2, :], oh[:, k2, 0, :], oh[:, k2, 1, :], ALU.add).then_inc(choice_marked, 1)
                if part == 5:
                    dve.wait_ge(bank_p_written, t + 6)
                    if exists(t - 1):
                        dve.wait_ge(base_moved, t)
                    nc.vector.tensor_tensor(pe_[:, k2, :], rank_ps, base[:, :], ALU.add).then_inc(rank_based, 1)
                    dve.wait_ge(rank_based, t + 1)
                    nc.vector.tensor_tensor(base[:, :], total_ps, base[:, :], ALU.add).then_inc(base_moved, 1)
                if part == 6:
                    dve.wait_ge(rank_based, t + 1)
                    nc.vector.tensor_tensor(pr[:, k2, :, :], oh[:, k2, :, :], pe_[:, k2, :].unsqueeze(1).broadcast_to([P, TOP, EXPERTS]),
                                            ALU.mult).then_inc(place_picked, 1)
                if part == 7:
                    dve.wait_ge(place_picked, t + 1)
                    if exists(t - U):
                        dve.wait_ge(rows_scattered[k], 32 * r)
                    with nc.allow_low_precision("whole numbers below 2^24, exact in either type"):
                        nc.vector.tensor_reduce(place[:, k, :], pr[:, k2, :, :], AX.X, ALU.add)
                if part == 8:
                    nc.vector.tensor_copy(pay[:, k, :, DEST:DEST + 1].bitcast(i32), ind[:, bass.ds(TOP * t, TOP)].unsqueeze(2)).then_inc(placed[k], 1)

            for lag in (0, 1):
                rope_cos(0, 0, lag); rope_add(0, 0, lag); rope_lo(0, 0, lag)
            rope_cos(0, 0, 2)
            dve.wait_ge(indices_loaded, 16)

            def shared_add(q):
                dve.wait_ge(shared_y_done, q + 1)
                dve.wait_ge(x1_hi_done, 4 * q + 4)
                xq = x1[:, 4 * q:4 * q + 4, :].rearrange("p t c -> p (t c)")
                nc.vector.tensor_tensor(xq, shared_y[q % 2], xq, ALU.add).then_inc(shared_added, 1)

            def shared(q):
                if q == 0:
                    dve.wait_ge(attended, TILES)
                for c in range(SC if q < GROUPS else 0):
                    dve.wait_ge(shared_up_done, 2 * q + c + 1); dve.wait_ge(shared_silu_done, 2 * q + c + 1)
                    if q >= 2 and c == 0:
                        dve.wait_ge(shared_y_done, q - 1)
                    nc.vector.tensor_tensor(hS[:, q % 2, c, :], sS[:, q % 2, c, :], b_e[2 + c][:, :], ALU.mult).then_inc(shared_hidden_done, 1)
                if q:
                    shared_add(q - 1)

            link = [0]

            def table():

                def chain(ins):
                    link[0] += 1
                    ins.then_inc(table_step, 1)
                    dve.wait_ge(table_step, link[0])
                dve.wait_ge(base_moved, TILES)
                nc.vector.tensor_copy(ends[:, :], base[:, :]).then_inc(table_made, 1)
                chain(nc.vector.tensor_tensor(cnt[:, :], base[:, :], C("first"), ALU.subtract))
                chain(nc.vector.tensor_scalar(nti[:, :], cnt[:, :], float(SLOTS - 1), None, ALU.add))
                chain(nc.vector.tensor_scalar(ntj[:, :], nti[:, :], SLOTS.bit_length() - 1, None, ALU.logical_shift_right))
                chain(nc.vector.tensor_copy(nt[0][:, :], ntj[:, :]))
                for n in range(3):
                    d = 1 << n
                    nc.vector.tensor_copy(nt[n + 1][:, 0:d], nt[n][:, 0:d]).then_inc(table_step, 1)
                    link[0] += 1
                    chain(nc.vector.tensor_tensor(nt[n + 1][:, d:], nt[n][:, d:], nt[n][:, 0:EXPERTS - d], ALU.add))
                chain(nc.vector.tensor_scalar(ge[:, :], nt[3][:, :], C("row"), None, ALU.is_le))
                chain(nc.vector.tensor_tensor(gn[:, :], ge[:, :], nt[0][:, :], ALU.mult))
                chain(nc.vector.tensor_reduce(te[:, 0:1], ge[:, :], AX.X, ALU.add))
                chain(nc.vector.tensor_reduce(te[:, 1:2], gn[:, :], AX.X, ALU.add))
                chain(nc.vector.tensor_tensor(te[:, 2:3], C("row"), te[:, 1:2], ALU.subtract))
                chain(nc.vector.tensor_scalar(te[:, 3:4], te[:, 2:3], float(SLOTS), None, ALU.mult))
                chain(nc.vector.tensor_scalar(te[:, 4:5], te[:, 0:1], float(REGION), None, ALU.mult))
                chain(nc.vector.tensor_tensor(te[:, 5:6], te[:, 3:4], te[:, 4:5], ALU.add))
                chain(nc.vector.tensor_scalar(te[:, 6:7], te[:, 0:1], float(EXPERTS - 1), None, ALU.min))
                nc.vector.tensor_copy(tab[:, :], te[:, 5:7]).then_inc(table_made, 1)

            def body(i, j):
                step = U * i + j
                dmask(i, j, 0)
                rope_add(i, j, 2)
                for pair in range(2):
                    mask(i, j, 0, pair)
                rope_lo(i, j, 2)
                if exists(step - 2) and j == 2:
                    dve.wait_ge(x_biased, i + 1)
                tail(i, j, -2, 1)
                tail(i, j, -3, 5)
                if exists(step - 7) and not exists(step - 2):
                    dve.wait_ge(logits_copied, min(step - 5, TILES)); dve.wait_ge(x1T_copied, min(step - 4, TILES))
                route(i, j, -7, 5)
                tail(i, j, -2, 2)
                if exists(step - 6):
                    dve.wait_ge(logits_copied, step - 5)
                route(i, j, -7, 6)
                route(i, j, -6, 0)
                route(i, j, -7, 7)
                tail(i, j, -4, 6)
                rope_cos(i, j, 3)
                route(i, j, -6, 1)
                if exists(step - 2):
                    dve.wait_ge(x1_stats, step - 1)
                gate(i, j, -1)
                tail(i, j, -2, 3)
                route(i, j, -7, 8)
                route(i, j, -6, 3)
                route(i, j, -6, 4)
                if exists(step - 7) and not exists(step - 6):
                    table()
                if beside(i, j) is not None:
                    shared(beside(i, j))
            steps(dve, body, TILES, AFTER, PEEL, TAIL)

            for q in range(AFTER - 1, GROUPS + 1):
                shared(q)

            def evac(i, j, lag):
                ok, t, k, r = stage(i, j, lag, SLOT_TILES)
                if not ok:
                    return
                dve.wait_ge(slots_turned, t + 1)
                nc.vector.tensor_copy(xs16[:, k % 2, :, :], slotsT).then_inc(slots_copied, 1)
                if exists(t - U, SLOT_TILES):
                    dve.wait_ge(y_scattered[k], 32 * r)
                    dve.wait_ge(yscaled[k], r)
                nc.vector.tensor_copy(meta[:, k, :, :].bitcast(i32), xin[:, k, :, DEST:DEST + 2].bitcast(i32)).then_inc(meta_copied, 1)

            def hidden(i, j, c):
                t = U * i + j
                dve.wait_ge(expert_silu_done[c], t + 1)
                if c == 0 and exists(t - 2, SLOT_TILES):
                    dve.wait_ge(expert_y_done, t - 1)
                ins = nc.vector.tensor_tensor(hT[:, j % 2, c, :], sg[:, j % 2, c, :], up_banks[j % 2][c][:, SLOTS:], ALU.mult)
                if c == IC - 1:
                    ins.then_inc(hidden_done, 1)

            evac(0, 0, 0)

            def experts(i, j):
                hidden(i, j, 0)
                hidden(i, j, 1)
                evac(i, j, 1)
                hidden(i, j, 2)
            steps(dve, experts, SLOT_TILES, 0, 2, 1)

            def final_scale(q):
                cols = slice(FT * q, FT * q + FT)
                dve.wait_ge(final_recip, q + 1)
                nc.vector.scalar_tensor_tensor(out=fnb[:, cols], in0=fmv[:, cols, 0], scalar=-1.0, in1=frs[:, cols],
                                               op0=ALU.mult, op1=ALU.mult).then_inc(final_rstd, 1)

            for q in range(FINALS):
                a, b = FT * q, FT * (q + 1)
                if q % 2:
                    dve.wait_ge(results_loaded[q], 32)
                    nc.vector.tensor_tensor(x1[:, a:b, :], x1[:, a:b, :], y0[:, a:b, :], ALU.add).then_inc(odd_added, 1)
                    dve.wait_ge(odd_added, q // 2 + 1)
                else:
                    dve.wait_ge(first_added, q // 2 + 1)
                nc.vector.tensor_tensor(x1[:, a:b, :], x1[:, a:b, :], y1[:, a:b, :], ALU.add).then_inc(second_added, 1)
                dve.wait_ge(second_added, q + 1)
                for t in range(a, b):
                    nc.vector.bn_stats(fst[:, t, :], x1[:, t, :]).then_inc(final_stats, 1)
                for t in range(a, b):
                    dve.wait_ge(final_stats, t + 1)
                    nc.vector.bn_aggr(fmv[:, t, :], fst[:, t, :]).then_inc(final_moments, 1)
                if q:
                    final_scale(q - 1)
            final_scale(FINALS - 1)

        @block.gpsimd
        def _(pool):
            nc.gpsimd.memset(zero[:, :], 0.0).then_inc(zeroed, 1)
            nc.gpsimd.memset(vexp[:, :, :, :], 0.0).then_inc(setup_pool, 1)
            nc.gpsimd.memset(sacc[:, 0, :], 0.0).then_inc(setup_pool, 1)
            nc.gpsimd.memset(qk16[:, :, :], 0.0).then_inc(setup_pool, 1)
            nc.gpsimd.memset(shi[:, 0, :], 0.0).then_inc(setup_pool, 1)
            nc.gpsimd.memset(slo[:, 0, :], 0.0).then_inc(state_lo_done, 1)
            nc.gpsimd.memset(pay[:, :, :, :], 0.0).then_inc(setup_pool, 1)
            nc.gpsimd.memset(stat[:, :, :], 1.0).then_inc(setup_pool, 1)
            pool.wait_ge(weights_loaded, 128)

            def rope_sin(i, j, lag):
                ok, t, k, r = stage(i, j, lag)
                if not ok:
                    return
                pool.wait_ge(qk_silu_done, t + 1)
                if exists(t - U):
                    pool.wait_ge(roped, t - U + 1)
                sin = cst[:, bass.ds(CONST_AT["sin"][0] + t * HD, HD)].rearrange("p (s d) -> p s d", s=2).unsqueeze(1).broadcast_to([P, 2 * HEADS, 2, HD // 2])
                swapped = bass.AP(qk, offset=k * 2 * P + HD // 2, ap=[[U * 2 * P, P], [HD, 2 * HEADS], [-(HD // 2), 2], [1, HD // 2]])
                ins = nc.gpsimd.tensor_tensor(rs[:, k, :].rearrange("p (h s d) -> p h s d", s=2, d=HD // 2), swapped, sin, ALU.mult)
                ins.then_inc(sin_done, 1)

            def v16(i, j, lag):
                ok, t, k, r = stage(i, j, lag)
                if not ok:
                    return
                v4 = lambda a: a[:, k, :].rearrange("p (b h d) -> p h b d", b=4, h=4)
                pool.wait_ge(v_hi_done, t + 1)
                nc.gpsimd.tensor_tensor(v4(vl), vdiag(k), v4(vh), ALU.subtract).then_inc(v_lo_done, 1)

            def st(i, j, lag, part):
                ok, t, k, r = stage(i, j, lag)
                if not ok:
                    return
                n, o, slot = (k + 1) % 2, k % 2, (k + 1) % U
                before = zero[:, :] if k == U - 1 else sacc[:, o, :]
                if part == 0:
                    pool.wait_ge(delta_masked, t + 1)
                    if exists(t - 1):
                        pool.wait_ge(state_added, t); pool.wait_ge(state_lo_done, t + 1)
                    nc.gpsimd.tensor_tensor(sacc[:, n, :], before, dm[:, o, :], ALU.add).then_inc(state_added, 1)
                if part == 1:
                    if exists(t - 3):
                        pool.wait_ge(attended, t - 2)
                    nc.gpsimd.tensor_tensor(shi[:, slot, :], before, dm[:, o, :], ALU.add).then_inc(state_hi_done, 1)
                if part == 2:
                    pool.wait_ge(state_hi_done, t + 1)
                    nc.gpsimd.tensor_tensor(slo[:, slot, :], sacc[:, n, :], shi[:, slot, :], ALU.subtract).then_inc(state_lo_done, 1)

            def powers(i, j):
                step = U * i + j
                if not (exists(step - 2) or exists(step - 3)):
                    return
                if exists(step - 2):
                    pool.wait_ge(squares_summed, step - 1)
                if exists(step - 3):
                    pool.wait_ge(x1_moments, step - 2)
                small = C("small")
                nc.gpsimd.tensor_tensor(ve[:, :], bass.AP(stat, offset=3 * (j % 2), ap=[[6, P], [2, 2]]), small[:, 0:2], ALU.add).then_inc(var_eps_done, 1)
                pool.wait_ge(var_eps_done, step - 1)
                nc.gpsimd.tensor_tensor(rstd[:, j % 2, :], ve[:, :], small[:, 2:3].broadcast_to([P, 2]), ALU.pow).then_inc(powers_done, 1)

            for lag in (0, 1, 2):
                rope_sin(0, 0, lag)
            v16(0, 0, 0)

            def scatter(i, j, lag, c):
                ok, t, k, r = stage(i, j, lag)
                if not ok:
                    return
                pool.wait_ge(x_loaded, 64)
                nc.gpsimd.indirect_dma_start(out=rows, out_offset=bass.IndirectOffsetOnAxis(ap=place[:, k, c:c + 1], axis=0),
                                             in_=pay[:, k, c, :], in_offset=None).then_inc(rows_scattered[k], 16)

            def bias(i, j):
                if isinstance(i, int) and i == 0:
                    pool.wait_ge(x_loaded, 64); pool.wait_ge(setup_act, 4)
                xq = x_sb[:, bass.ds(U * i, U), :]
                nc.gpsimd.tensor_tensor(xq, xq, brow[:, :].unsqueeze(1).broadcast_to([P, U, P]), ALU.add).then_inc(x_biased, 1)

            def split_shared():
                pool.wait_ge(weights_hi_done, 1)
                nc.gpsimd.tensor_tensor(sl[:, :, 0:SHARED], sst_[:, :, :], sh[:, :, 0:SHARED], ALU.subtract).then_inc(weights_lo_done, 1)

            def split(e):
                pool.wait_ge(weights_hi_done, e + 2)
                nc.gpsimd.tensor_tensor(wl[:, e, :, 0:INNER], wst[:, e, :, :], wh[:, e, :, 0:INNER], ALU.subtract).then_inc(weights_lo_done, 1)

            def body(i, j):
                step = U * i + j
                ok, t, k, r = stage(i, j, -8)
                if ok:
                    pool.wait_ge(placed[k], r + 1); pool.wait_ge(weighed[k], r + 1)
                v16(i, j, 1)
                scatter(i, j, -8, 0)
                powers(i, j)
                scatter(i, j, -8, 1)
                for part in range(3):
                    st(i, j, 0, part)
                rope_sin(i, j, 3)
                if j == 0 and exists(step):
                    bias(i, j)
                if isinstance(i, int) and step == TILES - 3:
                    split_shared()
                if isinstance(i, int) and step >= TILES:
                    split(step - TILES)
            steps(pool, body, TILES, AFTER, PEEL, TAIL)

            with pool.Fori(1, SLOT_TILES // U + 1) as n:
                for j in range(U):
                    pool.wait_ge(table_made, 1); pool.wait_ge(yscaled[j], n)
                    for b in range(2):
                        nc.gpsimd.indirect_dma_start(out=ydram, out_offset=bass.IndirectOffsetOnAxis(ap=meta[:, j, b, 0:1].bitcast(u32), axis=0),
                                                     in_=yb[:, j, b, :], in_offset=None).then_inc(y_scattered[j], 16)

            def inverse_deviation(q):
                cols, small = slice(FT * q, FT * q + FT), C("small")
                pool.wait_ge(final_moments, FT * (q + 1))
                nc.gpsimd.tensor_tensor(fve[:, cols], fmv[:, cols, 1], small[:, 1:2].broadcast_to([P, FT]), ALU.add).then_inc(final_var_eps, 1)
                pool.wait_ge(final_var_eps, q + 1)
                nc.gpsimd.tensor_tensor(frs[:, cols], fve[:, cols], small[:, 2:3].broadcast_to([P, FT]), ALU.pow).then_inc(final_recip, 1)

            for q in range(0, FINALS, 2):
                a, b = FT * q, FT * (q + 1)
                pool.wait_ge(results_loaded[q], 32)
                nc.gpsimd.tensor_tensor(x1[:, a:b, :], x1[:, a:b, :], y0[:, a:b, :], ALU.add).then_inc(first_added, 1)
                for done in range(max(q - 2, 0), q):
                    inverse_deviation(done)
            inverse_deviation(FINALS - 2)
            inverse_deviation(FINALS - 1)


def kernel(**inputs):
    import numpy as _np
    import concourse.bacc as _bacc
    from concourse import mybir as _mybir
    from concourse.bass_utils import run_bass_kernel_spmd as _run

    a = lambda n: _np.asarray(inputs["L0_attn_" + n])
    f = lambda n: _np.asarray(inputs["L0_ffn_" + n])
    x = a("x").reshape(TOKENS, CH)
    data = dict(
        x=x, xT=x.T, Wqkv=_np.concatenate([a("Wq"), a("Wk"), a("Wv")], 1), Wg1T=a("Wg1").T, Wg2=a("Wg2"), Wo=a("Wo"),
        ln=_np.stack([a("ln_w"), a("ln_b")], 1), gate_w=f("gate_w"), Wg=f("Wg"), Wu=f("Wu"), Wd=f("Wd"),
        Sgu=_np.stack([f("Sg"), f("Su")], 1), Sd=f("Sd"),
        consts=constants()[0], halves=half_constants(), indices=index_constants(), pads=pad_rows())
    nc = _bacc.Bacc("TRN2", target_bir_lowering=False, num_devices=1)
    arrays, args = {}, {}
    for name, array in data.items():
        array = _np.ascontiguousarray(array)
        arrays["in_" + name] = array
        args[name] = nc.dram_tensor("in_" + name, array.shape, _mybir.dt.from_np(array.dtype), kind="ExternalInput").ap()
    out = nc.dram_tensor("out_0", (TOKENS, CH), _mybir.dt.float32, kind="ExternalOutput").ap()
    build(nc, out=out, **args)
    r = _run(nc, [arrays], core_ids=[0])
    return _np.asarray(r.results[0]["out_0"]).reshape(4, SEQ, CH)
```

```python
import math
from contextlib import ExitStack

import numpy as np
import concourse.bass as bass
from concourse import mybir

TOKENS, CH, HEADS, HD = 4096, 128, 16, 8
P = 128
TILES = TOKENS // P
SEQ = 1024
BATCH_TILES = SEQ // P
EPS = 1e-5
BLOCKS = 4
U = 4
EXPERTS, TOP, INNER, SHARED = 8, 2, 352, 176
IC = 3
SC = 2
SLOTS = 2 * P
REGION = TOKENS + SLOTS
SLOT_TILES = (TOP * TOKENS + EXPERTS * (SLOTS - 1)) // SLOTS
DUMMY = SLOT_TILES - TOP * TOKENS // SLOTS
ROW = 132
DEST, WEIGHT = 128, 129
PEEL, TAIL, AFTER = 3, 1, 8
GROUPS = TILES // 4
FINALS, FT = 8, TILES // 8
DEVIATION_CUTS = (0, 2, 4, 6, 7, 8)
DEVIATION_LAG = 1
FINALS_ON_ACT = 6
YROWS = TOP * TOKENS + (EXPERTS + DUMMY) * SLOTS


def constants():
    f = np.float32
    d = HD
    inv = (f(1.0) / np.power(f(10000.0), np.arange(0, d, 2, dtype=f) / f(d))).astype(f)
    ang = (np.arange(SEQ, dtype=f)[:, None] * inv[None, :]).astype(f).astype(np.float64)
    cos = np.concatenate([np.cos(ang), np.cos(ang)], -1)
    sin = np.concatenate([-np.sin(ang), np.sin(ang)], -1)
    tab = lambda a: np.tile(a.reshape(BATCH_TILES, P, d).transpose(1, 0, 2), (1, TOKENS // SEQ, 1)).reshape(P, TILES * d)
    tri = (np.arange(P)[:, None] <= np.arange(P)[None, :])
    row = np.arange(P)
    col = np.arange(P)
    own = (row[:, None] // 32) == ((col[None, :] % 32) // 8)
    keep = np.tile(((np.arange(TILES) + 1) % BATCH_TILES != 0).astype(f)[None, :], (P, 1))
    center = 0.5 * (np.eye(P) - 1.0 / P)
    parts = {"cos": tab(cos), "sin": tab(sin), "tri": tri, "own": own, "keep": keep, "center": center,
             "iota": np.tile(np.arange(EXPERTS)[None, :], (P, 1)),
             "first": np.tile(np.arange(EXPERTS)[None, :] * REGION, (P, 1)),
             "row": np.arange(P)[:, None],
             "small": np.tile(np.array([[CH * EPS, EPS, -0.5]]), (P, 1))}
    at, n = {}, 0
    for k, a in parts.items():
        at[k] = (n, a.shape[1]); n += a.shape[1]
    return np.concatenate([np.asarray(a, f) for a in parts.values()], 1), at


def index_constants():
    p = np.arange(P)[:, None, None]
    pairs = (np.arange(TOP)[None, None, :] * TOKENS + np.arange(TILES)[None, :, None] * P + p).reshape(P, -1)
    return pairs.astype(np.int32)


def pad_rows():
    rows = np.zeros(((EXPERTS + DUMMY) * SLOTS, ROW), np.int32)
    rows[:, DEST] = TOP * TOKENS + np.arange(len(rows))
    return rows.view(np.float32)


def half_constants():
    r = np.arange(P)
    return np.concatenate([np.eye(P), r[:, None] < r[None, :], np.ones((P, P))], 1).astype(np.float16)


_, CONST_AT = constants()
CONST_W = sum(w for _, w in CONST_AT.values())


def build(nc, x, xT, Wqkv, Wg1T, Wg2, Wo, ln, gate_w, Wg, Wu, Wd, Sgu, Sd, consts, halves, indices, pads, out):
    f32, f16, i32, u32 = mybir.dt.float32, mybir.dt.float16, mybir.dt.int32, mybir.dt.uint32
    ALU, ACT, AX = mybir.AluOpType, mybir.ActivationFunctionType, mybir.AxisListType
    ctx = ExitStack()
    with ctx:
        sb = lambda n, s, d=f32: ctx.enter_context(nc.sbuf_tensor(n, s, d))
        ps = lambda n, s, d=f32: ctx.enter_context(nc.psum_tensor(n, s, d))
        sem = lambda n: ctx.enter_context(nc.semaphore(n))
        const_sb = sb("const_sb", [P, CONST_W])
        C = lambda k: const_sb[:, CONST_AT[k][0]:CONST_AT[k][0] + CONST_AT[k][1]]
        half = sb("half", [P, 3 * P], f16)
        identity, earlier_tokens, all_ones = half[:, 0:P], half[:, P:2 * P], half[:, 2 * P:]
        destinations = sb("destinations", [P, TOP * TILES], i32)
        w_in = sb("w_in", [P, 4 * P])
        g1T = sb("g1T", [HD, P])
        g2 = sb("g2", [HD, P])
        ln_w_b = sb("ln_w_b", [P, 2])
        wo = sb("wo", [P, P])
        wo_scaled = sb("wo_scaled", [P, P])
        ones = sb("ones", [P, P])
        ln_b_cols = sb("ln_b_cols", [P, P])
        rhs2 = sb("rhs2", [P, 2 * P])
        bias_row = sb("bias_row", [P, P])
        router_w = sb("router_w", [P, EXPERTS])
        router_w_hi = sb("router_w_hi", [P, EXPERTS], f16)
        router_w_lo = sb("router_w_lo", [P, EXPERTS], f16)
        zero = sb("zero", [P, P])

        x_sb = sb("x_sb", [P, TILES, P])
        x1 = sb("x1", [P, TILES, P])
        x1T = sb("x1T", [P, 2, TOKENS], f16)

        xT_ring = sb("xT_ring", [P, U, P])
        qk = sb("qk", [P, U, 2 * P])
        roped_qk = sb("roped_qk", [P, U, 2 * P])
        turned_qk = sb("turned_qk", [P, U, 2 * P])
        qk16 = sb("qk16", [P, U, 2 * 4 * P], f16)
        qkT = sb("qkT", [P, U, 8, P], f16)
        gate_tanh = sb("gate_tanh", [P, U, P])
        vexp = sb("vexp", [P, U, 4, P])
        v_hi = sb("v_hi", [P, U, P], f16)
        v_lo = sb("v_lo", [P, U, P], f16)
        masked_energies = sb("masked_energies", [P, 2, 4, 4 * P])
        delta_own = sb("delta_own", [P, P])
        delta_kept_own = sb("delta_kept_own", [P, 2, P])
        state_sum = sb("state_sum", [P, 2, P])
        state_hi = sb("state_hi", [P, U, P], f16)
        state_lo = sb("state_lo", [P, U, P], f16)
        gated_out = sb("gated_out", [P, 2, P])
        squares_out = sb("squares_out", [P, P])
        stat = sb("stat", [P, 2, 3])
        var_eps = sb("var_eps", [P, 2])
        rstd = sb("rstd", [P, 2, 2])
        x_plus = sb("x_plus", [P, 2, P])
        moment_parts = sb("moment_parts", [P, 2, 6])
        x1_halves = sb("x1_halves", [P, 2, 2, P], f16)

        logits = sb("logits", [P, U, EXPERTS])
        top_logits = sb("top_logits", [P, 2, 8])
        top_experts = sb("top_experts", [P, 2, 8], u32)
        one_hot = sb("one_hot", [P, 2, TOP, EXPERTS])
        chosen = sb("chosen", [P, 2, EXPERTS], f16)
        gap = sb("gap", [P, U])
        gap_tanh = sb("gap_tanh", [P, U])
        base = sb("base", [P, EXPERTS])
        expert_places = sb("expert_places", [P, 2, EXPERTS])
        picked_places = sb("picked_places", [P, 2, TOP, EXPERTS])
        place = sb("place", [P, U, TOP], u32)
        payloads = sb("payloads", [P, U, TOP, ROW])
        payload_halves = lambda k: payloads[:, k, :, 0:P].bitcast(f16)

        ends = sb("ends", [P, EXPERTS], i32)
        pair_counts = sb("pair_counts", [P, EXPERTS])
        counts_up = sb("counts_up", [P, EXPERTS], i32)
        tiles_int = sb("tiles_int", [P, EXPERTS], i32)
        tile_sums = [sb(f"tile_sums{n}", [P, EXPERTS]) for n in range(4)]
        ended = sb("ended", [P, EXPERTS])
        ended_tiles = sb("ended_tiles", [P, EXPERTS])
        entry = sb("entry", [P, 8])
        tile_entries = sb("tile_entries", [P, 2], i32)
        tile_list = sb("tile_list", [1, 2 * P], i32)

        FFN_LOADS = 16 * (3 + 2 + IC)
        ffn_staged = sb("ffn_staged", [P, EXPERTS, 2, INNER])
        w_hi = sb("w_hi", [P, EXPERTS, 2, IC * P], f16)
        w_lo = sb("w_lo", [P, EXPERTS, 2, IC * P], f16)
        w_down = sb("w_down", [P, EXPERTS, IC * P])
        w_hi_flat, w_lo_flat = (w[:, :, :, :].rearrange("p e g n -> p (e g n)") for w in (w_hi, w_lo))
        w_hi_rows, w_lo_rows = (w[:, :, :, :].rearrange("p e g n -> p (e g) n") for w in (w_hi, w_lo))
        w_down_flat = w_down[:, :, :].rearrange("p e n -> p (e n)")
        shared_staged = sb("shared_staged", [P, 2, SHARED])
        shared_hi = sb("shared_hi", [P, 2, SC * P], f16)
        shared_lo = sb("shared_lo", [P, 2, SC * P], f16)
        shared_w_down = sb("shared_w_down", [P, SC, P])

        flat = lambda a: a[:, :, :, :].rearrange("p a b c -> p (a b c)")
        slot_rows = flat(vexp)[:, 0:U * 2 * ROW].rearrange("p (a b n) -> p a b n", a=U, b=2)
        slots_T = sb("slots_T", [P, 2, 2, SLOTS], f16)
        slot_meta = sb("slot_meta", [P, U, 2, 2])
        silu_gate = flat(masked_energies)[:, 0:2 * IC * SLOTS].rearrange("p (a c n) -> p a c n", a=2, c=IC)
        hidden_T = flat(masked_energies)[:, 2 * IC * SLOTS:4 * IC * SLOTS].rearrange("p (a c n) -> p a c n", a=2, c=IC)
        scaled_y = sb("scaled_y", [P, U, 2, P])
        shared_hidden_T = flat(masked_energies)[:, 0:4 * 512].rearrange("p (a c n) -> p a c n", a=2, c=SC)
        shared_silu_T = flat(masked_energies)[:, 4 * 512:8 * 512].rearrange("p (a c n) -> p a c n", a=2, c=SC)

        y0 = x_sb[:, :, :]
        y1 = bass.AP(ffn_staged, offset=0, ap=[[EXPERTS * 2 * INNER, P], [P, TILES], [1, P]])
        final_parts = sb("final_parts", [P, TILES, 6])
        final_mean_var = sb("final_mean_var", [P, TILES, 2])
        final_var = sb("final_var", [P, TILES])
        final_inverse = sb("final_inverse", [P, TILES])
        final_shift = sb("final_shift", [P, TILES])

        rows = nc.dram_tensor("rows", [(EXPERTS + 1) * REGION, ROW], f32).ap()
        ydram = nc.dram_tensor("ydram", [YROWS, P], f32).ap()

        def vdiag(k):
            return bass.AP(vexp, offset=k * 4 * P, ap=[[U * 4 * P, P], [P + HD, 4], [32, 4], [1, HD]])

        b_in = ps("b_in", [P, 4 * P])
        b_t = ps("b_t", [P, 8, P], f16)
        b_es = ps("b_es", [P, 4, 4 * P])
        b_e = [b_es[:, i, :] for i in range(4)]
        b_o = ps("b_o", [P, 4 * P])
        b_p = ps("b_p", [P, 4 * P])
        delta, outT = b_o[:, 0:P], b_o[:, P:2 * P]
        projected_out = b_p[:, 0:2 * P]
        x1T_ps = b_p[:, 2 * P:3 * P].bitcast(f16)
        logits_ps = b_p[:, 3 * P:3 * P + EXPERTS]
        rank_ps = b_p[:, 3 * P + EXPERTS:3 * P + 2 * EXPERTS]
        total_ps = b_p[:, 3 * P + 2 * EXPERTS:3 * P + 3 * EXPERTS]
        slots_T_ps = b_in[:, 0:SLOTS].bitcast(f16).rearrange("p (a n) -> p a n", a=2)
        y_ps = b_t[:, :, :].rearrange("p a c -> p (a c)").bitcast(f32)
        shared_y = [b_in[:, :], y_ps]
        up_banks = [(b_e[0], b_e[1], b_e[2]), (b_e[3], b_o, b_p)]

        weights_loaded = sem("weights_loaded")
        x_loaded = sem("x_loaded")
        indices_loaded = sem("indices_loaded")
        ffn_loaded = sem("ffn_loaded")
        zeroed = sem("zeroed")
        setup_act = sem("setup_act")
        setup_products = sem("setup_products")
        setup_dve = sem("setup_dve")
        setup_pool = sem("setup_pool")
        weights_padded = sem("weights_padded")
        weights_hi_done = sem("weights_hi_done")
        weights_lo_done = sem("weights_lo_done")
        projected = sem("projected")
        qk_silu_done = sem("qk_silu_done")
        gate_tanh_done = sem("gate_tanh_done")
        v_hi_done = sem("v_hi_done")
        v_lo_done = sem("v_lo_done")
        cos_done = sem("cos_done")
        sin_done = sem("sin_done")
        roped = sem("roped")
        qk_hi_done = sem("qk_hi_done")
        qk_lo_done = sem("qk_lo_done")
        qk_turned = sem("qk_turned")
        qkT_copied = sem("qkT_copied")
        delta_done = sem("delta_done")
        delta_kept = sem("delta_kept")
        delta_masked = sem("delta_masked")
        state_added = sem("state_added")
        state_hi_done = sem("state_hi_done")
        state_lo_done = sem("state_lo_done")
        attended = sem("attended")
        gated = sem("gated")
        bank_p_written = sem("bank_p_written")
        squares_summed = sem("squares_summed")
        var_eps_done = sem("var_eps_done")
        powers_done = sem("powers_done")
        x_biased = sem("x_biased")
        x_summed = sem("x_summed")
        x1_stats = sem("x1_stats")
        x1_moments = sem("x1_moments")
        x1_done = sem("x1_done")
        x1_hi_done = sem("x1_hi_done")
        x1_lo_done = sem("x1_lo_done")
        x1T_copied = sem("x1T_copied")
        x1_packed = sem("x1_packed")
        logits_done = sem("logits_done")
        logits_copied = sem("logits_copied")
        max_found = sem("max_found")
        expert_found = sem("expert_found")
        gap_done = sem("gap_done")
        gap_tanh_done = sem("gap_tanh_done")
        one_hot_done = sem("one_hot_done")
        choice_marked = sem("choice_marked")
        rank_based = sem("rank_based")
        base_moved = sem("base_moved")
        place_picked = sem("place_picked")
        table_step = sem("table_step")
        table_made = sem("table_made")
        table_loaded = sem("table_loaded")
        fill_rows_stored = sem("fill_rows_stored")
        dummy_rows_stored = sem("dummy_rows_stored")
        shared_gate_done = sem("shared_gate_done")
        shared_up_done = sem("shared_up_done")
        shared_silu_done = sem("shared_silu_done")
        shared_hidden_done = sem("shared_hidden_done")
        shared_y_done = sem("shared_y_done")
        shared_added = sem("shared_added")
        slots_turned = sem("slots_turned")
        slots_copied = sem("slots_copied")
        meta_copied = sem("meta_copied")
        hidden_done = sem("hidden_done")
        expert_y_done = sem("expert_y_done")
        first_half_added = sem("first_half_added")
        first_added = sem("first_added")
        second_added = sem("second_added")
        final_stats = sem("final_stats")
        final_moments = sem("final_moments")
        final_var_eps = sem("final_var_eps")
        final_recip = sem("final_recip")
        final_rstd = sem("final_rstd")
        normalised = sem("normalised")
        last_normalised = sem("last_normalised")
        out_stored = sem("out_stored")
        xT_loaded = [sem(f"xT_loaded{k}") for k in range(U)]
        expert_up_done = [sem(f"expert_up_done{c}") for c in range(IC)]
        expert_silu_done = [sem(f"expert_silu_done{c}") for c in range(IC)]
        energies_done = [sem(f"energies_done{h}") for h in range(2)]
        masked = [sem(f"masked{h}") for h in range(2)]
        rows_scattered = [sem(f"rows_scattered{k}") for k in range(U)]
        slots_loaded = [sem(f"slots_loaded{k}") for k in range(U)]
        placed = [sem(f"placed{k}") for k in range(U)]
        weighed = [sem(f"weighed{k}") for k in range(U)]
        yscaled = [sem(f"yscaled{k}") for k in range(U)]
        y_scattered = [sem(f"y_scattered{k}") for k in range(U)]
        results_loaded = [sem(f"results_loaded{k}") for k in range(FINALS)]
        block = ctx.enter_context(nc.Block())

        def steps(eng, body, n, after, peel, tail):
            for i in range(peel):
                for j in range(U):
                    body(i, j)
            with eng.Fori(peel, n // U - tail) as i:
                for j in range(U):
                    body(i, j)
            for step in range((n // U - tail) * U, n + after):
                body(step // U, step % U)

        def beside(i, j):
            return U * i + j - TILES - 1 if isinstance(i, int) and U * i + j > TILES else None

        def exists(t, n=TILES):
            return not isinstance(t, int) or 0 <= t < n

        def stage(i, j, lag, n=TILES):
            k = j + lag
            return exists(U * i + k, n), U * i + k, k % U, i + k // U

        @block.sync
        def _(sp):
            sp.dma_start(const_sb[:, :], consts).then_inc(weights_loaded, 16)
            sp.dma_start(w_in[:, 0:3 * P], Wqkv).then_inc(weights_loaded, 16)
            sp.dma_start(wo[:, :], Wo).then_inc(weights_loaded, 16)
            sp.dma_start(ln_w_b[:, :], ln).then_inc(weights_loaded, 16)
            for k in range(U):
                sp.dma_start(xT_ring[:, k, :], xT[:, k * P:(k + 1) * P]).then_inc(xT_loaded[k], 16)
            sp.dma_start(destinations[:, :], indices).then_inc(indices_loaded, 16)
            for b in range(4):
                sp.dma_start(x_sb[:, 8 * b:8 * b + 8, :], x[SEQ * b:SEQ * (b + 1), :].rearrange("(t p) c -> p t c", p=P)).then_inc(x_loaded, 16)
            sp.dma_start(rows[EXPERTS * REGION:EXPERTS * REGION + DUMMY * SLOTS, :], pads[EXPERTS * SLOTS:, :]).then_inc(dummy_rows_stored, 16)
            w_down_chunks = w_down[:, :, :].rearrange("p e (c h) -> p e c h", c=IC)

            def load_xT(i):
                for j in range(U):
                    sp.wait_ge(projected, U * i + j + 1)
                    sp.dma_start(xT_ring[:, j, :], xT[:, bass.ds((U * i + j + U) * P, P)]).then_inc(xT_loaded[j], 16)

            load_xT(0)
            sp.dma_start(shared_staged[:, :, :], Sgu).then_inc(ffn_loaded, 16)
            sp.dma_start(ffn_staged[:, :, 0, :], Wg.rearrange("e h i -> h e i")).then_inc(ffn_loaded, 16)
            load_xT(1)
            sp.dma_start(ffn_staged[:, :, 1, :], Wu.rearrange("e h i -> h e i")).then_inc(ffn_loaded, 16)
            sp.dma_start(shared_w_down[:, 0, :], Sd[0:P, :]).then_inc(ffn_loaded, 16)
            sp.dma_start(shared_w_down[0:SHARED - P, 1, :], Sd[P:SHARED, :]).then_inc(ffn_loaded, 16)
            load_xT(2)
            for c in range(IC):
                n = min(P, INNER - c * P)
                sp.dma_start(w_down_chunks[0:n, :, c, :], Wd[:, c * P:c * P + n, :].rearrange("e i h -> i e h")).then_inc(ffn_loaded, 16)
            with sp.Fori(3, TILES // U - 1) as i:
                load_xT(i)
            sp.wait_ge(table_made, 1)
            for e in range(EXPERTS // 2):
                end = sp.value_load(ends[0:1, e:e + 1], min_val=0, max_val=EXPERTS * REGION)
                sp.dma_start(rows[bass.ds(end, SLOTS), :], pads[e * SLOTS:(e + 1) * SLOTS, :]).then_inc(fill_rows_stored, 16)
            sp.wait_ge(table_made, 2)
            sp.dma_start(tile_list[0:1, :], tile_entries[:, :]).then_inc(table_loaded, 16)
            sp.wait_ge(table_loaded, 16)
            for k in range(U):
                sp.wait_ge(rows_scattered[k], 2 * 16 * (TILES // U))
            sp.wait_ge(fill_rows_stored, 16 * EXPERTS)
            sp.wait_ge(dummy_rows_stored, 16)

            def load(i, j):
                t = U * i + j
                at = sp.value_load(tile_list[0:1, bass.ds(2 * t, 1)], min_val=0, max_val=EXPERTS * REGION + (DUMMY - 1) * SLOTS)
                at = sp.snap(at)
                if exists(t - U, SLOT_TILES):
                    sp.wait_ge(slots_turned, t - U + 1)
                    sp.wait_ge(meta_copied, t - U + 1)
                    sp.wait_ge(table_loaded, 16)
                sp.dma_start(slot_rows[:, j, :, :], rows[bass.ds(at, SLOTS), :].rearrange("(b p) w -> p b w", p=P)).then_inc(slots_loaded[j], 16)
            steps(sp, load, SLOT_TILES, 0, 2, 0)

            for k in range(U):
                sp.wait_ge(y_scattered[k], 32 * ((SLOT_TILES - k + U - 1) // U))
            for q in range(FINALS):
                for c, dst in enumerate((y0, y1)):
                    sp.dma_start(dst[:, FT * q:FT * q + FT, :], ydram[c * TOKENS + q * FT * P:c * TOKENS + (q + 1) * FT * P, :]
                                 .rearrange("(t p) c -> p t c", p=P)).then_inc(results_loaded[q], 16)
            for q in range(FINALS):
                if q < FINALS_ON_ACT:
                    sp.wait_ge(normalised, FT * (q + 1))
                else:
                    sp.wait_ge(last_normalised, FT * (q - FINALS_ON_ACT + 1))
                sp.dma_start(out[q * FT * P:(q + 1) * FT * P, :].rearrange("(t p) c -> p t c", p=P), x1[:, FT * q:FT * q + FT, :]).then_inc(out_stored, 16)
            sp.wait_ge(out_stored, 16 * FINALS)

        @block.tensor
        def _(pe):
            pe.wait_ge(weights_loaded, 128)
            pe.wait_ge(setup_dve, 3)
            nc.tensor.matmul(b_p[:, 0:P], C("center"), wo_scaled[:, :], start=True, stop=True)
            nc.tensor.matmul(b_p[:, P:2 * P], g1T[:, :], g2[:, :], start=True, stop=True)
            nc.tensor.matmul(b_p[:, 2 * P:3 * P], ln_b_cols[:, :], wo[:, :], start=True, stop=True).then_inc(setup_products, 1)

            def proj(i, j, lag):
                ok, t, k, r = stage(i, j, lag)
                if not ok:
                    return
                pe.wait_ge(xT_loaded[k], 16 * (r + 1))
                if exists(t - 1):
                    pe.wait_ge(v_hi_done, t)
                nc.tensor.matmul(b_in[:, 0:3 * P], xT_ring[:, k, :], w_in[:, 0:3 * P], start=True, stop=True)
                nc.tensor.matmul(b_in[:, 3 * P:], w_in[:, 3 * P:], xT_ring[:, k, :], start=True, stop=True).then_inc(projected, 1)

            def qk_turn(i, j, lag):
                ok, t, k, r = stage(i, j, lag)
                if not ok:
                    return
                pe.wait_ge(qk_lo_done, t + 1); pe.wait_ge(qk_hi_done, t + 1)
                if exists(t - 1):
                    pe.wait_ge(qkT_copied, t)
                for b in range(2 * BLOCKS):
                    mm = nc.tensor.transpose(b_t[:, b, :], qk16[:, k, b * P:(b + 1) * P], identity)
                mm.then_inc(qk_turned, 1)

            def energies(i, j, lag):
                ok, t, k, r = stage(i, j, lag)
                if not ok:
                    return
                pe.wait_ge(qkT_copied, t + 1)
                for pair in ((0, 1), (2, 3)):
                    if exists(t - 1):
                        pe.wait_ge(masked[pair[0] // 2], t)
                    for b in range(BLOCKS):
                        for h4 in pair:
                            own_rows = slice(32 * h4, 32 * h4 + 32)
                            mm = nc.tensor.matmul(b_es[:, h4, b * P:(b + 1) * P], qkT[own_rows, k, 4 + b, :],
                                                  qkT[own_rows, k, b, :], start=True, stop=True)
                    mm.then_inc(energies_done[pair[0] // 2], 1)

            def state(i, j, lag):
                ok, t, k, r = stage(i, j, lag)
                if not ok:
                    return
                pe.wait_ge(v_lo_done, t + 1)
                if exists(t - 2):
                    pe.wait_ge(gated, t - 1)
                for b in range(BLOCKS):
                    kk = qk16[:, k, (4 + b) * P:(5 + b) * P]
                    o = delta[:, 32 * b:32 * b + 32]
                    vcol = slice(32 * b, 32 * b + 32)
                    nc.tensor.matmul(o, kk, v_hi[:, k, vcol], start=True, stop=False)
                    mm = nc.tensor.matmul(o, kk, v_lo[:, k, vcol], start=False, stop=True)
                mm.then_inc(delta_done, 1)

            def attend(i, j, lag):
                ok, t, k, r = stage(i, j, lag)
                if not ok:
                    return
                pe.wait_ge(delta_masked, t + 2 if exists(t + 1) else TILES)
                for h4 in range(4):
                    if h4 % 2 == 0:
                        pe.wait_ge(masked[h4 // 2], t + 1)
                    for b in range(BLOCKS):
                        cols = slice(32 * b, 32 * b + 32)
                        nc.tensor.matmul(outT[cols, :], vexp[:, k, h4, cols], masked_energies[:, k % 2, h4, b * P:(b + 1) * P],
                                         start=(h4 == 0), stop=False, tile_position=(0, 32 * b))
                pe.wait_ge(state_lo_done, t + 1)
                for b in range(BLOCKS):
                    cols = slice(32 * b, 32 * b + 32)
                    nc.tensor.matmul(outT[cols, :], state_hi[:, k, cols], qkT[:, k, b, :], start=False, stop=False, tile_position=(0, 32 * b))
                    mm = nc.tensor.matmul(outT[cols, :], state_lo[:, k, cols], qkT[:, k, b, :], start=False, stop=True, tile_position=(0, 32 * b))
                mm.then_inc(attended, 1)

            def router(i, j, lag):
                ok, t, k, r = stage(i, j, lag)
                if not ok:
                    return
                pe.wait_ge(x1T_copied, t + 1)
                xh, xl = x1T[:, 0, bass.ds(t * P, P)], x1T[:, 1, bass.ds(t * P, P)]
                nc.tensor.matmul(logits_ps, xh, router_w_hi[:, :], start=True, stop=False)
                nc.tensor.matmul(logits_ps, xl, router_w_hi[:, :], start=False, stop=False)
                nc.tensor.matmul(logits_ps, xh, router_w_lo[:, :], start=False, stop=True).then_inc(logits_done, 1)

            def rank(i, j, lag):
                ok, t, k, r = stage(i, j, lag)
                if not ok:
                    return
                pe.wait_ge(choice_marked, t + 1)
                nc.tensor.matmul(rank_ps, earlier_tokens, chosen[:, k % 2, :], start=True, stop=True)
                return nc.tensor.matmul(total_ps, all_ones, chosen[:, k % 2, :], start=True, stop=True)

            def proj2(i, j, lag):
                ok, t, k, r = stage(i, j, lag)
                if not ok:
                    return
                pe.wait_ge(gated, t + 1)
                return nc.tensor.matmul(projected_out, gated_out[:, k % 2, :], rhs2[:, :], start=True, stop=True)

            def bank_p(i, j):
                step = U * i + j
                if not (exists(step - 2) or exists(step - 7)):
                    return
                if exists(step - 3):
                    pe.wait_ge(x_summed, step - 2)
                if exists(step - 6):
                    pe.wait_ge(x1T_copied, step - 5)
                if exists(step - 7):
                    pe.wait_ge(logits_copied, step - 6)
                if exists(step - 8):
                    pe.wait_ge(base_moved, step - 7)
                router(i, j, -6)
                last = rank(i, j, -7)
                last = x1_turn(i, j, -5) or last
                last = proj2(i, j, -2) or last
                last.then_inc(bank_p_written, 1)

            def x1_turn(i, j, lag):
                ok, t, k, r = stage(i, j, lag)
                if not ok:
                    return
                pe.wait_ge(x1_lo_done, t + 1)
                nc.tensor.transpose(x1T_ps[:, 0:P], x1_halves[:, k % 2, 0, :], identity)
                return nc.tensor.transpose(x1T_ps[:, P:2 * P], x1_halves[:, k % 2, 1, :], identity)

            pe.wait_ge(setup_act, 4)
            proj(0, 0, 0); proj(0, 0, 1)
            qk_turn(0, 0, 0)
            proj(0, 0, 2)

            def shared_up(q):
                for c in range(SC):
                    if q:
                        pe.wait_ge(shared_hidden_done, 2 * q - 1 + c)
                    for gu in range(2):
                        bank = b_e[2 * gu + c][:, :]
                        w, wlo = shared_hi[:, gu, c * P:(c + 1) * P], shared_lo[:, gu, c * P:(c + 1) * P]
                        xh, xl = x1T[:, 0, q * 512:(q + 1) * 512], x1T[:, 1, q * 512:(q + 1) * 512]
                        nc.tensor.matmul(bank, w, xh, start=True, stop=False)
                        nc.tensor.matmul(bank, w, xl, start=False, stop=False)
                        nc.tensor.matmul(bank, wlo, xh, start=False, stop=True).then_inc(shared_up_done if gu else shared_gate_done, 1)

            def shared_down(q):
                k = q % 2
                pe.wait_ge(shared_hidden_done, 2 * q + 2)
                if q >= 2:
                    pe.wait_ge(shared_added, q - 1)
                for n in range(4):
                    o = shared_y[k][:, n * P:(n + 1) * P]
                    nc.tensor.matmul(o, shared_hidden_T[:, k, 0, n * P:(n + 1) * P], shared_w_down[:, 0, :], start=True, stop=False)
                    mm = nc.tensor.matmul(o, shared_hidden_T[0:SHARED - P, k, 1, n * P:(n + 1) * P], shared_w_down[0:SHARED - P, 1, :], start=False, stop=True)
                mm.then_inc(shared_y_done, 1)

            def shared(q):
                if q == 0:
                    pe.wait_ge(weights_hi_done, 1); pe.wait_ge(weights_lo_done, 1)
                    pe.wait_ge(weights_padded, 4); pe.wait_ge(ffn_loaded, FFN_LOADS)
                    for pair in range(2):
                        pe.wait_ge(masked[pair], TILES)
                    pe.wait_ge(v_hi_done, TILES); pe.wait_ge(qkT_copied, TILES)
                if q < GROUPS:
                    pe.wait_ge(x1T_copied, 4 * q + 4)
                    shared_up(q)
                if q:
                    shared_down(q - 1)

            def body(i, j):
                energies(i, j, 0)
                state(i, j, 0)
                bank_p(i, j)
                proj(i, j, 3)
                qk_turn(i, j, 1)
                attend(i, j, -1)
                if beside(i, j) is not None:
                    shared(beside(i, j))
            steps(pe, body, TILES, AFTER, PEEL, TAIL)
            for q in range(AFTER - 1, GROUPS + 1):
                shared(q)

            pe.wait_ge(table_loaded, 16)
            pe.wait_ge(shared_hidden_done, 2 * GROUPS); pe.wait_ge(shared_added, GROUPS)
            pe.wait_ge(weights_hi_done, 1 + EXPERTS); pe.wait_ge(weights_lo_done, 1 + EXPERTS)
            pe.wait_ge(base_moved, TILES)

            def turn(i, j, lag):
                ok, t, k, r = stage(i, j, lag, SLOT_TILES)
                if not ok:
                    return
                pe.wait_ge(slots_loaded[k], 16 * (r + 1))
                for b in range(2):
                    for a in range(2):
                        mm = nc.tensor.transpose(slots_T_ps[:, a, b * P:(b + 1) * P], slot_rows[:, k, b, 64 * a:64 * a + 64].bitcast(f16), identity)
                mm.then_inc(slots_turned, 1)

            def expert_of(t):
                return pe.value_load(tile_list[0:1, bass.ds(2 * t + 1, 1)], min_val=0, max_val=EXPERTS - 1)

            def up(i, j, e):
                t = U * i + j
                pe.wait_ge(slots_copied, t + 1)
                for c in range(IC):
                    for gu in range(2):
                        o = up_banks[j % 2][c][:, gu * SLOTS:(gu + 1) * SLOTS]
                        at = e * (2 * IC * P) + (gu * IC + c) * P
                        w, wlo = w_hi_flat[:, bass.ds(at, P)], w_lo_flat[:, bass.ds(at, P)]
                        nc.tensor.matmul(o, w, slots_T[:, j % 2, 0, :], start=True, stop=False)
                        nc.tensor.matmul(o, w, slots_T[:, j % 2, 1, :], start=False, stop=False)
                        mm = nc.tensor.matmul(o, wlo, slots_T[:, j % 2, 0, :], start=False, stop=True)
                    mm.then_inc(expert_up_done[c], 1)

            def down(i, j, lag, e):
                ok, t, k, r = stage(i, j, lag, SLOT_TILES)
                if not ok:
                    return
                pe.wait_ge(hidden_done, t + 1)
                if exists(t - 1, SLOT_TILES):
                    pe.wait_ge(yscaled[(j + lag - 1) % U], i + (j + lag - 1) // U + 1)
                for b in range(2):
                    for c in range(IC):
                        n = min(P, INNER - c * P)
                        mm = nc.tensor.matmul(y_ps[:, b * P:(b + 1) * P], hidden_T[0:n, k % 2, c, b * P:(b + 1) * P],
                                              w_down_flat[0:n, bass.ds(e * (IC * P) + c * P, P)], start=(c == 0), stop=(c == IC - 1))
                mm.then_inc(expert_y_done, 1)

            turn(0, 0, 0)
            owner = [None] * U

            def experts(i, j):
                t = U * i + j
                last_owner = owner[j - 1] if j else (expert_of(t - 1) if exists(t - 1, SLOT_TILES) else None)
                if exists(t, SLOT_TILES):
                    owner[j] = expert_of(t)
                    up(i, j, owner[j])
                turn(i, j, 1)
                down(i, j, -1, last_owner)
            steps(pe, experts, SLOT_TILES, 1, 2, 0)

        @block.scalar
        def _(act):
            act.dma_start(g1T[:, :], Wg1T).then_inc(weights_loaded, 16)
            act.dma_start(g2[:, :], Wg2).then_inc(weights_loaded, 16)
            act.dma_start(half[:, :], halves).then_inc(weights_loaded, 16)
            act.dma_start(router_w[:, :], gate_w).then_inc(weights_loaded, 16)
            act.wait_ge(zeroed, 1)
            nc.scalar.activation(squares_out[:, 0:1], zero[:, 0:1], ACT.Silu)
            act.wait_ge(weights_loaded, 128)
            act.wait_ge(setup_products, 1)
            nc.scalar.activation(rhs2[:, P:], b_p[:, 0:P], ACT.Copy, scale=math.sqrt(CH)).then_inc(setup_act, 1)
            nc.scalar.activation(w_in[:, 3 * P:], b_p[:, P:2 * P], ACT.Copy).then_inc(setup_act, 1)
            nc.scalar.activation(bias_row[:, :], b_p[:, 2 * P:3 * P], ACT.Copy).then_inc(setup_act, 1)
            nc.scalar.activation(rhs2[:, 0:P], C("center"), ACT.Copy).then_inc(setup_act, 1)
            act.wait_ge(setup_pool, 6)

            def silu_qk(i, j, lag):
                ok, t, k, r = stage(i, j, lag)
                if not ok:
                    return
                act.wait_ge(projected, t + 1)
                if exists(t - U):
                    act.wait_ge(cos_done, t - U + 1); act.wait_ge(sin_done, t - U + 1)
                nc.scalar.activation(qk[:, k, :], b_in[:, 0:2 * P], ACT.Silu).then_inc(qk_silu_done, 1)

            def gate_v(i, j, lag):
                ok, t, k, r = stage(i, j, lag)
                if not ok:
                    return
                if exists(t - U):
                    act.wait_ge(gated, t - U + 1)
                nc.scalar.activation(gate_tanh[:, k, :], b_in[:, 3 * P:], ACT.Tanh, scale=0.5).then_inc(gate_tanh_done, 1)
                if exists(t - U):
                    act.wait_ge(attended, t - U + 1)
                nc.scalar.activation(vdiag(k), b_in[:, 2 * P:3 * P].rearrange("p (b h d) -> p h b d", b=4, h=4),
                                     ACT.Copy)
                if exists(t - U):
                    act.wait_ge(delta_done, t - U + 1)
                nc.scalar.activation(v_hi[:, k, :], b_in[:, 2 * P:3 * P], ACT.Copy).then_inc(v_hi_done, 1)

            def hi16(i, j, lag):
                ok, t, k, r = stage(i, j, lag)
                if not ok:
                    return
                act.wait_ge(roped, t + 1)
                if exists(t - U):
                    act.wait_ge(qk_turned, t - U + 1); act.wait_ge(delta_done, t - U + 1)
                out = bass.AP(qk16, offset=k * 8 * P, ap=[[U * 8 * P, P], [4 * P + HD, 2], [32, HEADS], [HD, 2], [1, HD]])
                src = bass.AP(roped_qk, offset=k * 2 * P, ap=[[U * 2 * P, P], [P, 2], [HD, HEADS], [0, 2], [1, HD]])
                nc.scalar.activation(out, src, ACT.Copy).then_inc(qk_hi_done, 1)

            def qkT_copy(i, j, lag):
                ok, t, k, r = stage(i, j, lag)
                if not ok:
                    return
                act.wait_ge(qk_turned, t + 1)
                if exists(t - U):
                    act.wait_ge(attended, t - U + 1)
                nc.scalar.activation(qkT[:, k, :, :], b_t[:, :, :], ACT.Copy).then_inc(qkT_copied, 1)

            def x1T_copy(i, j, lag):
                ok, t, k, r = stage(i, j, lag)
                if not ok:
                    return
                act.wait_ge(bank_p_written, t + 4)
                nc.scalar.activation(x1T[:, :, bass.ds(t * P, P)], x1T_ps.rearrange("p (a c) -> p a c", a=2), ACT.Copy).then_inc(x1T_copied, 1)

            def squares(i, j, lag):
                ok, t, k, r = stage(i, j, lag)
                if not ok:
                    return
                act.wait_ge(bank_p_written, t + 1)
                if exists(t - 1):
                    act.wait_ge(squares_summed, t)
                nc.scalar.activation(squares_out[:, :], projected_out[:, 0:P], ACT.Square, accum_out=stat[:, k % 2, 0:1]).then_inc(squares_summed, 1)

            def logit_out(i, j, lag):
                ok, t, k, r = stage(i, j, lag)
                if not ok:
                    return
                act.wait_ge(logits_done, t + 1)
                if exists(t - 2):
                    act.wait_ge(expert_found, t - 1)
                nc.scalar.activation(logits[:, k, :], logits_ps, ACT.Copy).then_inc(logits_copied, 1)

            def payload(i, j, lag):
                ok, t, k, r = stage(i, j, lag)
                if not ok:
                    return
                act.wait_ge(x1_lo_done, t + 1); act.wait_ge(x1_hi_done, t + 1)
                if exists(t - U):
                    act.wait_ge(rows_scattered[k], 32 * r)
                both = x1_halves[:, k % 2, :, :].rearrange("p a c -> p (a c)").unsqueeze(1).broadcast_to([P, TOP, 2 * P])
                nc.scalar.activation(payload_halves(k), both, ACT.Copy).then_inc(x1_packed, 1)

            def weights(i, j, lag):
                ok, t, k, r = stage(i, j, lag)
                if not ok:
                    return
                act.wait_ge(gap_done, t + 1)
                nc.scalar.activation(gap_tanh[:, k:k + 1], gap[:, k:k + 1], ACT.Tanh, scale=0.5).then_inc(gap_tanh_done, 1)
                act.wait_ge(gap_tanh_done, t + 1)
                if exists(t - U):
                    act.wait_ge(rows_scattered[k], 32 * r)
                nc.scalar.activation(payloads[:, k, 0, WEIGHT:WEIGHT + 1], gap_tanh[:, k:k + 1], ACT.Copy, scale=0.5, bias=0.5)
                nc.scalar.activation(payloads[:, k, 1, WEIGHT:WEIGHT + 1], gap_tanh[:, k:k + 1], ACT.Copy, scale=-0.5, bias=0.5).then_inc(weighed[k], 1)

            def split_shared():
                act.wait_ge(ffn_loaded, FFN_LOADS)
                nc.scalar.activation(shared_hi[:, :, 0:SHARED], shared_staged[:, :, :], ACT.Copy).then_inc(weights_hi_done, 1)

            def split(e):
                nc.scalar.activation(w_hi[:, e, :, 0:INNER], ffn_staged[:, e, :, :], ACT.Copy).then_inc(weights_hi_done, 1)

            def x1hi(i, j, lag):
                ok, t, k, r = stage(i, j, lag)
                if not ok:
                    return
                act.wait_ge(x1_done, t + 1)
                if exists(t - 2):
                    act.wait_ge(bank_p_written, t + 2); act.wait_ge(x1_packed, t - 1)
                nc.scalar.activation(x1_halves[:, k % 2, 0, :], x1[:, t, :], ACT.Copy).then_inc(x1_hi_done, 1)

            silu_qk(0, 0, 0); gate_v(0, 0, 0)
            hi16(0, 0, 0)
            silu_qk(0, 0, 1); gate_v(0, 0, 1)
            qkT_copy(0, 0, 0)
            hi16(0, 0, 1)
            silu_qk(0, 0, 2); gate_v(0, 0, 2)

            def shared(q):
                for c in range(SC):
                    act.wait_ge(shared_gate_done, 2 * q + c + 1)
                    if q >= 2:
                        act.wait_ge(shared_hidden_done, 2 * (q - 2) + c + 1)
                    elif q == 0 and c == 0:
                        act.wait_ge(attended, TILES)
                    nc.scalar.activation(shared_silu_T[:, q % 2, c, :], b_e[c][:, :], ACT.Silu).then_inc(shared_silu_done, 1)

            def body(i, j):
                step = U * i + j
                hi16(i, j, 2)
                if exists(step - 2) or exists(step - 6):
                    act.wait_ge(bank_p_written, step - 1)
                logit_out(i, j, -6)
                x1T_copy(i, j, -5)
                squares(i, j, -2)
                silu_qk(i, j, 3)
                qkT_copy(i, j, 1)
                payload(i, j, -5)
                if isinstance(i, int) and step == TILES - 4:
                    split_shared()
                if isinstance(i, int) and step >= TILES:
                    split(step - TILES)
                x1hi(i, j, -3)
                weights(i, j, -6)
                gate_v(i, j, 3)
                if beside(i, j) is not None:
                    shared(beside(i, j))
            steps(act, body, TILES, AFTER, PEEL, TAIL)
            act.wait_ge(table_made, 1)
            for e in range(EXPERTS // 2, EXPERTS):
                end = act.value_load(ends[0:1, e:e + 1], min_val=0, max_val=EXPERTS * REGION)
                act.dma_start(rows[bass.ds(end, SLOTS), :], pads[e * SLOTS:(e + 1) * SLOTS, :]).then_inc(fill_rows_stored, 16)
            for q in range(AFTER - 1, GROUPS):
                shared(q)

            def silu(i, j):
                ok, t, k, r = stage(i, j, 0, SLOT_TILES)
                if not ok:
                    return
                if exists(t - 2, SLOT_TILES):
                    act.wait_ge(hidden_done, t - 1)
                for c in range(IC):
                    act.wait_ge(expert_up_done[c], t + 1)
                    nc.scalar.activation(silu_gate[:, j % 2, c, :], up_banks[j % 2][c][:, 0:SLOTS], ACT.Silu).then_inc(expert_silu_done[c], 1)

            def scale(i, j, lag):
                ok, t, k, r = stage(i, j, lag, SLOT_TILES)
                if not ok:
                    return
                act.wait_ge(expert_y_done, t + 1); act.wait_ge(meta_copied, t + 1)
                if exists(t - U, SLOT_TILES):
                    act.wait_ge(y_scattered[k], 32 * r)
                for b in range(2):
                    ins = nc.scalar.activation(scaled_y[:, k, b, :], y_ps[:, b * P:(b + 1) * P], ACT.Copy, scale=slot_meta[:, k, b, 1:2])
                ins.then_inc(yscaled[k], 1)

            def experts(i, j):
                silu(i, j)
                scale(i, j, -1)
            steps(act, experts, SLOT_TILES, 1, 2, 0)

            for q in range(FINALS_ON_ACT):
                act.wait_ge(final_rstd, 1 + sum(p <= q for p in DEVIATION_CUTS[1:]))
                for t in range(FT * q, FT * q + FT):
                    nc.scalar.activation(x1[:, t, :], x1[:, t, :], ACT.Identity, scale=final_inverse[:, t:t + 1],
                                         bias=final_shift[:, t:t + 1]).then_inc(normalised, 1)

        @block.vector
        def _(dve):
            dve.wait_ge(weights_loaded, 128)
            nc.vector.memset(ones[:, :], 1.0).then_inc(setup_dve, 1)
            nc.vector.tensor_copy(base[:, :], C("first"))
            nc.vector.memset(w_hi_rows[:, :, INNER:], 0.0).then_inc(weights_padded, 1)
            nc.vector.memset(w_lo_rows[:, :, INNER:], 0.0).then_inc(weights_padded, 1)
            nc.vector.memset(shared_hi[:, :, SHARED:], 0.0).then_inc(weights_padded, 1)
            nc.vector.memset(shared_lo[:, :, SHARED:], 0.0).then_inc(weights_padded, 1)
            nc.vector.tensor_scalar(wo_scaled[:, :], wo[:, :], ln_w_b[:, 0:1], None, ALU.mult).then_inc(setup_dve, 1)
            dve.wait_ge(setup_dve, 1)
            nc.vector.tensor_scalar(ln_b_cols[:, :], ones[:, :], ln_w_b[:, 1:2], None, ALU.mult).then_inc(setup_dve, 1)
            nc.vector.tensor_copy(router_w_hi[:, :], router_w[:, :]).then_inc(setup_dve, 1)
            dve.wait_ge(setup_dve, 4)
            nc.vector.tensor_tensor(router_w_lo[:, :], router_w[:, :], router_w_hi[:, :], ALU.subtract).then_inc(setup_dve, 1)

            def rope_cos(i, j, lag):
                ok, t, k, r = stage(i, j, lag)
                if not ok:
                    return
                dve.wait_ge(qk_silu_done, t + 1)
                if exists(t - U):
                    dve.wait_ge(qk_lo_done, t - U + 1); dve.wait_ge(qk_hi_done, t - U + 1)
                cos = const_sb[:, bass.ds(CONST_AT["cos"][0] + t * HD, HD)].unsqueeze(1).broadcast_to([P, 2 * HEADS, HD])
                nc.vector.tensor_tensor(roped_qk[:, k, :].rearrange("p (h d) -> p h d", d=HD),
                                        qk[:, k, :].rearrange("p (h d) -> p h d", d=HD), cos, ALU.mult).then_inc(cos_done, 1)

            def rope_add(i, j, lag):
                ok, t, k, r = stage(i, j, lag)
                if not ok:
                    return
                dve.wait_ge(cos_done, t + 1); dve.wait_ge(sin_done, t + 1)
                nc.vector.tensor_tensor(roped_qk[:, k, :], roped_qk[:, k, :], turned_qk[:, k, :], ALU.add).then_inc(roped, 1)

            def rope_lo(i, j, lag):
                ok, t, k, r = stage(i, j, lag)
                if not ok:
                    return
                dve.wait_ge(qk_hi_done, t + 1)
                v = lambda o, w: bass.AP(qk16, offset=k * 8 * P + o, ap=[[U * 8 * P, P], [w, 2], [32, HEADS], [1, HD]])
                nc.vector.tensor_tensor(v(2 * HD, 4 * P - 2 * HD), roped_qk[:, k, :].rearrange("p (a h d) -> p a h d", a=2, d=HD),
                                        v(0, 4 * P + HD), ALU.subtract).then_inc(qk_lo_done, 1)

            def mask(i, j, lag, pair):
                ok, t, k, r = stage(i, j, lag)
                if not ok:
                    return
                dve.wait_ge(energies_done[pair], t + 1)
                if exists(t - 2):
                    dve.wait_ge(attended, t - 1)
                heads = slice(2 * pair, 2 * pair + 2)
                tri = C("tri").unsqueeze(1).broadcast_to([P, 2 * BLOCKS, P])
                nc.vector.tensor_tensor(masked_energies[:, k % 2, heads, :].rearrange("p h (b n) -> p (h b) n", b=BLOCKS),
                                        b_es[:, heads, :].rearrange("p h (b n) -> p (h b) n", b=BLOCKS), tri, ALU.mult).then_inc(masked[pair], 1)

            def dmask(i, j, lag):
                ok, t, k, r = stage(i, j, lag)
                if not ok:
                    return
                dve.wait_ge(delta_done, t + 1)
                if exists(t - 2):
                    dve.wait_ge(state_hi_done, t - 1)
                if j < U - 1:
                    nc.vector.tensor_tensor(delta_kept_own[:, j % 2, :], delta, C("own"), ALU.mult).then_inc(delta_masked, 1)
                    return
                keep = const_sb[:, bass.ds(CONST_AT["keep"][0] + t, 1)]
                nc.vector.scalar_tensor_tensor(out=delta_own[:, :], in0=delta, scalar=keep, in1=C("own"),
                                               op0=ALU.mult, op1=ALU.mult).then_inc(delta_kept, 1)
                dve.wait_ge(delta_kept, i + 1); dve.wait_ge(state_added, t)
                nc.vector.scalar_tensor_tensor(out=delta_kept_own[:, j % 2, :], in0=state_sum[:, j % 2, :], scalar=keep, in1=delta_own[:, :],
                                               op0=ALU.mult, op1=ALU.add).then_inc(delta_masked, 1)

            def gate(i, j, lag):
                ok, t, k, r = stage(i, j, lag)
                if not ok:
                    return
                dve.wait_ge(attended, t + 1); dve.wait_ge(gate_tanh_done, t + 1)
                if exists(t - 2):
                    dve.wait_ge(bank_p_written, t - 1)
                nc.vector.scalar_tensor_tensor(out=gated_out[:, k % 2, :], in0=gate_tanh[:, k, :], scalar=1.0, in1=outT,
                                               op0=ALU.add, op1=ALU.mult).then_inc(gated, 1)

            def tail(i, j, lag, part):
                ok, t, k, r = stage(i, j, lag)
                if not ok:
                    return
                k2 = k % 2
                if part == 1:
                    dve.wait_ge(powers_done, t + 1)
                    nc.vector.scalar_tensor_tensor(out=x_plus[:, k2, :], in0=projected_out[:, P:2 * P], scalar=rstd[:, k2, 0:1], in1=x_sb[:, t, :],
                                                   op0=ALU.mult, op1=ALU.add).then_inc(x_summed, 1)
                if part == 2:
                    dve.wait_ge(x_summed, t + 1)
                    nc.vector.bn_stats(moment_parts[:, k2, :], x_plus[:, k2, :]).then_inc(x1_stats, 1)
                if part == 3:
                    nc.vector.bn_aggr(stat[:, 1 - k2, 1:3], moment_parts[:, k2, :]).then_inc(x1_moments, 1)
                if part == 5:
                    dve.wait_ge(powers_done, t + 2)
                    nc.vector.tensor_scalar(x1[:, t, :], x_plus[:, k2, :], stat[:, 1 - k2, 1:2], rstd[:, 1 - k2, 1:2],
                                            ALU.subtract, ALU.mult).then_inc(x1_done, 1)
                if part == 6:
                    dve.wait_ge(x1_hi_done, t + 1)
                    nc.vector.tensor_tensor(x1_halves[:, k2, 1, :], x1[:, t, :], x1_halves[:, k2, 0, :], ALU.subtract).then_inc(x1_lo_done, 1)

            def route(i, j, lag, part):
                ok, t, k, r = stage(i, j, lag)
                if not ok:
                    return
                k2 = k % 2
                if part == 0:
                    dve.wait_ge(weights_loaded, 128)
                    nc.vector.max(top_logits[:, k2, :], logits[:, k, :]).then_inc(max_found, 1)
                if part == 1:
                    dve.wait_ge(weights_loaded, 128)
                    dve.wait_ge(max_found, t + 1)
                    nc.vector.max_index(top_experts[:, k2, :], top_logits[:, k2, :], logits[:, k, :]).then_inc(expert_found, 1)
                    if exists(t - U):
                        dve.wait_ge(weighed[k], r)
                    nc.vector.tensor_tensor(gap[:, k:k + 1], top_logits[:, k2, 0:1], top_logits[:, k2, 1:2], ALU.subtract).then_inc(gap_done, 1)
                if part == 3:
                    dve.wait_ge(expert_found, t + 1)
                    nc.vector.tensor_tensor(one_hot[:, k2, :, :], C("iota").unsqueeze(1).broadcast_to([P, TOP, EXPERTS]),
                                            top_experts[:, k2, 0:TOP].unsqueeze(2).broadcast_to([P, TOP, EXPERTS]), ALU.is_equal).then_inc(one_hot_done, 1)
                if part == 4:
                    dve.wait_ge(one_hot_done, t + 1)
                    if exists(t - 2):
                        dve.wait_ge(bank_p_written, t + 4)
                    nc.vector.tensor_tensor(chosen[:, k2, :], one_hot[:, k2, 0, :], one_hot[:, k2, 1, :], ALU.add).then_inc(choice_marked, 1)
                if part == 5:
                    dve.wait_ge(bank_p_written, t + 6)
                    if exists(t - 1):
                        dve.wait_ge(base_moved, t)
                    nc.vector.tensor_tensor(expert_places[:, k2, :], rank_ps, base[:, :], ALU.add).then_inc(rank_based, 1)
                    dve.wait_ge(rank_based, t + 1)
                    nc.vector.tensor_tensor(base[:, :], total_ps, base[:, :], ALU.add).then_inc(base_moved, 1)
                if part == 6:
                    dve.wait_ge(rank_based, t + 1)
                    nc.vector.tensor_tensor(picked_places[:, k2, :, :], one_hot[:, k2, :, :],
                                            expert_places[:, k2, :].unsqueeze(1).broadcast_to([P, TOP, EXPERTS]),
                                            ALU.mult).then_inc(place_picked, 1)
                if part == 7:
                    dve.wait_ge(place_picked, t + 1)
                    if exists(t - U):
                        dve.wait_ge(rows_scattered[k], 32 * r)
                    with nc.allow_low_precision("whole numbers below 2^24, exact in either type"):
                        nc.vector.tensor_reduce(place[:, k, :], picked_places[:, k2, :, :], AX.X, ALU.add)
                if part == 8:
                    nc.vector.tensor_copy(payloads[:, k, :, DEST:DEST + 1].bitcast(i32),
                                          destinations[:, bass.ds(TOP * t, TOP)].unsqueeze(2)).then_inc(placed[k], 1)

            for lag in (0, 1):
                rope_cos(0, 0, lag); rope_add(0, 0, lag); rope_lo(0, 0, lag)
            rope_cos(0, 0, 2)
            dve.wait_ge(indices_loaded, 16)

            def shared_add(q):
                dve.wait_ge(shared_y_done, q + 1)
                dve.wait_ge(x1_hi_done, 4 * q + 4)
                xq = x1[:, 4 * q:4 * q + 4, :].rearrange("p t c -> p (t c)")
                nc.vector.tensor_tensor(xq, shared_y[q % 2], xq, ALU.add).then_inc(shared_added, 1)

            def shared(q):
                if q == 0:
                    dve.wait_ge(attended, TILES)
                for c in range(SC if q < GROUPS else 0):
                    dve.wait_ge(shared_up_done, 2 * q + c + 1); dve.wait_ge(shared_silu_done, 2 * q + c + 1)
                    if q >= 2 and c == 0:
                        dve.wait_ge(shared_y_done, q - 1)
                    nc.vector.tensor_tensor(shared_hidden_T[:, q % 2, c, :], shared_silu_T[:, q % 2, c, :],
                                            b_e[2 + c][:, :], ALU.mult).then_inc(shared_hidden_done, 1)
                if q:
                    shared_add(q - 1)

            link = [0]

            def table():

                def chain(ins):
                    link[0] += 1
                    ins.then_inc(table_step, 1)
                    dve.wait_ge(table_step, link[0])
                dve.wait_ge(base_moved, TILES)
                nc.vector.tensor_copy(ends[:, :], base[:, :]).then_inc(table_made, 1)
                chain(nc.vector.tensor_tensor(pair_counts[:, :], base[:, :], C("first"), ALU.subtract))
                chain(nc.vector.tensor_scalar(counts_up[:, :], pair_counts[:, :], float(SLOTS - 1), None, ALU.add))
                chain(nc.vector.tensor_scalar(tiles_int[:, :], counts_up[:, :], SLOTS.bit_length() - 1, None, ALU.logical_shift_right))
                chain(nc.vector.tensor_copy(tile_sums[0][:, :], tiles_int[:, :]))
                for n in range(3):
                    d = 1 << n
                    nc.vector.tensor_copy(tile_sums[n + 1][:, 0:d], tile_sums[n][:, 0:d]).then_inc(table_step, 1)
                    link[0] += 1
                    chain(nc.vector.tensor_tensor(tile_sums[n + 1][:, d:], tile_sums[n][:, d:], tile_sums[n][:, 0:EXPERTS - d], ALU.add))
                chain(nc.vector.tensor_scalar(ended[:, :], tile_sums[3][:, :], C("row"), None, ALU.is_le))
                chain(nc.vector.tensor_tensor(ended_tiles[:, :], ended[:, :], tile_sums[0][:, :], ALU.mult))
                chain(nc.vector.tensor_reduce(entry[:, 0:1], ended[:, :], AX.X, ALU.add))
                chain(nc.vector.tensor_reduce(entry[:, 1:2], ended_tiles[:, :], AX.X, ALU.add))
                chain(nc.vector.tensor_tensor(entry[:, 2:3], C("row"), entry[:, 1:2], ALU.subtract))
                chain(nc.vector.tensor_scalar(entry[:, 3:4], entry[:, 2:3], float(SLOTS), None, ALU.mult))
                chain(nc.vector.tensor_scalar(entry[:, 4:5], entry[:, 0:1], float(REGION), None, ALU.mult))
                chain(nc.vector.tensor_tensor(entry[:, 5:6], entry[:, 3:4], entry[:, 4:5], ALU.add))
                chain(nc.vector.tensor_scalar(entry[:, 6:7], entry[:, 0:1], float(EXPERTS - 1), None, ALU.min))
                nc.vector.tensor_copy(tile_entries[:, :], entry[:, 5:7]).then_inc(table_made, 1)

            def body(i, j):
                step = U * i + j
                dmask(i, j, 0)
                rope_add(i, j, 2)
                for pair in range(2):
                    mask(i, j, 0, pair)
                rope_lo(i, j, 2)
                if exists(step - 2) and j == 2:
                    dve.wait_ge(x_biased, i + 1)
                tail(i, j, -2, 1)
                tail(i, j, -3, 5)
                if exists(step - 7) and not exists(step - 2):
                    dve.wait_ge(logits_copied, min(step - 5, TILES)); dve.wait_ge(x1T_copied, min(step - 4, TILES))
                route(i, j, -7, 5)
                tail(i, j, -2, 2)
                if exists(step - 6):
                    dve.wait_ge(logits_copied, step - 5)
                route(i, j, -7, 6)
                route(i, j, -6, 0)
                route(i, j, -7, 7)
                tail(i, j, -4, 6)
                rope_cos(i, j, 3)
                route(i, j, -6, 1)
                if exists(step - 2):
                    dve.wait_ge(x1_stats, step - 1)
                gate(i, j, -1)
                tail(i, j, -2, 3)
                route(i, j, -7, 8)
                route(i, j, -6, 3)
                route(i, j, -6, 4)
                if exists(step - 7) and not exists(step - 6):
                    table()
                if beside(i, j) is not None:
                    shared(beside(i, j))
            steps(dve, body, TILES, AFTER, PEEL, TAIL)

            for q in range(AFTER - 1, GROUPS + 1):
                shared(q)

            def evac(i, j, lag):
                ok, t, k, r = stage(i, j, lag, SLOT_TILES)
                if not ok:
                    return
                dve.wait_ge(slots_turned, t + 1)
                nc.vector.tensor_copy(slots_T[:, k % 2, :, :], slots_T_ps).then_inc(slots_copied, 1)
                if exists(t - U, SLOT_TILES):
                    dve.wait_ge(y_scattered[k], 32 * r)
                    dve.wait_ge(yscaled[k], r)
                nc.vector.tensor_copy(slot_meta[:, k, :, :].bitcast(i32), slot_rows[:, k, :, DEST:DEST + 2].bitcast(i32)).then_inc(meta_copied, 1)

            def hidden(i, j, c):
                t = U * i + j
                dve.wait_ge(expert_silu_done[c], t + 1)
                if c == 0 and exists(t - 2, SLOT_TILES):
                    dve.wait_ge(expert_y_done, t - 1)
                ins = nc.vector.tensor_tensor(hidden_T[:, j % 2, c, :], silu_gate[:, j % 2, c, :], up_banks[j % 2][c][:, SLOTS:], ALU.mult)
                if c == IC - 1:
                    ins.then_inc(hidden_done, 1)

            evac(0, 0, 0)

            def experts(i, j):
                hidden(i, j, 0)
                hidden(i, j, 1)
                evac(i, j, 1)
                hidden(i, j, 2)
            steps(dve, experts, SLOT_TILES, 0, 2, 0)

            def final_scale(n):
                cols = slice(FT * DEVIATION_CUTS[n], FT * DEVIATION_CUTS[n + 1])
                dve.wait_ge(final_recip, n + 1)
                if DEVIATION_CUTS[n] >= FINALS_ON_ACT:
                    for t in range(FT * DEVIATION_CUTS[n], FT * DEVIATION_CUTS[n + 1]):
                        nc.vector.tensor_scalar(x1[:, t, :], x1[:, t, :], final_mean_var[:, t, 0:1], final_inverse[:, t:t + 1],
                                                ALU.subtract, ALU.mult).then_inc(last_normalised, 1)
                    return
                nc.vector.scalar_tensor_tensor(out=final_shift[:, cols], in0=final_mean_var[:, cols, 0], scalar=-1.0, in1=final_inverse[:, cols],
                                               op0=ALU.mult, op1=ALU.mult).then_inc(final_rstd, 1)

            for q in range(FINALS):
                a, b = FT * q, FT * (q + 1)
                if q:
                    dve.wait_ge(first_added, q)
                else:
                    dve.wait_ge(results_loaded[0], 32)
                    nc.vector.tensor_tensor(x1[:, a:b, :], x1[:, a:b, :], y0[:, a:b, :], ALU.add).then_inc(first_half_added, 1)
                    dve.wait_ge(first_half_added, 1)
                nc.vector.tensor_tensor(x1[:, a:b, :], x1[:, a:b, :], y1[:, a:b, :], ALU.add).then_inc(second_added, 1)
                dve.wait_ge(second_added, q + 1)
                for t in range(a, b):
                    nc.vector.bn_stats(final_parts[:, t, :], x1[:, t, :]).then_inc(final_stats, 1)
                for t in range(a, b):
                    dve.wait_ge(final_stats, t + 1)
                    nc.vector.bn_aggr(final_mean_var[:, t, :], final_parts[:, t, :]).then_inc(final_moments, 1)
                if q in DEVIATION_CUTS[1:]:
                    final_scale(DEVIATION_CUTS.index(q) - 1)
            final_scale(len(DEVIATION_CUTS) - 2)

        @block.gpsimd
        def _(pool):
            nc.gpsimd.memset(zero[:, :], 0.0).then_inc(zeroed, 1)
            nc.gpsimd.memset(vexp[:, :, :, :], 0.0).then_inc(setup_pool, 1)
            nc.gpsimd.memset(state_sum[:, 0, :], 0.0).then_inc(setup_pool, 1)
            nc.gpsimd.memset(qk16[:, :, :], 0.0).then_inc(setup_pool, 1)
            nc.gpsimd.memset(state_hi[:, 0, :], 0.0).then_inc(setup_pool, 1)
            nc.gpsimd.memset(state_lo[:, 0, :], 0.0).then_inc(state_lo_done, 1)
            nc.gpsimd.memset(payloads[:, :, :, :], 0.0).then_inc(setup_pool, 1)
            nc.gpsimd.memset(stat[:, :, :], 1.0).then_inc(setup_pool, 1)
            pool.wait_ge(weights_loaded, 128)

            def rope_sin(i, j, lag):
                ok, t, k, r = stage(i, j, lag)
                if not ok:
                    return
                pool.wait_ge(qk_silu_done, t + 1)
                if exists(t - U):
                    pool.wait_ge(roped, t - U + 1)
                sin = const_sb[:, bass.ds(CONST_AT["sin"][0] + t * HD, HD)].rearrange("p (s d) -> p s d", s=2)
                sin = sin.unsqueeze(1).broadcast_to([P, 2 * HEADS, 2, HD // 2])
                swapped = bass.AP(qk, offset=k * 2 * P + HD // 2, ap=[[U * 2 * P, P], [HD, 2 * HEADS], [-(HD // 2), 2], [1, HD // 2]])
                ins = nc.gpsimd.tensor_tensor(turned_qk[:, k, :].rearrange("p (h s d) -> p h s d", s=2, d=HD // 2), swapped, sin, ALU.mult)
                ins.then_inc(sin_done, 1)

            def v16(i, j, lag):
                ok, t, k, r = stage(i, j, lag)
                if not ok:
                    return
                v4 = lambda a: a[:, k, :].rearrange("p (b h d) -> p h b d", b=4, h=4)
                pool.wait_ge(v_hi_done, t + 1)
                nc.gpsimd.tensor_tensor(v4(v_lo), vdiag(k), v4(v_hi), ALU.subtract).then_inc(v_lo_done, 1)

            def st(i, j, lag, part):
                ok, t, k, r = stage(i, j, lag)
                if not ok:
                    return
                n, o, slot = (k + 1) % 2, k % 2, (k + 1) % U
                before = zero[:, :] if k == U - 1 else state_sum[:, o, :]
                if part == 0:
                    pool.wait_ge(delta_masked, t + 1)
                    if exists(t - 1):
                        pool.wait_ge(state_added, t); pool.wait_ge(state_lo_done, t + 1)
                    nc.gpsimd.tensor_tensor(state_sum[:, n, :], before, delta_kept_own[:, o, :], ALU.add).then_inc(state_added, 1)
                if part == 1:
                    if exists(t - 3):
                        pool.wait_ge(attended, t - 2)
                    nc.gpsimd.tensor_tensor(state_hi[:, slot, :], before, delta_kept_own[:, o, :], ALU.add).then_inc(state_hi_done, 1)
                if part == 2:
                    pool.wait_ge(state_hi_done, t + 1)
                    nc.gpsimd.tensor_tensor(state_lo[:, slot, :], state_sum[:, n, :], state_hi[:, slot, :], ALU.subtract).then_inc(state_lo_done, 1)

            def powers(i, j):
                step = U * i + j
                if not (exists(step - 2) or exists(step - 3)):
                    return
                if exists(step - 2):
                    pool.wait_ge(squares_summed, step - 1)
                if exists(step - 3):
                    pool.wait_ge(x1_moments, step - 2)
                small = C("small")
                nc.gpsimd.tensor_tensor(var_eps[:, :], bass.AP(stat, offset=3 * (j % 2), ap=[[6, P], [2, 2]]), small[:, 0:2], ALU.add).then_inc(var_eps_done, 1)
                pool.wait_ge(var_eps_done, step - 1)
                nc.gpsimd.tensor_tensor(rstd[:, j % 2, :], var_eps[:, :], small[:, 2:3].broadcast_to([P, 2]), ALU.pow).then_inc(powers_done, 1)

            for lag in (0, 1, 2):
                rope_sin(0, 0, lag)
            v16(0, 0, 0)

            def scatter(i, j, lag, c):
                ok, t, k, r = stage(i, j, lag)
                if not ok:
                    return
                pool.wait_ge(x_loaded, 64)
                nc.gpsimd.indirect_dma_start(out=rows, out_offset=bass.IndirectOffsetOnAxis(ap=place[:, k, c:c + 1], axis=0),
                                             in_=payloads[:, k, c, :], in_offset=None).then_inc(rows_scattered[k], 16)

            def bias(i, j):
                if isinstance(i, int) and i == 0:
                    pool.wait_ge(x_loaded, 64); pool.wait_ge(setup_act, 4)
                xq = x_sb[:, bass.ds(U * i, U), :]
                nc.gpsimd.tensor_tensor(xq, xq, bias_row[:, :].unsqueeze(1).broadcast_to([P, U, P]), ALU.add).then_inc(x_biased, 1)

            def split_shared():
                pool.wait_ge(weights_hi_done, 1)
                nc.gpsimd.tensor_tensor(shared_lo[:, :, 0:SHARED], shared_staged[:, :, :], shared_hi[:, :, 0:SHARED], ALU.subtract).then_inc(weights_lo_done, 1)

            def split(e):
                pool.wait_ge(weights_hi_done, e + 2)
                nc.gpsimd.tensor_tensor(w_lo[:, e, :, 0:INNER], ffn_staged[:, e, :, :], w_hi[:, e, :, 0:INNER], ALU.subtract).then_inc(weights_lo_done, 1)

            def body(i, j):
                step = U * i + j
                ok, t, k, r = stage(i, j, -8)
                if ok:
                    pool.wait_ge(placed[k], r + 1); pool.wait_ge(weighed[k], r + 1)
                v16(i, j, 1)
                scatter(i, j, -8, 0)
                powers(i, j)
                scatter(i, j, -8, 1)
                for part in range(3):
                    st(i, j, 0, part)
                rope_sin(i, j, 3)
                if j == 0 and exists(step):
                    bias(i, j)
                if isinstance(i, int) and step == TILES - 3:
                    split_shared()
                if isinstance(i, int) and step >= TILES:
                    split(step - TILES)
            steps(pool, body, TILES, AFTER, PEEL, TAIL)

            def scatter_results(j, n):
                pool.wait_ge(table_made, 1); pool.wait_ge(yscaled[j], n)
                for b in range(2):
                    nc.gpsimd.indirect_dma_start(out=ydram, out_offset=bass.IndirectOffsetOnAxis(ap=slot_meta[:, j, b, 0:1].bitcast(u32), axis=0),
                                                 in_=scaled_y[:, j, b, :], in_offset=None).then_inc(y_scattered[j], 16)

            with pool.Fori(1, SLOT_TILES // U + 1) as n:
                for j in range(U):
                    scatter_results(j, n)
            for j in range(SLOT_TILES % U):
                scatter_results(j, SLOT_TILES // U + 1)

            def inverse_deviation(n):
                cols, small = slice(FT * DEVIATION_CUTS[n], FT * DEVIATION_CUTS[n + 1]), C("small")
                width = FT * (DEVIATION_CUTS[n + 1] - DEVIATION_CUTS[n])
                pool.wait_ge(final_moments, FT * DEVIATION_CUTS[n + 1])
                nc.gpsimd.tensor_tensor(final_var[:, cols], final_mean_var[:, cols, 1],
                                        small[:, 1:2].broadcast_to([P, width]), ALU.add).then_inc(final_var_eps, 1)
                pool.wait_ge(final_var_eps, n + 1)
                nc.gpsimd.tensor_tensor(final_inverse[:, cols], final_var[:, cols], small[:, 2:3].broadcast_to([P, width]), ALU.pow).then_inc(final_recip, 1)

            for q in range(1, FINALS):
                a, b = FT * q, FT * (q + 1)
                pool.wait_ge(results_loaded[q], 32)
                nc.gpsimd.tensor_tensor(x1[:, a:b, :], x1[:, a:b, :], y0[:, a:b, :], ALU.add).then_inc(first_added, 1)
                if q - DEVIATION_LAG in DEVIATION_CUTS[1:]:
                    inverse_deviation(DEVIATION_CUTS.index(q - DEVIATION_LAG) - 1)
            for n in range(len(DEVIATION_CUTS) - 1):
                if DEVIATION_CUTS[n + 1] + DEVIATION_LAG >= FINALS:
                    inverse_deviation(n)


def kernel(**inputs):
    import numpy as _np
    import concourse.bacc as _bacc
    from concourse import mybir as _mybir
    from concourse.bass_utils import run_bass_kernel_spmd as _run

    a = lambda n: _np.asarray(inputs["L0_attn_" + n])
    f = lambda n: _np.asarray(inputs["L0_ffn_" + n])
    x = a("x").reshape(TOKENS, CH)
    data = dict(
        x=x, xT=x.T, Wqkv=_np.concatenate([a("Wq"), a("Wk"), a("Wv")], 1), Wg1T=a("Wg1").T, Wg2=a("Wg2"), Wo=a("Wo"),
        ln=_np.stack([a("ln_w"), a("ln_b")], 1), gate_w=f("gate_w"), Wg=f("Wg"), Wu=f("Wu"), Wd=f("Wd"),
        Sgu=_np.stack([f("Sg"), f("Su")], 1), Sd=f("Sd"),
        consts=constants()[0], halves=half_constants(), indices=index_constants(), pads=pad_rows())
    nc = _bacc.Bacc("TRN2", target_bir_lowering=False, num_devices=1)
    arrays, args = {}, {}
    for name, array in data.items():
        array = _np.ascontiguousarray(array)
        arrays["in_" + name] = array
        args[name] = nc.dram_tensor("in_" + name, array.shape, _mybir.dt.from_np(array.dtype), kind="ExternalInput").ap()
    out = nc.dram_tensor("out_0", (TOKENS, CH), _mybir.dt.float32, kind="ExternalOutput").ap()
    build(nc, out=out, **args)
    r = _run(nc, [arrays], core_ids=[0])
    return _np.asarray(r.results[0]["out_0"]).reshape(4, SEQ, CH)
```
